# Optimizing a Trainium2 kernel written in Bass

```python
import numpy as np
import jax
import jax.numpy as jnp

def _softmax(x, axis=-1):
    return jax.nn.softmax(x, axis=axis)

def _gelu(x):
    return jax.nn.gelu(x, approximate=True)

def _silu(x):
    return jax.nn.silu(x)

def _sigmoid(x):
    return jax.nn.sigmoid(x)

def _layernorm(x, axis=-1, eps=1e-05):
    m = jnp.mean(x, axis=axis, keepdims=True)
    v = jnp.var(x, axis=axis, keepdims=True)
    return (x - m) / jnp.sqrt(v + eps)

def _scatter_add(tgt, idx, src, axis=0):
    return tgt.at[idx].add(src)

def _segment_sum(src, seg, n):
    return jax.ops.segment_sum(src, seg, n)
kernel_name = 'mk_hybrid_d1_jaxref_r8_30f164'

def setup_inputs(seed: int=0):
    np.random.seed(seed)
    _w = jnp.asarray

    def _L0_attn_a_setup():
        import jax, jax.numpy as jnp
        import numpy as np
        B, S, D = (4, 256, 128)
        key = jax.random.key(seed)
        k1, k2, k3, k4 = jax.random.split(key, 4)
        x = jax.random.normal(k1, (B, S, D), dtype=jnp.float32)
        Qw = jax.random.normal(k2, (D, D), dtype=jnp.float32) / 40
        Kw = jax.random.normal(k3, (D, D), dtype=jnp.float32) / 40
        Vw = jax.random.normal(k4, (D, D), dtype=jnp.float32) / 40
        return {'x': x, 'Qw': Qw, 'Kw': Kw, 'Vw': Vw}
    _L0_attn_a_in = _L0_attn_a_setup()

    def _L0_attn_b_setup():
        import jax, jax.numpy as jnp
        import numpy as np
        B, T, D = (2, 256, 128)
        H = 16
        HD = D // H
        DL = 64
        NR = 64
        EPS = 1.1920929e-07

        def _rms_norm(x, w):
            ms = jnp.mean(jnp.square(x), axis=-1, keepdims=True)
            return x * jax.lax.rsqrt(ms + EPS) * w
        key = jax.random.key(seed)
        ks = jax.random.split(key, 10)
        s = 0.02
        return {'x': jax.random.normal(ks[0], (B, T, D), dtype=jnp.float32), 'W_DQ': jax.random.normal(ks[1], (DL, HD), dtype=jnp.float32) * s, 'W_UQ': jax.random.normal(ks[2], (HD, DL), dtype=jnp.float32) * s, 'W_DKV': jax.random.normal(ks[3], (2 * DL, HD), dtype=jnp.float32) * s, 'W_UKV': jax.random.normal(ks[4], (2 * HD, 2 * DL), dtype=jnp.float32) * s, 'W_QR': jax.random.normal(ks[5], (NR, HD), dtype=jnp.float32) * s, 'W_KR': jax.random.normal(ks[6], (NR, HD), dtype=jnp.float32) * s, 'W_O': jax.random.normal(ks[7], (HD, HD), dtype=jnp.float32) * s, 'q_norm_w': jnp.ones((HD,), dtype=jnp.float32), 'k_norm_w': jnp.ones((HD,), dtype=jnp.float32)}
    _L0_attn_b_in = _L0_attn_b_setup()

    def _L0_ffn_setup():
        import jax, jax.numpy as jnp
        import numpy as np
        B, S, H, NH, E, F = (4, 128, 128, 16, 8, 512)
        D = H // NH
        EPS = 1e-05

        def _layernorm(x, g, b):
            mu = jnp.mean(x, axis=-1, keepdims=True)
            var = jnp.var(x, axis=-1, keepdims=True)
            return (x - mu) * jax.lax.rsqrt(var + EPS) * g + b
        key = jax.random.key(seed)
        ks = jax.random.split(key, 16)
        s = 0.02
        return {'x': jax.random.normal(ks[0], (B, S, H), jnp.float32), 'ln1_g': jnp.ones((H,), jnp.float32), 'ln1_b': jnp.zeros((H,), jnp.float32), 'ln2_g': jnp.ones((H,), jnp.float32), 'ln2_b': jnp.zeros((H,), jnp.float32), 'wq': jax.random.normal(ks[1], (H, H), jnp.float32) * s, 'bq': jnp.zeros((H,), jnp.float32), 'wk': jax.random.normal(ks[2], (H, H), jnp.float32) * s, 'bk': jnp.zeros((H,), jnp.float32), 'wv': jax.random.normal(ks[3], (H, H), jnp.float32) * s, 'bv': jnp.zeros((H,), jnp.float32), 'wo': jax.random.normal(ks[4], (H, H), jnp.float32) * s, 'bo': jnp.zeros((H,), jnp.float32), 'gate_w': jax.random.normal(ks[5], (H, E), jnp.float32) * s, 'gate_b': jnp.zeros((E,), jnp.float32), 'w1': jax.random.normal(ks[6], (E, H, F), jnp.float32) * s, 'b1': jnp.zeros((E, F), jnp.float32), 'w2': jax.random.normal(ks[7], (E, F, H), jnp.float32) * s, 'b2': jnp.zeros((E, H), jnp.float32)}
    _L0_ffn_in = _L0_ffn_setup()
    _d = {'L0_attn_a_x': _L0_attn_a_in['x'], 'L0_attn_a_Qw': _L0_attn_a_in['Qw'], 'L0_attn_a_Kw': _L0_attn_a_in['Kw'], 'L0_attn_a_Vw': _L0_attn_a_in['Vw'], 'L0_attn_b_W_DQ': _L0_attn_b_in['W_DQ'], 'L0_attn_b_W_UQ': _L0_attn_b_in['W_UQ'], 'L0_attn_b_W_DKV': _L0_attn_b_in['W_DKV'], 'L0_attn_b_W_UKV': _L0_attn_b_in['W_UKV'], 'L0_attn_b_W_QR': _L0_attn_b_in['W_QR'], 'L0_attn_b_W_KR': _L0_attn_b_in['W_KR'], 'L0_attn_b_W_O': _L0_attn_b_in['W_O'], 'L0_attn_b_q_norm_w': _L0_attn_b_in['q_norm_w'], 'L0_attn_b_k_norm_w': _L0_attn_b_in['k_norm_w'], 'L0_ffn_ln1_g': _L0_ffn_in['ln1_g'], 'L0_ffn_ln1_b': _L0_ffn_in['ln1_b'], 'L0_ffn_ln2_g': _L0_ffn_in['ln2_g'], 'L0_ffn_ln2_b': _L0_ffn_in['ln2_b'], 'L0_ffn_wq': _L0_ffn_in['wq'], 'L0_ffn_bq': _L0_ffn_in['bq'], 'L0_ffn_wk': _L0_ffn_in['wk'], 'L0_ffn_bk': _L0_ffn_in['bk'], 'L0_ffn_wv': _L0_ffn_in['wv'], 'L0_ffn_bv': _L0_ffn_in['bv'], 'L0_ffn_wo': _L0_ffn_in['wo'], 'L0_ffn_bo': _L0_ffn_in['bo'], 'L0_ffn_gate_w': _L0_ffn_in['gate_w'], 'L0_ffn_gate_b': _L0_ffn_in['gate_b'], 'L0_ffn_w1': _L0_ffn_in['w1'], 'L0_ffn_b1': _L0_ffn_in['b1'], 'L0_ffn_w2': _L0_ffn_in['w2'], 'L0_ffn_b2': _L0_ffn_in['b2']}
    _x0 = _d['L0_attn_a_x']
    _d['L0_attn_a_x'] = jax.random.normal(jax.random.fold_in(jax.random.key(seed), 1), (8, 256, 128), dtype=_x0.dtype)
    del _x0
    return _d

def reference(L0_attn_a_x, L0_attn_a_Qw, L0_attn_a_Kw, L0_attn_a_Vw, L0_attn_b_W_DQ, L0_attn_b_W_UQ, L0_attn_b_W_DKV, L0_attn_b_W_UKV, L0_attn_b_W_QR, L0_attn_b_W_KR, L0_attn_b_W_O, L0_attn_b_q_norm_w, L0_attn_b_k_norm_w, L0_ffn_ln1_g, L0_ffn_ln1_b, L0_ffn_ln2_g, L0_ffn_ln2_b, L0_ffn_wq, L0_ffn_bq, L0_ffn_wk, L0_ffn_bk, L0_ffn_wv, L0_ffn_bv, L0_ffn_wo, L0_ffn_bo, L0_ffn_gate_w, L0_ffn_gate_b, L0_ffn_w1, L0_ffn_b1, L0_ffn_w2, L0_ffn_b2):

    def _L0_attn_a_ref(x, Qw, Kw, Vw):
        import jax, jax.numpy as jnp
        import numpy as np
        B, S, D = (4, 256, 128)
        Q = x @ Qw
        K = x @ Kw
        V = x @ Vw
        d = x.shape[-1]
        S_len = x.shape[-2]
        mask = jnp.where(jnp.tril(jnp.ones((S_len, S_len), dtype=x.dtype)) == 0, -jnp.inf, 0.0).astype(x.dtype)
        scores = jnp.einsum('bqd,bkd->bqk', Q, K) / jnp.sqrt(jnp.asarray(d, x.dtype))
        scores = scores + mask
        attn = jax.nn.softmax(scores, axis=-1)
        return jnp.einsum('bqk,bkd->bqd', attn, V)

    def _L0_attn_b_ref(x, W_DQ, W_UQ, W_DKV, W_UKV, W_QR, W_KR, W_O, q_norm_w, k_norm_w):
        import jax, jax.numpy as jnp
        import numpy as np
        B, T, D = (2, 256, 128)
        H = 16
        HD = D // H
        DL = 64
        NR = 64
        EPS = 1.1920929e-07

        def _rms_norm(x, w):
            ms = jnp.mean(jnp.square(x), axis=-1, keepdims=True)
            return x * jax.lax.rsqrt(ms + EPS) * w
        b, t, d = x.shape
        scale = HD ** (-0.5)
        xh = x.reshape(b, t, H, HD).transpose(0, 2, 1, 3)
        c_q = jnp.einsum('bhtd,ld->bhtl', xh, W_DQ)
        q_c = jnp.einsum('bhtl,dl->bhtd', c_q, W_UQ)
        q_c_norm = _rms_norm(q_c, q_norm_w)
        q_r = jnp.einsum('bhtd,rd->bhtr', q_c_norm, W_QR)
        q = jnp.concatenate([q_c_norm, q_r], axis=-1)
        c_kv = jnp.einsum('bhtd,ld->bhtl', xh, W_DKV)
        kv = jnp.einsum('bhtl,dl->bhtd', c_kv, W_UKV)
        k_c, v_c = (kv[..., :HD], kv[..., HD:])
        k_c_norm = _rms_norm(k_c, k_norm_w)
        k_r = jnp.einsum('bhtd,rd->bhtr', xh, W_KR)
        k = jnp.concatenate([k_c_norm, k_r], axis=-1)
        scores = jnp.einsum('bhqd,bhkd->bhqk', q, k) * scale
        causal = jnp.triu(jnp.full((t, t), -jnp.inf, dtype=scores.dtype), k=1)
        attn = jax.nn.softmax(scores + causal, axis=-1)
        ctx = jnp.einsum('bhqk,bhkd->bhqd', attn, v_c)
        out = jnp.einsum('bhtd,od->bhto', ctx, W_O)
        return out.transpose(0, 2, 1, 3).reshape(b, t, d)

    def _L0_ffn_ref(x, ln1_g, ln1_b, ln2_g, ln2_b, wq, bq, wk, bk, wv, bv, wo, bo, gate_w, gate_b, w1, b1, w2, b2):
        import jax, jax.numpy as jnp
        import numpy as np
        B, S, H, NH, E, F = (4, 128, 128, 16, 8, 512)
        D = H // NH
        EPS = 1e-05

        def _layernorm(x, g, b):
            mu = jnp.mean(x, axis=-1, keepdims=True)
            var = jnp.var(x, axis=-1, keepdims=True)
            return (x - mu) * jax.lax.rsqrt(var + EPS) * g + b
        b, s, h = x.shape
        hn = _layernorm(x, ln1_g, ln1_b)
        q = (hn @ wq + bq).reshape(b, s, NH, D).transpose(0, 2, 1, 3)
        k = (hn @ wk + bk).reshape(b, s, NH, D).transpose(0, 2, 1, 3)
        v = (hn @ wv + bv).reshape(b, s, NH, D).transpose(0, 2, 1, 3)
        scores = jnp.einsum('bhqd,bhkd->bhqk', q, k) / jnp.sqrt(jnp.float32(D))
        attn = jax.nn.softmax(scores, axis=-1)
        o = jnp.einsum('bhqk,bhkd->bhqd', attn, v)
        o = o.transpose(0, 2, 1, 3).reshape(b, s, h)
        x = x + (o @ wo + bo)
        hn2 = _layernorm(x, ln2_g, ln2_b).reshape(-1, h)
        logits = hn2 @ gate_w + gate_b
        idx = jnp.argmax(logits, axis=-1)
        mid = jax.nn.relu(jnp.einsum('th,ehf->etf', hn2, w1) + b1[:, None, :])
        y = jnp.einsum('etf,efh->eth', mid, w2) + b2[:, None, :]
        moe = y[idx, jnp.arange(hn2.shape[0])]
        return x + moe.reshape(b, s, h)
    x = L0_attn_a_x
    x = x + _L0_attn_a_ref(_layernorm(x, axis=-1), L0_attn_a_Qw, L0_attn_a_Kw, L0_attn_a_Vw)
    x = x + _L0_ffn_ref(_layernorm(x, axis=-1), L0_ffn_ln1_g, L0_ffn_ln1_b, L0_ffn_ln2_g, L0_ffn_ln2_b, L0_ffn_wq, L0_ffn_bq, L0_ffn_wk, L0_ffn_bk, L0_ffn_wv, L0_ffn_bv, L0_ffn_wo, L0_ffn_bo, L0_ffn_gate_w, L0_ffn_gate_b, L0_ffn_w1, L0_ffn_b1, L0_ffn_w2, L0_ffn_b2)
    x = x + _L0_attn_b_ref(_layernorm(x, axis=-1), L0_attn_b_W_DQ, L0_attn_b_W_UQ, L0_attn_b_W_DKV, L0_attn_b_W_UKV, L0_attn_b_W_QR, L0_attn_b_W_KR, L0_attn_b_W_O, L0_attn_b_q_norm_w, L0_attn_b_k_norm_w)
    x = x + _L0_ffn_ref(_layernorm(x, axis=-1), L0_ffn_ln1_g, L0_ffn_ln1_b, L0_ffn_ln2_g, L0_ffn_ln2_b, L0_ffn_wq, L0_ffn_bq, L0_ffn_wk, L0_ffn_bk, L0_ffn_wv, L0_ffn_bv, L0_ffn_wo, L0_ffn_bo, L0_ffn_gate_w, L0_ffn_gate_b, L0_ffn_w1, L0_ffn_b1, L0_ffn_w2, L0_ffn_b2)
    return x

_drawn_inputs = setup_inputs


def setup_inputs(seed=0):
    import zlib

    import numpy as np

    out = dict(_drawn_inputs(seed))
    spreads = {'L0_attn_b_q_norm_w': (1.0, 0.6),
     'L0_attn_b_k_norm_w': (1.0, 0.6),
     'L0_ffn_ln1_g': (1.0, 0.6),
     'L0_ffn_ln1_b': (0.0, 0.8),
     'L0_ffn_ln2_g': (1.0, 0.2),
     'L0_ffn_ln2_b': (0.0, 0.1),
     'L0_ffn_bq': (0.0, 0.8),
     'L0_ffn_bk': (0.0, 0.8),
     'L0_ffn_bv': (0.0, 0.306),
     'L0_ffn_bo': (0.0, 0.1),
     'L0_ffn_gate_b': (0.0, 0.1),
     'L0_ffn_b1': (0.0, 0.315),
     'L0_ffn_b2': (0.0, 0.1)}
    factors = {'L0_attn_a_Qw': 8.0,
     'L0_attn_a_Kw': 8.0,
     'L0_attn_b_W_DQ': 8.0,
     'L0_attn_b_W_UQ': 8.0,
     'L0_attn_b_W_DKV': 8.0,
     'L0_attn_b_W_UKV': 8.0,
     'L0_attn_b_W_QR': 8.0,
     'L0_attn_b_W_KR': 8.0,
     'L0_attn_b_W_O': 8.0,
     'L0_ffn_wq': 8.0,
     'L0_ffn_wk': 8.0,
     'L0_ffn_wv': 4.876}
    for name, (base, spread) in spreads.items():
        noise = np.random.default_rng([zlib.crc32(name.encode()), seed]).standard_normal(out[name].shape)
        drawn = base * np.exp(spread * noise) if base else spread * noise
        out[name] = jnp.asarray(drawn.astype(out[name].dtype))
    for name, factor in factors.items():
        out[name] = (out[name] * factor).astype(out[name].dtype)
    return out
```

```python
from contextlib import ExitStack

import concourse.bass as bass
from concourse import mybir

F32 = mybir.dt.float32
BF16 = mybir.dt.bfloat16
I32 = mybir.dt.int32
ALU = mybir.AluOpType
ACT = mybir.ActivationFunctionType
AX_X = mybir.AxisListType.X

P = 128
B, S = 8, 256
T = B * S
NT = T // P
CH = 512
NC = T // CH
H, DH = 16, 8
E, F = 8, 512
FC = F // P
NR = NT + E - 1
ROWS = 9 * DH
AUG = ROWS + 2
SLOTS = 3
SLOT = H * S
LN_EPS = 1e-5
RMS_EPS = 1.1920929e-07
NEG = -1e30
HEAD_SCALE = DH ** -0.5
PART = P * T
PB = P * S


def at_least(eng, sem, count):
    if isinstance(count, int) and count <= 0:
        return
    eng.wait_ge(sem, count)


def hybrid_block_kernel(nc, a, out):
    ctx = ExitStack()
    with ctx:
        ctx.enter_context(nc.allow_non_contiguous_dma("small weights are laid out on load"))

        def sb(name, shape, dt=F32):
            return ctx.enter_context(nc.sbuf_tensor(name, shape, dt))

        def sems(prefix, names):
            each = {n: ctx.enter_context(nc.semaphore(prefix + "_" + n)) for n in names.split()}
            return each

        qk_parts = nc.dram_tensor("qk_parts", (2, 3, B, P * S), BF16, kind="Internal")
        routed_x = nc.dram_tensor("routed_x", (NR * P, P), F32, kind="Internal")
        routed_y = nc.dram_tensor("routed_y", (NR * P, P), F32, kind="Internal")

        X = sb("X", [P, T])
        HAT = sb("HAT", [P, T])
        U = sb("U", [P, T])
        V = sb("V", [P, T])
        XT = sb("XT", [P, T])
        QP = sb("QP", [P, 3 * T], BF16)
        KP = sb("KP", [P, 3 * T], BF16)
        QS = sb("QS", [P, SLOTS * SLOT], BF16)
        KS = sb("KS", [P, SLOTS * SLOT], BF16)
        VP = sb("VP", [P, 2 * H * 32])
        PR = sb("PR", [P, 8 * CH])
        OT = sb("OT", [P, S])
        RC = sb("RC", [P, S])
        RES = sb("RES", [P, 2 * CH])
        MN = sb("MN", [P, 2 * 2 * 8])
        MHI = sb("MHI", [8, 2 * S], BF16)
        MLO = sb("MLO", [8, 2 * S], BF16)
        W1 = sb("W1", [P, E * F])
        W2 = sb("W2", [P, E * F])
        B1R = sb("B1R", [P, E * F])
        B2R = sb("B2R", [P, E * P])
        wa = {n: sb("a_" + n, [P, P]) for n in ("Qw", "Kw", "Vw")}
        WN = RES[:, 0:2 * P]
        WQ, WK, WV, WO = (sb(n, [P, P]) for n in ("WQ", "WK", "WV", "WO"))
        GW = sb("GW", [P, E])
        GBR = sb("GBR", [P, E])
        BVR = sb("BVR", [P, P])
        BOR = sb("BOR", [P, P])
        COLS = sb("COLS", [P, 8])
        BQ, BK, G1, BE1, G2, BE2, QNW, KNW = (COLS[:, i:i + 1] for i in range(8))
        EPS = sb("EPS", [P, 2])
        BDQ, BDK, BDG, BDV, BDO = (sb(n, [P, P]) for n in ("BDQ", "BDK", "BDG", "BDV", "BDO"))
        SMALL = sb("SMALL", [P, 64])
        IDF = sb("IDF", [P, P])
        IDB = sb("IDB", [P, P], BF16)
        MSK = sb("MSK", [P, 2 * P], BF16)
        MSKT = sb("MSKT", [P, P], BF16)
        TRI = sb("TRI", [P, P], BF16)
        ONB = sb("ONB", [P, P], BF16)
        SELN = [sb(f"SELN{g}", [P, P]) for g in range(2)]
        SELD = [sb(f"SELD{g}", [P, P]) for g in range(2)]
        BLK = sb("BLK", [P, P])
        BLKP = sb("BLKP", [P, P])
        BON = sb("BON", [P, P])
        REV = sb("REV", [P, E])
        J128 = sb("J128", [P, NT])
        I24 = sb("I24", [P, NR])
        ST = sb("ST", [P, NT * 6])
        tok = {n: sb("t_" + n, [P, NT]) for n in ("a", "b", "mean", "var", "std", "rstd", "c", "rt", "nm", "rs")}
        R = {n: RES[:, i * P:(i + 1) * P] for i, n in enumerate(("lg", "eq", "hot", "cnt", "s0", "s1", "slot"))}
        HOTB = sb("HOTB", [P, NT * E], BF16)
        RT_ = {n: sb("r_" + n, [P, E]) for n in ("n", "m0", "m1", "base")}
        TOP = sb("TOP", [P, NT])
        SLF = sb("SLF", [P, NT])
        SLOTI = sb("SLOTI", [P, NT], I32)
        CMP = RC[:, 0:NR * E]
        EXF = sb("EXF", [P, NR])
        EXI = sb("EXI", [P, NR], I32)

        bank = [ctx.enter_context(nc.psum_tensor(f"bank{i}", [P, CH], F32)) for i in range(8)]

        QT = QS[:, 0:2 * T].bitcast(F32)
        KT = QS[:, 2 * T:4 * T].bitcast(F32)
        PA = PR[:, 0:2 * S]
        PT = PR[:, 2 * S:4 * S]
        TW = PR
        XS = [PR[:, i * P:(i + 1) * P] for i in range(4)]
        XST = [PR[:, (4 + i) * P:(5 + i) * P] for i in range(2)]
        YS = [PR[:, (6 + i) * P:(7 + i) * P] for i in range(4)]
        MID = [PR[:, (12 + 4 * i) * P:(16 + 4 * i) * P] for i in range(2)]
        MIDT = [PR[:, (20 + 4 * i) * P:(24 + 4 * i) * P] for i in range(2)]
        GATH = XT
        RAW = [RES[:, g * S:(g + 1) * S] for g in range(2)]

        ld = sems("ld", "x wa wb ffn blk small moe zero")
        cst = sems("cst", "pool dve pe")
        ph = sems("phase", "pe act dve pool sp")
        step = sems("step", "dve act")
        norm_names = "var std hat xt_ps xt "
        parts_names = " qa ka r2 q_done parts0 parts1 parts2 parts3"
        pa = sems("a", norm_names + "q_ps k_ps v_ps q_ev k_ev v_ev scored maxed exped pt_ps pt o_ps done")
        core_names = ("qk_in0 qk_in1 qk_ready scored maxed m_t m_hi m_lo shift0 shift1 st exped pv v_padded raw0 raw1 selected "
                      "inverted normed projected added")
        ffn_names = ("v_var v_std v_hat v_xt_ps v_xt logits hot prefix slots experts "
                     "xs0 xs1 xs2 xs3 x_t x_tb up mid m_t m_tb down y ys0 ys1 ys2 ys3 xu done")
        s_pre = sems("p", norm_names + "var2 std2 q_ps k_ps v_ps v_ev u0 sq ms_ps sd g_ps kq bd_ps bd" + parts_names)
        s_core = sems("c", core_names)
        s_post = sems("e", ffn_names)
        routed = [sems(f"rows{i}", "scattered gathered") for i in range(3)]
        FFN, ATTN_B = "ffn", "attention b"
        LAYERS = (FFN, ATTN_B, FFN)
        s_out = ctx.enter_context(nc.semaphore("s_out"))

        counts = {"dve": 0, "act": 0}

        def dve_then(dve, ins):
            counts["dve"] += 1
            ins.then_inc(step["dve"], 1)
            dve.wait_ge(step["dve"], counts["dve"])

        def phase_end(eng, own, k):
            eng.drain().then_inc(own, 1)
            for other in (ph["pe"], ph["act"], ph["dve"], ph["pool"], ph["sp"]):
                if other is not own:
                    eng.wait_ge(other, k)

        def clear(eng, phase):
            for sem in phase.values():
                eng.sem_clear(sem)

        def tile_(buf, t, n=1):
            return buf[:, t * P:(t + n) * P]

        def ln_dve(dve, s, src, twice):
            for t in range(NT):
                last = dve.bn_stats(ST[:, 6 * t:6 * t + 6], tile_(src, t))
            dve_then(dve, last)
            st = ST[:, :].rearrange("p (t k) -> p t k", k=6)
            me, ve, mo, vo = (st[:, :, i] for i in (1, 2, 4, 5))
            ta, tb, mean, var = (tok[n][:, :] for n in ("a", "b", "mean", "var"))
            dve.tensor_tensor(ta, me, mo, ALU.subtract)
            dve.tensor_tensor(tb, ve, vo, ALU.add)
            dve_then(dve, dve.tensor_tensor(mean, me, mo, ALU.add))
            dve.tensor_scalar(mean, mean, 0.5, None, ALU.mult)
            dve_then(dve, dve.tensor_tensor(ta, ta, ta, ALU.mult))
            dve_then(dve, dve.scalar_tensor_tensor(out=var, in0=ta, scalar=float(P // 4), in1=tb,
                                                   op0=ALU.mult, op1=ALU.add))
            dve.tensor_scalar(var, var, 1.0 / P, None, ALU.mult).then_inc(s["var"], 1)
            dve.wait_ge(s["std"], 1)
            rstd = tok["rstd"][:, :]
            dve_then(dve, dve.reciprocal(rstd, tok["std"][:, :]))
            scale = rstd
            if twice:
                dve_then(dve, dve.tensor_tensor(ta, var, rstd, ALU.mult))
                dve.tensor_tensor(ta, ta, rstd, ALU.mult).then_inc(s["var2"], 1)
                dve.wait_ge(s["std2"], 1)
                dve_then(dve, dve.reciprocal(tb, tok["c"][:, :]))
                scale = tok["rt"][:, :]
                dve_then(dve, dve.tensor_tensor(scale, tb, rstd, ALU.mult))
            for t in range(NT):
                dve.tensor_scalar(tile_(HAT, t), tile_(src, t), mean[:, t:t + 1], scale[:, t:t + 1],
                                  ALU.subtract, ALU.mult).then_inc(s["hat"], 1)

        def ln_act(act, s, twice):
            act.wait_ge(s["var"], 1)
            act.activation(tok["std"][:, :], tok["var"][:, :], ACT.Sqrt, bias=EPS[:, 0:1]).then_inc(s["std"], 1)
            if twice:
                act.wait_ge(s["var2"], 1)
                act.activation(tok["c"][:, :], tok["a"][:, :], ACT.Sqrt, bias=EPS[:, 0:1]).then_inc(s["std2"], 1)

        def transpose_pe(pe, s):
            for c in range(NC):
                pe.wait_ge(s["hat"], 4 * c + 4)
                for i in range(4):
                    last = pe.transpose(bank[c][:, i * P:(i + 1) * P], tile_(HAT, 4 * c + i), IDF[:, :])
                last.then_inc(s["xt_ps"], 1)

        def transpose_act(act, s, gain=None, bias=None):
            for c in range(NC):
                act.wait_ge(s["xt_ps"], c + 1)
                dst = XT[:, c * CH:(c + 1) * CH]
                if gain is None:
                    act.activation(dst, bank[c][:, :], ACT.Copy).then_inc(s["xt"], 1)
                else:
                    act.activation(dst, bank[c][:, :], ACT.Identity, scale=gain, bias=bias).then_inc(s["xt"], 1)

        def attn_a_pe(pe):
            s = pa
            transpose_pe(pe, s)
            for c in range(NC):
                pe.wait_ge(s["xt"], c + 1)
                xc = XT[:, c * CH:(c + 1) * CH]
                if c == 0:
                    pe.wait_ge(ld["wa"], 48)
                if c >= 2:
                    pe.wait_ge(s["q_ev"], c - 1)
                    pe.wait_ge(s["k_ev"], c - 1)
                pe.matmul(bank[4 + c % 2][:, :], wa["Qw"][:, :], xc, start=True, stop=True).then_inc(s["q_ps"], 1)
                pe.matmul(bank[6 + c % 2][:, :], wa["Kw"][:, :], xc, start=True, stop=True).then_inc(s["k_ps"], 1)
                for i in range(4):
                    last = pe.matmul(bank[c][:, i * P:(i + 1) * P], tile_(XT, 4 * c + i), wa["Vw"][:, :],
                                     start=True, stop=True)
                last.then_inc(s["v_ps"], 1)
            pe.wait_ge(s["q_ev"], NC)
            pe.wait_ge(s["k_ev"], NC)
            pe.wait_ge(s["v_ev"], NC)
            for step_ in range(NT + 2):
                t = step_
                if t < NT:
                    b, w = t // 2, (t % 2 + 1) * P
                    at_least(pe, s["exped"], t - 1)
                    pe.matmul(bank[t % 2][:, 0:w], tile_(QT, t), KT[:, b * S:b * S + w], start=True, stop=False)
                    pe.matmul(bank[t % 2][:, w - P:w], IDB[:, :], MSK[:, 0:P], start=False, stop=True)\
                        .then_inc(s["scored"], 1)
                t = step_ - 1
                if 0 <= t < NT:
                    pe.wait_ge(s["exped"], t + 1)
                    at_least(pe, s["pt"], t - 1)
                    for k in range(t % 2 + 1):
                        last = pe.transpose(bank[2 + t % 2][:, k * P:(k + 1) * P],
                                            PA[:, (t % 2) * S + k * P:(t % 2) * S + (k + 1) * P], IDF[:, :])
                    last.then_inc(s["pt_ps"], 1)
                t = step_ - 2
                if 0 <= t < NT:
                    pe.wait_ge(s["pt"], t + 1)
                    at_least(pe, s["done"], t - 1)
                    n = t % 2 + 1
                    for k in range(n):
                        last = pe.matmul(bank[4 + t % 2][:, 0:P], PT[:, (t % 2) * S + k * P:(t % 2) * S + (k + 1) * P],
                                         tile_(V, 2 * (t // 2) + k), start=(k == 0), stop=(k == n - 1))
                    last.then_inc(s["o_ps"], 1)

        def attn_a_act(act):
            s = pa
            act.wait_ge(cst["dve"], 1)
            ln_act(act, s, False)
            transpose_act(act, s)
            for c in range(NC):
                act.wait_ge(s["q_ps"], c + 1)
                act.activation(QT[:, c * CH:(c + 1) * CH], bank[4 + c % 2][:, :], ACT.Copy).then_inc(s["q_ev"], 1)
                act.wait_ge(s["v_ps"], c + 1)
                act.activation(V[:, c * CH:(c + 1) * CH], bank[c][:, :], ACT.Copy).then_inc(s["v_ev"], 1)
            for t in range(NT):
                w = (t % 2 + 1) * P
                act.wait_ge(s["maxed"], t + 1)
                at_least(act, s["pt_ps"], t - 1)
                act.activation(PA[:, (t % 2) * S:(t % 2) * S + w], bank[t % 2][:, 0:w], ACT.Exp,
                               bias=tok["nm"][:, t:t + 1], scale=float(P) ** -0.5,
                               accum_out=tok["rs"][:, t:t + 1]).then_inc(s["exped"], 1)

        def attn_a_dve(dve):
            s = pa
            dve.wait_ge(ld["x"], 16)
            ln_dve(dve, s, X, False)
            for c in range(NC):
                dve.wait_ge(s["k_ps"], c + 1)
                dve.tensor_copy(KT[:, c * CH:(c + 1) * CH], bank[6 + c % 2][:, :]).then_inc(s["k_ev"], 1)
            for step_ in range(NT + 2):
                t = step_
                if t < NT:
                    w = (t % 2 + 1) * P
                    dve.wait_ge(s["scored"], t + 1)
                    dve_then(dve, dve.tensor_reduce(out=tok["a"][:, t:t + 1], in_=bank[t % 2][:, 0:w], axis=AX_X,
                                                    op=ALU.max))
                    dve.tensor_scalar(tok["nm"][:, t:t + 1], tok["a"][:, t:t + 1], -(float(P) ** -0.5), None,
                                      ALU.mult).then_inc(s["maxed"], 1)
                t = step_ - 1
                if 0 <= t < NT:
                    w = (t % 2 + 1) * P
                    dve.wait_ge(s["pt_ps"], t + 1)
                    at_least(dve, s["o_ps"], t - 1)
                    dve.tensor_copy(PT[:, (t % 2) * S:(t % 2) * S + w], bank[2 + t % 2][:, 0:w]).then_inc(s["pt"], 1)
                t = step_ - 2
                if 0 <= t < NT:
                    dve_then(dve, dve.reciprocal(tok["b"][:, t:t + 1], tok["rs"][:, t:t + 1]))
                    dve.wait_ge(s["o_ps"], t + 1)
                    dve.scalar_tensor_tensor(out=tile_(X, t), in0=bank[4 + t % 2][:, 0:P], scalar=tok["b"][:, t:t + 1],
                                             in1=tile_(X, t), op0=ALU.mult, op1=ALU.add).then_inc(s["done"], 1)

        def slot_of(b):
            return (b % SLOTS) * SLOT

        def core_pe(pe, s, causal, wout):
            def scores(b, n):
                if n == 0:
                    pe.wait_ge(s["qk_ready"], b + 1)
                at_least(pe, s["maxed"], 16 * b + n - 1)
                dst = bank[n % 2]
                k = KS[0:ROWS, bass.ds(slot_of(b) + n * S, S)]
                for qt in range(2):
                    d = dst[:, qt * S:(qt + 1) * S]
                    last = pe.matmul(d, QS[0:ROWS, bass.ds(slot_of(b) + n * S + qt * P, P)], k,
                                     start=True, stop=not causal)
                    if causal and qt == 0:
                        last = pe.matmul(d, IDB[:, :], MSK[:, :], start=False, stop=True)
                    elif causal:
                        last = pe.matmul(d[:, P:S], IDB[:, :], MSK[:, 0:P], start=False, stop=True)
                last.then_inc(s["scored"], 1)

            def shifted(b, n):
                if n == 0:
                    pe.wait_ge(s["shift0"], 32 * (b + 1))
                if n == 8:
                    pe.wait_ge(s["shift1"], 32 * (b + 1))
                at_least(pe, s["exped"], 16 * b + n - 1)
                dst = bank[2 + n % 2]
                for kt in range(2):
                    lo = P if causal and kt else 0
                    d = dst[:, kt * S:kt * S + S - lo]
                    last = pe.matmul(d, KS[0:AUG, bass.ds(slot_of(b) + n * S + kt * P, P)],
                                     QS[0:AUG, bass.ds(slot_of(b) + n * S + lo, S - lo)],
                                     start=True, stop=not causal)
                    if causal:
                        last = pe.matmul(d[:, 0:P], IDB[:, :], MSKT[:, :], start=False, stop=True)
                last.then_inc(s["st"], 1)

            def maxima(b, u):
                pe.wait_ge(s["maxed"], 16 * b + 8 * u + 8)
                at_least(pe, s["m_lo"], 2 * b + u)
                for qt in range(2):
                    last = pe.transpose(bank[5][0:8, u * S + qt * P:u * S + (qt + 1) * P],
                                        MN[:, u * 16 + qt * 8:u * 16 + qt * 8 + 8], IDF[:, :])
                last.then_inc(s["m_t"], 1)

            def values(b, q, kt):
                if kt == 0:
                    pe.wait_ge(s["exped"], 16 * b + 4 * q + 4)
                    pe.wait_ge(s["v_padded"], 4 * b + q + 1)
                if kt == 0 and q == 0:
                    at_least(pe, s["raw0"], b)
                if kt == 0 and q == 2:
                    at_least(pe, s["raw1"], b)
                lo = P if causal and kt else 0
                for j in range(4):
                    h, n = 4 * j + q, 4 * q + j
                    last = pe.matmul(bank[4 if q < 2 else 7][32 * j:32 * j + 32, lo:S],
                                     VP[:, (kt * H + h) * 32:(kt * H + h + 1) * 32],
                                     PR[:, (n % 8) * CH + kt * S:(n % 8) * CH + kt * S + S - lo],
                                     start=(q % 2 == 0 and kt == 0), stop=(q % 2 == 1 and kt == 1))
                if kt == 1:
                    last.then_inc(s["pv"], 1)

            def select(b, k):
                g = k % 2
                if k == 0:
                    pe.wait_ge(s["raw0"], b + 1)
                    at_least(pe, s["added"], b)
                if k == 1:
                    pe.wait_ge(s["raw1"], b + 1)
                o = (1 - k // 2) * S
                last = pe.matmul(bank[6][:, o:o + S], (SELD, SELN)[k // 2][g][:, :], RAW[g],
                                 start=(g == 0), stop=(g == 1))
                if k == 3:
                    last.then_inc(s["selected"], 1)

            def project(b):
                pe.wait_ge(s["normed"], b + 1)
                for i in range(2):
                    last = pe.matmul(bank[6][:, i * P:(i + 1) * P], OT[:, i * P:(i + 1) * P], wout[:, :],
                                     start=True, stop=True)
                last.then_inc(s["projected"], 1)

            def batch(b, now, before, last_):
                for n in range(H):
                    if now:
                        scores(b, n)
                    if before:
                        shifted(b - 1, n)
                    q, odd = n // 4, n % 2
                    if odd and q == 0 and last_:
                        values(b - 2, 3, n // 2)
                    if odd and q > 0 and before:
                        values(b - 1, q - 1, n // 2 % 2)
                    if n == 1 and before:
                        maxima(b - 1, 1)
                    if n == 9 and now:
                        maxima(b, 0)
                    if n in (6, 7, 8) and last_:
                        select(b - 2, n - 6)
                    if n == 8 and last_:
                        select(b - 2, 3)
                    if n == 14 and last_:
                        project(b - 2)

            pe.wait_ge(s_pre["q_done"], 2 * NC)
            batch(0, True, False, False)
            batch(1, True, True, False)
            with pe.Fori(2, B) as b:
                batch(b, True, True, True)
            batch(B, False, True, True)
            batch(B + 1, False, False, True)

        def core_act(act, s, causal):
            def exps(b, n):
                act.wait_ge(s["st"], 16 * b + n + 1)
                if n % 4 == 0:
                    at_least(act, s["pv"], 4 * b + n // 4 - 1)
                w = CH - P if causal else CH
                act.activation(PR[:, (n % 8) * CH:(n % 8) * CH + w], bank[2 + n % 2][:, 0:w], ACT.Exp,
                               scale=HEAD_SCALE).then_inc(s["exped"], 1)

            def high(b, u):
                act.wait_ge(s["m_t"], 2 * b + u + 1)
                at_least(act, s["shift1"] if u else s["shift0"], 32 * b)
                act.activation(MHI[:, u * S:(u + 1) * S], bank[5][0:8, u * S:(u + 1) * S], ACT.Copy)\
                    .then_inc(s["m_hi"], 1)

            def raw(b, g):
                act.wait_ge(s["pv"], 4 * b + 2 * g + 2)
                at_least(act, s["selected"], b)
                act.activation(RAW[g], bank[7 if g else 4][:, 0:S], ACT.Copy).then_inc(s["raw1" if g else "raw0"], 1)

            def batch(b, now, before, last_):
                for n in range(H):
                    if before:
                        exps(b - 1, n)
                    if n == 2 and before:
                        high(b - 1, 1)
                    if n == 4 and last_:
                        raw(b - 2, 1)
                    if n == 10 and now:
                        high(b, 0)
                    if n == 13 and before:
                        raw(b - 1, 0)

            batch(0, True, False, False)
            batch(1, True, True, False)
            with act.Fori(2, B) as b:
                batch(b, True, True, True)
            batch(B, False, True, True)
            batch(B + 1, False, False, True)

        def core_dve(dve, s, acc):
            def maximum(b, n):
                dve.wait_ge(s["scored"], 16 * b + n + 1)
                if n % 8 == 0:
                    at_least(dve, s["m_t"], 2 * b - 1 + n // 8)
                u = n // 8
                o = MN[:, u * 16:(u + 1) * 16].rearrange("p (t n) -> p t n", n=8)[:, :, n % 8]
                dve.tensor_reduce(out=o, in_=bank[n % 2][:, :].rearrange("p (t k) -> p t k", k=S), axis=AX_X,
                                  op=ALU.max, negate=True).then_inc(s["maxed"], 1)

            def low(b, u):
                dve.wait_ge(s["m_hi"], 2 * b + u + 1)
                at_least(dve, s["shift1"] if u else s["shift0"], 32 * b)
                dve.tensor_tensor(MLO[:, u * S:(u + 1) * S], bank[5][0:8, u * S:(u + 1) * S],
                                  MHI[:, u * S:(u + 1) * S], ALU.subtract).then_inc(s["m_lo"], 1)

            def invert(b, i):
                dve.wait_ge(s["selected"], b + 1)
                dve.reciprocal(RC[:, i * P:(i + 1) * P], bank[6][:, S + i * P:S + (i + 1) * P]).then_inc(s["inverted"], 1)

            def divide(b):
                dve.wait_ge(s["inverted"], 2 * b + 2)
                at_least(dve, s["projected"], b)
                dve.tensor_tensor(OT[:, :], bank[6][:, 0:S], RC[:, :], ALU.mult).then_inc(s["normed"], 1)

            def add(b):
                dve.wait_ge(s["projected"], b + 1)
                d = acc[:, bass.ds(b * S, S)]
                dve.tensor_tensor(d, d, bank[6][:, 0:S], ALU.add).then_inc(s["added"], 1)

            def batch(b, now, before, last_):
                for n in range(H):
                    if now:
                        maximum(b, n)
                    if n == 3 and before:
                        low(b - 1, 1)
                    if n in (9, 10) and last_:
                        invert(b - 2, n - 9)
                    if n == 11 and now:
                        low(b, 0)
                    if n == 12 and last_:
                        divide(b - 2)
                    if n == 15 and last_:
                        add(b - 2)

            if acc is U:
                dve.wait_ge(s_pre["u0"], NT + 1)
            batch(0, True, False, False)
            batch(1, True, True, False)
            with dve.Fori(2, B) as b:
                batch(b, True, True, True)
            batch(B, False, True, True)
            batch(B + 1, False, False, True)

        def core_pool(pool, s):
            def pad(b):
                src = V[:, bass.ds(b * S, S)].rearrange("p (k j r d) -> p k j r d", k=2, j=4, r=4)
                dst = VP[:, :].rearrange("p (k j r c) -> p k j r c", k=2, j=4, r=4)
                for r in range(4):
                    at_least(pool, s["pv"], 4 * b - 3 + r)
                    o = 16 * (r % 2)
                    pool.tensor_copy(dst[:, :, :, r, o:o + DH], src[:, :, :, r, :]).then_inc(s["v_padded"], 1)

            pool.wait_ge(s_pre["v_ev"], NC)
            pad(0)
            with pool.Fori(1, B) as b:
                pad(b)

        def core_sp(sp, s, parts):
            def store_parts(c):
                sp.wait_ge(s_pre["q_done"], 2 * (c + 1))
                for x, buf in ((0, QP), (1, KP)):
                    for i in range(3):
                        sp.dma_start(bass.AP(qk_parts, (3 * x + i) * PART + 2 * c * PB, [[S, P], [PB, 2], [1, S]]),
                                     buf[:, i * T + c * CH:i * T + (c + 1) * CH]).then_inc(parts[c], 16)

            def load(b):
                sp.wait_ge(parts[b // 2], 96)
                at_least(sp, s["st"], 16 * (b - SLOTS + 1))
                sem, o = (s["qk_in0"], s["qk_in1"])[b % 2], slot_of(b)
                for i in range(3):
                    rows = slice(3 * DH * i, 3 * DH * (i + 1))
                    sp.dma_start(QS[rows, o:o + SLOT],
                                 bass.AP(qk_parts, i * PART + b * PB, [[0, 3], [SLOT, DH], [1, SLOT]])).then_inc(sem, 16)
                    sp.dma_start(KS[rows, o:o + SLOT],
                                 bass.AP(qk_parts, 3 * PART + b * PB, [[PART, 3], [SLOT, DH], [1, SLOT]]))\
                        .then_inc(sem, 16)

            def ready(b):
                sp.wait_ge((s["qk_in0"], s["qk_in1"])[b % 2], 96 * (b // 2 + 1))
                sp.sem_inc(s["qk_ready"], 1)

            def shift(b, u):
                sp.wait_ge(s["m_lo"], 2 * b + u + 1)
                o = slot_of(b) + u * 8 * S
                for row, m in ((ROWS, MHI), (ROWS + 1, MLO)):
                    sp.dma_start(QS[row:row + 1, o:o + 8 * S].rearrange("o (n t) -> o n t", t=S),
                                 m[:, u * S:(u + 1) * S]).then_inc(s["shift1"] if u else s["shift0"], 16)

            for c in range(NC):
                store_parts(c)
                if c == 1:
                    load(0)
                    load(1)
            ready(0)
            for b in range(B + 1):
                if 1 <= b < B - 1:
                    load(b + 1)
                if b >= 1:
                    shift(b - 1, 1)
                if b < B:
                    shift(b, 0)
                if b + 1 < B:
                    ready(b + 1)

        def ffn_pre_pe(pe, s):
            transpose_pe(pe, s)
            for c in range(NC):
                pe.wait_ge(s["xt"], c + 1)
                xc = XT[:, c * CH:(c + 1) * CH]
                at_least(pe, s["r2"], 2 * (c - 1))
                pe.matmul(bank[4 + c % 2][:, :], WQ[:, :], xc, start=True, stop=True).then_inc(s["q_ps"], 1)
                pe.matmul(bank[6 + c % 2][:, :], WK[:, :], xc, start=True, stop=True).then_inc(s["k_ps"], 1)
                for i in range(4):
                    last = pe.matmul(bank[c][:, i * P:(i + 1) * P], tile_(XT, 4 * c + i), WV[:, :],
                                     start=True, stop=True)
                last.then_inc(s["v_ps"], 1)

        def ffn_pre_act(act, s):
            ln_act(act, s, True)
            transpose_act(act, s, G1, BE1)
            for c in range(NC):
                for i, (sem, bk, bias, buf) in enumerate(((s["q_ps"], 4, BQ, QP), (s["k_ps"], 6, BK, KP))):
                    act.wait_ge(sem, c + 1)
                    act.activation(buf[:, c * CH:(c + 1) * CH], bank[bk + c % 2][:, :], ACT.Identity, bias=bias)\
                        .then_inc(s["qa"], 1)
                for i, buf in enumerate((QP, KP)):
                    act.wait_ge(s["r2"], 2 * c + i + 1)
                    act.activation(buf[:, T + c * CH:T + (c + 1) * CH], RES[:, i * CH:(i + 1) * CH], ACT.Copy)\
                        .then_inc(s["ka"], 1)

        def ffn_pre_dve(dve, s):
            ln_dve(dve, s, X, True)
            for c in range(NC):
                for i, (bk, bias, buf) in enumerate(((4, BQ, QP), (6, BK, KP))):
                    dve.wait_ge(s["qa"], 2 * c + i + 1)
                    at_least(dve, s["q_done"], 2 * (c - 1) + i + 1)
                    dve.scalar_tensor_tensor(out=RES[:, i * CH:(i + 1) * CH], in0=bank[bk + c % 2][:, :], scalar=bias,
                                             in1=buf[:, c * CH:(c + 1) * CH], op0=ALU.add, op1=ALU.subtract)\
                        .then_inc(s["r2"], 1)
                dve.wait_ge(s["v_ps"], c + 1)
                dve.tensor_tensor(V[:, c * CH:(c + 1) * CH].rearrange("p (t n) -> p t n", n=P),
                                  bank[c][:, :].rearrange("p (t n) -> p t n", n=P),
                                  BVR[:, :].rearrange("p (o n) -> p o n", o=1).to_broadcast([P, 4, P]), ALU.add)\
                    .then_inc(s["v_ev"], 1)
                for i, buf in enumerate((QP, KP)):
                    dve.wait_ge(s["ka"], 2 * c + i + 1)
                    dve.tensor_tensor(buf[:, 2 * T + c * CH:2 * T + (c + 1) * CH], RES[:, i * CH:(i + 1) * CH],
                                      buf[:, T + c * CH:T + (c + 1) * CH], ALU.subtract).then_inc(s["q_done"], 1)

        def ffn_pre_pool(pool, s):
            for t in range(NT):
                pool.wait_ge(s["hat"], t + 1)
                pool.tensor_scalar(tile_(U, t), tile_(HAT, t), tok["c"][:, t:t + 1], None, ALU.mult)\
                    .then_inc(s["u0"], 1)
            pool.wait_ge(s["u0"], NT)
            u = U[:, :].rearrange("p (t n) -> p t n", n=P)
            pool.tensor_tensor(u, u, BOR[:, :].rearrange("p (o n) -> p o n", o=1).to_broadcast([P, NT, P]), ALU.add)\
                .then_inc(s["u0"], 1)

        def expert_reg(eng, i):
            return eng.value_load(EXI[0:1, i:i + 1], min_val=0, max_val=E - 1)

        def ffn_post_pe(pe, s):
            v = dict(hat=s["v_hat"], xt_ps=s["v_xt_ps"])
            transpose_pe(pe, v)
            for t in range(NT):
                if t % 4 == 0:
                    pe.wait_ge(s["v_xt"], t // 4 + 1)
                last = pe.matmul(bank[4][:, t * E:(t + 1) * E], tile_(XT, t), GW[:, :], start=True, stop=True)
            last.then_inc(s["logits"], 1)
            pe.wait_ge(s["hot"], 1)
            pe.matmul(bank[5][:, 0:P], TRI[:, :], HOTB[:, :], start=True, stop=True)
            pe.matmul(bank[5][:, P:2 * P], ONB[:, :], HOTB[:, :], start=True, stop=True).then_inc(s["prefix"], 1)
            pe.wait_ge(s["experts"], 1)
            xs = (s["xs0"], s["xs1"], s["xs2"], s["xs3"])
            for k in range(NR + 3):
                i = k
                if i < NR:
                    pe.wait_ge(xs[i % 4], 16 * (i // 4 + 1))
                    at_least(pe, s["x_tb"], i - 1)
                    pe.transpose(bank[i % 2][:, 0:P], XS[i % 4], IDF[:, :]).then_inc(s["x_t"], 1)
                i = k - 1
                if 0 <= i < NR:
                    e = expert_reg(pe, i)
                    pe.wait_ge(s["x_tb"], i + 1)
                    at_least(pe, s["mid"], i - 1)
                    pe.matmul(bank[2 + i % 2][:, :], XST[i % 2], W1[:, bass.ds(e * F, F)], start=True, stop=True)\
                        .then_inc(s["up"], 1)
                i = k - 2
                if 0 <= i < NR:
                    pe.wait_ge(s["mid"], i + 1)
                    at_least(pe, s["m_tb"], i - 1)
                    for c in range(FC):
                        last = pe.transpose(bank[4 + i % 2][:, c * P:(c + 1) * P], MID[i % 2][:, c * P:(c + 1) * P],
                                            IDF[:, :])
                    last.then_inc(s["m_t"], 1)
                i = k - 3
                if 0 <= i < NR:
                    e = expert_reg(pe, i)
                    pe.wait_ge(s["m_tb"], i + 1)
                    at_least(pe, s["y"], i - 1)
                    for c in range(FC):
                        last = pe.matmul(bank[6 + i % 2][:, 0:P], MIDT[i % 2][:, c * P:(c + 1) * P],
                                         W2[:, bass.ds(e * F + c * P, P)], start=(c == 0), stop=(c == FC - 1))
                    last.then_inc(s["down"], 1)

        def ffn_post_act(act, s):
            ln_act(act, dict(var=s["v_var"], std=s["v_std"]), False)
            transpose_act(act, dict(xt_ps=s["v_xt_ps"], xt=s["v_xt"]), G2, BE2)
            for k in range(NR + 2):
                i = k
                if i < NR:
                    act.wait_ge(s["x_t"], i + 1)
                    at_least(act, s["up"], i - 1)
                    act.activation(XST[i % 2], bank[i % 2][:, 0:P], ACT.Identity, scale=G2, bias=BE2).then_inc(s["x_tb"], 1)
                i = k - 2
                if 0 <= i < NR:
                    act.wait_ge(s["m_t"], i + 1)
                    at_least(act, s["down"], i - 1)
                    act.activation(MIDT[i % 2], bank[4 + i % 2][:, :], ACT.Relu).then_inc(s["m_tb"], 1)

        def ffn_post_dve(dve, s, rows):
            ln_dve(dve, dict(var=s["v_var"], std=s["v_std"], hat=s["v_hat"]), U, False)
            dve.wait_ge(s["logits"], 1)

            def te(buf):
                return buf.rearrange("p (t e) -> p t e", e=E)

            def over_t(row):
                return row.rearrange("p (o e) -> p o e", o=1).to_broadcast([P, NT, E])

            def over_e(col):
                return col.rearrange("p (t o) -> p t o", o=1).to_broadcast([P, NT, E])

            lg, eq, hot, cnt, s0, s1, sl = (te(R[n]) for n in ("lg", "eq", "hot", "cnt", "s0", "s1", "slot"))
            dve_then(dve, dve.tensor_tensor(lg, te(bank[4][:, 0:P]), over_t(GBR[:, :]), ALU.add))
            dve_then(dve, dve.tensor_reduce(out=TOP[:, :], in_=lg, axis=AX_X, op=ALU.max))
            dve_then(dve, dve.tensor_tensor(eq, lg, over_e(TOP[:, :]), ALU.is_equal))
            dve_then(dve, dve.tensor_tensor(eq, eq, over_t(REV[:, :]), ALU.mult))
            dve_then(dve, dve.tensor_reduce(out=TOP[:, :], in_=eq, axis=AX_X, op=ALU.max))
            dve_then(dve, dve.tensor_tensor(hot, over_e(TOP[:, :]), over_t(REV[:, :]), ALU.is_equal))
            dve.tensor_copy(HOTB[:, :], R["hot"]).then_inc(s["hot"], 1)
            dve.wait_ge(s["prefix"], 1)
            dve_then(dve, dve.tensor_copy(cnt, te(bank[5][:, P:2 * P])))
            src, dst, other = cnt, s0, s1
            for d in (1, 2, 4, 8):
                dve.tensor_copy(dst[:, 0:d, :], src[:, 0:d, :])
                dve_then(dve, dve.tensor_tensor(dst[:, d:, :], src[:, d:, :], src[:, 0:NT - d, :], ALU.add))
                src, dst, other = dst, other, dst
            total = src[:, NT - 1, :]
            cmp_n = CMP[:, 0:E * NT].rearrange("p (e j) -> p e j", j=NT)
            dve_then(dve, dve.tensor_tensor(cmp_n, total.rearrange("p (e o) -> p e o", o=1).to_broadcast([P, E, NT]),
                                            J128[:, :].rearrange("p (o j) -> p o j", o=1).to_broadcast([P, E, NT]),
                                            ALU.is_gt))
            dve_then(dve, dve.tensor_reduce(out=RT_["n"][:, :], in_=cmp_n, axis=AX_X, op=ALU.add))
            a_, b_ = RT_["n"], RT_["m0"]
            for d in (1, 2, 4):
                dve.tensor_copy(b_[:, 0:d], a_[:, 0:d])
                dve_then(dve, dve.tensor_tensor(b_[:, d:E], a_[:, d:E], a_[:, 0:E - d], ALU.add))
                a_, b_ = b_, (RT_["m1"] if b_ is RT_["m0"] else RT_["m0"])
            ends = a_
            dve_then(dve, dve.tensor_tensor(RT_["base"][:, :], ends[:, :], RT_["n"][:, :], ALU.subtract))
            dve_then(dve, dve.tensor_scalar(RT_["base"][:, :], RT_["base"][:, :], float(P), None, ALU.mult))
            dve_then(dve, dve.tensor_tensor(sl, src, cnt, ALU.subtract))
            dve_then(dve, dve.tensor_tensor(sl, te(bank[5][:, 0:P]), sl, ALU.add))
            dve_then(dve, dve.tensor_tensor(sl, sl, over_t(RT_["base"][:, :]), ALU.add))
            dve_then(dve, dve.tensor_tensor(sl, sl, hot, ALU.mult))
            dve_then(dve, dve.tensor_reduce(out=SLF[:, :], in_=sl, axis=AX_X, op=ALU.add))
            dve.tensor_copy(SLOTI[:, :], SLF[:, :]).then_inc(s["slots"], 1)
            cmp_i = CMP[:, :].rearrange("p (i e) -> p i e", e=E)
            dve_then(dve, dve.tensor_tensor(cmp_i, ends[:, :].rearrange("p (o e) -> p o e", o=1).to_broadcast([P, NR, E]),
                                            I24[:, :].rearrange("p (i o) -> p i o", o=1).to_broadcast([P, NR, E]),
                                            ALU.is_le))
            dve_then(dve, dve.tensor_reduce(out=EXF[:, :], in_=cmp_i, axis=AX_X, op=ALU.add))
            dve_then(dve, dve.tensor_scalar(EXF[:, :], EXF[:, :], float(E - 1), None, ALU.min))
            dve.tensor_copy(EXI[:, :], EXF[:, :]).then_inc(s["experts"], 1)
            dve.wait_ge(s["experts"], 1)
            ys = (s["ys0"], s["ys1"], s["ys2"], s["ys3"])
            for k in range(1, NR + 3):
                i = k - 1
                if i < NR:
                    e = expert_reg(dve, i)
                    dve.wait_ge(s["up"], i + 1)
                    at_least(dve, s["m_t"], i - 1)
                    dve.tensor_tensor(MID[i % 2], bank[2 + i % 2][:, :], B1R[:, bass.ds(e * F, F)], ALU.add)\
                        .then_inc(s["mid"], 1)
                i = k - 3
                if 0 <= i < NR:
                    e = expert_reg(dve, i)
                    dve.wait_ge(s["down"], i + 1)
                    at_least(dve, ys[i % 4], 16 * (i // 4))
                    dve.tensor_tensor(YS[i % 4], bank[6 + i % 2][:, 0:P], B2R[:, bass.ds(e * P, P)], ALU.add)\
                        .then_inc(s["y"], 1)
            for c in range(NC):
                c4 = slice(c * CH, (c + 1) * CH)
                dve.tensor_tensor(X[:, c4], X[:, c4], U[:, c4], ALU.add).then_inc(s["xu"], 1)
            dve.wait_ge(s["xu"], NC)
            dve.wait_ge(rows["gathered"], 16 * NT)
            for c in range(NC):
                c4 = slice(c * CH, (c + 1) * CH)
                dve.tensor_tensor(X[:, c4], X[:, c4], GATH[:, c4], ALU.add).then_inc(s["done"], 1)

        def rows_of(t):
            return bass.IndirectOffsetOnAxis(SLOTI[:, t:t + 1], 0)

        def ffn_post_pool(pool, s, rows):
            pool.wait_ge(s["slots"], 1)
            for t in range(NT):
                pool.indirect_dma_start(bass.AP(routed_x, 0, [[P, NR * P], [1, P]]), rows_of(t), tile_(HAT, t), None)\
                    .then_inc(rows["scattered"], 16)
            ys = (s["ys0"], s["ys1"], s["ys2"], s["ys3"])
            for i in range(4):
                pool.wait_ge(ys[i], 16 * ((NR - 1 - i) // 4 + 1))
            for t in range(NT):
                pool.indirect_dma_start(tile_(GATH, t), None, bass.AP(routed_y, 0, [[P, NR * P], [1, P]]), rows_of(t))\
                    .then_inc(rows["gathered"], 16)

        def ffn_post_sp(sp, s, rows):
            xs = (s["xs0"], s["xs1"], s["xs2"], s["xs3"])
            ys = (s["ys0"], s["ys1"], s["ys2"], s["ys3"])

            def store(i):
                sp.wait_ge(s["y"], i + 1)
                sp.dma_start(bass.AP(routed_y, i * P * P, [[P, P], [1, P]]), YS[i % 4]).then_inc(ys[i % 4], 16)

            sp.wait_ge(rows["scattered"], 16 * NT)
            for i in range(NR):
                at_least(sp, s["x_t"], i - 3)
                sp.dma_start(XS[i % 4], bass.AP(routed_x, i * P * P, [[P, P], [1, P]])).then_inc(xs[i % 4], 16)
                if i >= 6:
                    store(i - 6)
            for i in range(NR - 6, NR):
                store(i)

        def b_pre_pe(pe, s):
            pe.wait_ge(s["bd"], 1)
            pe.matmul(bank[4][:, 0:P], TW[0:64, 0:P], TW[0:64, P:2 * P], start=True, stop=True)
            pe.matmul(bank[4][:, P:2 * P], TW[:, 2 * P:3 * P], TW[:, 3 * P:4 * P], start=True, stop=True)
            pe.matmul(bank[4][:, 2 * P:3 * P], TW[0:64, 4 * P:5 * P], TW[0:64, 5 * P:6 * P], start=True, stop=True)
            pe.matmul(bank[4][:, 3 * P:4 * P], TW[:, 2 * P:3 * P], TW[:, 6 * P:7 * P], start=True, stop=True)\
                .then_inc(s["bd_ps"], 1)
            transpose_pe(pe, s)
            pe.wait_ge(s["bd"], 2)
            for c in range(NC):
                pe.wait_ge(s["xt"], c + 1)
                xc = XT[:, c * CH:(c + 1) * CH]
                for i in range(4):
                    last = pe.matmul(bank[c][:, i * P:(i + 1) * P], tile_(XT, 4 * c + i), BDV[:, :],
                                     start=True, stop=True)
                last.then_inc(s["v_ps"], 1)
                at_least(pe, s["kq"], 2 * c)
                pe.matmul(bank[4][:, :], BDQ[:, :], xc, start=True, stop=True).then_inc(s["q_ps"], 1)
                pe.matmul(bank[5][:, :], BDK[:, :], xc, start=True, stop=True).then_inc(s["q_ps"], 1)
                for i in range(2):
                    pe.wait_ge(s["sq"], 2 * c + i + 1)
                    at_least(pe, s["sd"], 2 * c + i)
                    pe.matmul(bank[6][:, :], BON[:, :], TW[:, i * CH:(i + 1) * CH], start=True, stop=True)\
                        .then_inc(s["ms_ps"], 1)
                pe.matmul(bank[7][:, :], BDG[:, :], xc, start=True, stop=True).then_inc(s["g_ps"], 1)

        def b_pre_act(act, s):
            ln_act(act, s, False)
            transpose_act(act, s)
            for c in range(NC):
                for i in range(2):
                    act.wait_ge(s["q_ps"], 2 * c + i + 1)
                    at_least(act, s["ms_ps"], 2 * (c - 1) + i + 1)
                    act.activation(TW[:, i * CH:(i + 1) * CH], bank[4 + i][:, :], ACT.Square).then_inc(s["sq"], 1)
                for i in range(2):
                    act.wait_ge(s["ms_ps"], 2 * c + i + 1)
                    at_least(act, s["kq"], 2 * (c - 1) + i + 1)
                    act.activation(TW[:, (2 + i) * CH:(3 + i) * CH], bank[6][:, :], ACT.Sqrt, bias=EPS[:, 1:2])\
                        .then_inc(s["sd"], 1)
                for i, buf in enumerate((QP, KP)):
                    act.wait_ge(s["kq"], 2 * c + i + 1)
                    act.activation(buf[:, c * CH:(c + 1) * CH], TW[:, (4 + i) * CH:(5 + i) * CH], ACT.Copy)\
                        .then_inc(s["qa"], 1)
                for i, buf in enumerate((QP, KP)):
                    act.wait_ge(s["r2"], 2 * c + i + 1)
                    act.activation(buf[:, T + c * CH:T + (c + 1) * CH], RES[:, i * CH:(i + 1) * CH], ACT.Copy)\
                        .then_inc(s["ka"], 1)

        def b_pre_dve(dve, s):
            def tiled(dst, src, by_head, n):
                rep = src.rearrange("p (o d) -> p o d", o=1) if by_head else src.rearrange("p (d o) -> p d o", o=1)
                shape = [n, H, DH] if by_head else [n, DH, H]
                view = dst.rearrange("p (a b) -> p a b", b=shape[2])
                return dve.tensor_copy(view, rep.to_broadcast(shape))

            tiled(TW[0:64, 0:P], SMALL[0:64, 0:8], True, 64)
            tiled(TW[0:64, P:2 * P], SMALL[0:64, 8:16], False, 64)
            tiled(TW[:, 2 * P:3 * P], SMALL[:, 16:24], True, P)
            tiled(TW[:, 3 * P:4 * P], SMALL[:, 24:32], False, P)
            tiled(TW[0:64, 4 * P:5 * P], SMALL[0:64, 40:48], True, 64)
            tiled(TW[0:64, 5 * P:6 * P], SMALL[0:64, 48:56], False, 64)
            tiled(TW[:, 6 * P:7 * P], SMALL[:, 32:40], True, P).then_inc(s["bd"], 1)
            dve.tensor_tensor(BDO[:, :].rearrange("p (h o) -> p h o", o=DH),
                              BLK[:, :].rearrange("p (h o) -> p h o", o=DH),
                              SMALL[:, 56:64].rearrange("p (x o) -> p x o", x=1).to_broadcast([P, H, DH]), ALU.mult)
            dve.wait_ge(s["bd_ps"], 1)
            for i, (dst, blk) in enumerate(((BDQ, BLKP), (BDK, BLKP), (BDG, BLKP), (BDV, BLK))):
                last = dve.tensor_tensor(dst[:, :], bank[4][:, i * P:(i + 1) * P], blk[:, :], ALU.mult)
            last.then_inc(s["bd"], 1)
            ln_dve(dve, s, X, False)
            for c in range(NC):
                dve.wait_ge(s["v_ps"], c + 1)
                dve.tensor_copy(V[:, c * CH:(c + 1) * CH], bank[c][:, :]).then_inc(s["v_ev"], 1)
                for i, w in enumerate((QNW, KNW)):
                    dve.wait_ge(s["sd"], 2 * c + i + 1)
                    inv, dst = TW[:, (2 + i) * CH:(3 + i) * CH], TW[:, (4 + i) * CH:(5 + i) * CH]
                    at_least(dve, s["qa"], 2 * (c - 1) + i + 1)
                    dve_then(dve, dve.reciprocal(inv, inv))
                    norm = dve.scalar_tensor_tensor(out=dst, in0=bank[4 + i][:, :], scalar=w, in1=inv,
                                                    op0=ALU.mult, op1=ALU.mult)
                    if i == 0:
                        norm.then_inc(s["kq"], 1)
                    else:
                        dve_then(dve, norm)
                        dve.wait_ge(s["g_ps"], c + 1)
                        dve.tensor_tensor(dst, bank[7][:, :], dst, ALU.add).then_inc(s["kq"], 1)
                for i, buf in enumerate((QP, KP)):
                    dve.wait_ge(s["qa"], 2 * c + i + 1)
                    at_least(dve, s["q_done"], 2 * (c - 1) + i + 1)
                    dve.wait_ge(s["kq"], 2 * c + i + 1)
                    dve.tensor_tensor(RES[:, i * CH:(i + 1) * CH], TW[:, (4 + i) * CH:(5 + i) * CH],
                                      buf[:, c * CH:(c + 1) * CH], ALU.subtract).then_inc(s["r2"], 1)
                for i, buf in enumerate((QP, KP)):
                    dve.wait_ge(s["ka"], 2 * c + i + 1)
                    dve.tensor_tensor(buf[:, 2 * T + c * CH:2 * T + (c + 1) * CH], RES[:, i * CH:(i + 1) * CH],
                                      buf[:, T + c * CH:T + (c + 1) * CH], ALU.subtract).then_inc(s["q_done"], 1)

        def parts_of(p):
            return (p["parts0"], p["parts1"], p["parts2"], p["parts3"])

        block = ctx.enter_context(nc.Block())

        @block.sync
        def _(sp):
            sp.dma_start(X[:, :].rearrange("p (t c) -> p t c", c=P),
                         bass.AP(a["x"].tensor, 0, [[P, P], [P * P, NT], [1, P]])).then_inc(ld["x"], 16)
            for n in ("Qw", "Kw", "Vw"):
                sp.dma_start(wa[n][:, :], a[n]).then_inc(ld["wa"], 16)

            def column(dst, name, dims, first=0):
                sp.dma_start(dst, bass.AP(a[name].tensor, first, dims)).then_inc(ld["small"], 16)

            def repeated(dst, name, n, sem):
                sp.dma_start(dst, bass.AP(a[name].tensor, 0, [[0, P], [1, n]])).then_inc(sem, 16)

            for dst, name in ((WN[:, 0:P], "wq"), (WN[:, P:2 * P], "wk"), (WV[:, :], "wv"), (WO[:, :], "wo")):
                sp.dma_start(dst, a[name]).then_inc(ld["ffn"], 16)
            sp.dma_start(GW[:, :], a["gate_w"]).then_inc(ld["ffn"], 16)
            repeated(GBR[:, :], "gate_b", E, ld["ffn"])
            repeated(BVR[:, :], "bv", P, ld["ffn"])
            repeated(BOR[:, :], "bo", P, ld["ffn"])
            for dst, name in ((G1, "ln1_g"), (BE1, "ln1_b"), (G2, "ln2_g"), (BE2, "ln2_b")):
                column(dst, name, [[1, P], [1, 1]])
            for dst, name in ((BQ, "bq"), (BK, "bk")):
                for d in range(DH):
                    column(dst[H * d:H * (d + 1), :], name, [[DH, 4], [4 * DH, 4]], d)
            for dst, name in ((QNW, "q_norm_w"), (KNW, "k_norm_w")):
                column(dst, name, [[1, DH], [0, H]])
            column(SMALL[0:64, 0:8], "W_DQ", [[8, 64], [1, 8]])
            column(SMALL[0:64, 8:16], "W_UQ", [[1, 64], [64, 8]])
            column(SMALL[:, 16:24], "W_DKV", [[8, P], [1, 8]])
            column(SMALL[:, 24:40], "W_UKV", [[1, P], [P, 16]])
            column(SMALL[0:64, 40:48], "W_KR", [[8, 64], [1, 8]])
            column(SMALL[0:64, 48:56], "W_QR", [[8, 64], [1, 8]])
            for o in range(DH):
                column(SMALL[:, 56 + o:57 + o], "W_O", [[0, H], [1, DH]], DH * o)
            sp.dma_start(W1[:, :].rearrange("p (e f) -> p e f", f=F),
                         bass.AP(a["w1"].tensor, 0, [[F, P], [P * F, E], [1, F]])).then_inc(ld["moe"], 16)
            sp.dma_start(W2[:, :].rearrange("p (g n) -> p g n", n=P),
                         bass.AP(a["w2"].tensor, 0, [[P, P], [P * P, E * FC], [1, P]])).then_inc(ld["moe"], 16)
            repeated(B1R[:, :], "b1", E * F, ld["moe"])
            repeated(B2R[:, :], "b2", E * P, ld["moe"])
            sp.wait_ge(cst["dve"], 1)
            for k in range(3):
                n = min(8, NR - 8 * k)
                sp.dma_start(bass.AP(routed_x, 8 * k * P * P, [[P, P], [P * P, n], [1, P]]),
                             U[:, 0:n * P].rearrange("p (i c) -> p i c", c=P)).then_inc(ld["zero"], 16)
            sp.wait_ge(ld["zero"], 48)
            sp.wait_ge(ld["moe"], 64)
            sp.wait_ge(ld["ffn"], 128)
            sp.wait_ge(ld["small"], 36 * 16)
            k = 1
            phase_end(sp, ph["sp"], k)
            for n, layer in enumerate(LAYERS):
                if n:
                    clear(sp, s_post)
                core_sp(sp, s_core, parts_of(s_pre))
                k += 1
                phase_end(sp, ph["sp"], k)
                clear(sp, s_pre)
                clear(sp, s_core)
                if layer is ATTN_B:
                    k += 1
                    phase_end(sp, ph["sp"], k)
                else:
                    ffn_post_sp(sp, s_post, routed[n])
                    k += 1
                    phase_end(sp, ph["sp"], k)
            sp.dma_start(bass.AP(out.tensor, 0, [[P, P], [P * P, NT], [1, P]]),
                         X[:, :].rearrange("p (t c) -> p t c", c=P)).then_inc(s_out, 16)
            sp.wait_ge(s_out, 16)

        @block.gpsimd
        def _(pool):
            built = 0

            def done(ins, k=1):
                nonlocal built
                ins.then_inc(cst["pool"], 1)
                built += 1
                if k:
                    pool.wait_ge(cst["pool"], built)

            def where(buf, pattern, cm, base, op, fill):
                done(pool.affine_select(out=buf, in_=buf, compare_op=op, fill=fill, base=base, pattern=pattern,
                                        channel_multiplier=cm))

            for buf, v in ((IDF, 0.0), (IDB, 0.0), (MSK, NEG), (MSKT, 0.0), (TRI, 1.0), (BLK, 1.0), (BLKP, 1.0),
                           (BON, 0.0), (SELN[0], 0.0), (SELN[1], 0.0), (SELD[0], 0.0), (SELD[1], 0.0)):
                done(pool.memset(buf[:, :], v))
            done(pool.memset(MSK[:, 0:P], 0.0))
            for buf in (IDF, IDB):
                where(buf[:, :], [[-1, P]], 1, 0, ALU.not_equal, 1.0)
            where(MSK[:, 0:P], [[-1, P]], 1, 0, ALU.is_ge, NEG)
            where(MSKT[:, :], [[1, P]], -1, 0, ALU.is_ge, NEG)
            where(TRI[:, :], [[1, P]], -1, -1, ALU.is_ge, 0.0)
            for g in range(2):
                for sel, base, d in ((SELN[g], 0, -1), (SELD[g], -DH, 0)):
                    v = sel[:, :].rearrange("p (j r d) -> p j r d", j=4, r=4)[:, :, 2 * g:2 * g + 2, :]
                    where(v, [[-32, 4], [-16, 2], [d, DH]], 1, base, ALU.not_equal, 1.0)
            v = BLK[:, :].rearrange("p (h d) -> p h d", d=DH)
            where(v, [[-DH, H], [0, DH]], 1, 0, ALU.is_ge, 0.0)
            where(v, [[DH, H], [0, DH]], -1, DH - 1, ALU.is_ge, 0.0)
            v = BLKP[:, :].rearrange("p (d r j) -> p d r j", r=4, j=4)
            where(v, [[0, DH], [-DH, 4], [-4 * DH, 4]], 1, 0, ALU.is_ge, 0.0)
            where(v, [[0, DH], [DH, 4], [4 * DH, 4]], -1, DH - 1, ALU.is_ge, 0.0)
            v = BON[:, :].rearrange("p (d n) -> p d n", n=H)
            for d in range(DH):
                where(v, [[0, DH], [-1, H]], 1, -H * d, ALU.not_equal, 1.0 / DH)
            done(pool.iota(REV[:, :], [[-1, E]], base=E, channel_multiplier=0, allow_small_or_imprecise_dtypes=True))
            done(pool.iota(J128[:, :], [[P, NT]], base=0, channel_multiplier=0, allow_small_or_imprecise_dtypes=True))
            done(pool.iota(I24[:, :], [[1, NR]], base=0, channel_multiplier=0, allow_small_or_imprecise_dtypes=True))
            pool.wait_ge(ld["ffn"], 128)
            for i, dst in enumerate((WQ, WK)):
                src = WN[:, i * P:(i + 1) * P].rearrange("p (j r d) -> p j r d", j=4, r=4)
                view = dst[:, :].rearrange("p (d r j) -> p d r j", r=4, j=4)
                for r in range(4):
                    done(pool.tensor_copy(view[:, :, r, :].rearrange("p d j -> p j d"), src[:, :, r, :]), 0)
            k = 1
            phase_end(pool, ph["pool"], k)
            for n, layer in enumerate(LAYERS):
                if layer is FFN:
                    ffn_pre_pool(pool, s_pre)
                core_pool(pool, s_core)
                k += 1
                phase_end(pool, ph["pool"], k)
                if layer is FFN:
                    ffn_post_pool(pool, s_post, routed[n])
                k += 1
                phase_end(pool, ph["pool"], k)

        @block.scalar
        def _(act):
            attn_a_act(act)
            k = 1
            phase_end(act, ph["act"], k)
            for n, layer in enumerate(LAYERS):
                if layer is ATTN_B:
                    b_pre_act(act, s_pre)
                else:
                    ffn_pre_act(act, s_pre)
                core_act(act, s_core, layer is ATTN_B)
                k += 1
                phase_end(act, ph["act"], k)
                if layer is FFN:
                    ffn_post_act(act, s_post)
                k += 1
                phase_end(act, ph["act"], k)

        @block.vector
        def _(dve):
            dve.memset(EPS[:, 0:1], LN_EPS)
            dve.memset(EPS[:, 1:2], RMS_EPS)
            dve.memset(ONB[:, :], 1.0)
            dve_then(dve, dve.memset(VP[:, :], 0.0))
            for i in range(2):
                v = VP[:, :].rearrange("p (kj g i c) -> p kj g i c", g=2, i=2, c=32)
                dve.memset(v[:, :, :, i, 16 * i + DH:16 * i + DH + 1], 1.0)
            dve.memset(KS[64:96, :], 1.0)
            dve.memset(U[:, 0:8 * P], 0.0).then_inc(cst["dve"], 1)
            attn_a_dve(dve)
            k = 1
            phase_end(dve, ph["dve"], k)
            for n, layer in enumerate(LAYERS):
                if layer is ATTN_B:
                    b_pre_dve(dve, s_pre)
                else:
                    ffn_pre_dve(dve, s_pre)
                core_dve(dve, s_core, X if layer is ATTN_B else U)
                k += 1
                phase_end(dve, ph["dve"], k)
                if layer is FFN:
                    ffn_post_dve(dve, s_post, routed[n])
                k += 1
                phase_end(dve, ph["dve"], k)

        @block.tensor
        def _(pe):
            pe.wait_ge(cst["pool"], 19)
            attn_a_pe(pe)
            k = 1
            phase_end(pe, ph["pe"], k)
            for n, layer in enumerate(LAYERS):
                if layer is ATTN_B:
                    b_pre_pe(pe, s_pre)
                else:
                    ffn_pre_pe(pe, s_pre)
                core_pe(pe, s_core, layer is ATTN_B, BDO if layer is ATTN_B else WO)
                k += 1
                phase_end(pe, ph["pe"], k)
                if layer is FFN:
                    ffn_post_pe(pe, s_post)
                k += 1
                phase_end(pe, ph["pe"], k)


_A, _B, _FF = "L0_attn_a_", "L0_attn_b_", "L0_ffn_"
_NAMES = {n: _A + n for n in ("x", "Qw", "Kw", "Vw")}
_NAMES |= {n: _B + n for n in ("W_DQ", "W_UQ", "W_DKV", "W_UKV", "W_QR", "W_KR", "W_O", "q_norm_w", "k_norm_w")}
_NAMES |= {n: _FF + n for n in ("ln1_g", "ln1_b", "ln2_g", "ln2_b", "wq", "bq", "wk", "bk", "wv", "bv", "wo", "bo",
                                "gate_w", "gate_b", "w1", "b1", "w2", "b2")}


def kernel(**inputs):
    import numpy as np
    import concourse.bacc as bacc
    from concourse.bass_utils import run_bass_kernel_spmd

    nc = bacc.Bacc("TRN2", target_bir_lowering=False, num_devices=1)
    arrays, args = {}, {}
    for short, name in _NAMES.items():
        arr = np.ascontiguousarray(inputs[name])
        arrays[f"in_{short}"] = arr
        args[short] = nc.dram_tensor(f"in_{short}", arr.shape, mybir.dt.from_np(arr.dtype), kind="ExternalInput").ap()
    out = nc.dram_tensor("out_x", (B, S, P), F32, kind="ExternalOutput").ap()
    hybrid_block_kernel(nc, args, out)
    r = run_bass_kernel_spmd(nc, [arrays], core_ids=[0])
    return r.results[0]["out_x"]
```

```python
from contextlib import ExitStack

import concourse.bass as bass
from concourse import mybir

F32 = mybir.dt.float32
BF16 = mybir.dt.bfloat16
I32 = mybir.dt.int32
ALU = mybir.AluOpType
ACT = mybir.ActivationFunctionType
AX_X = mybir.AxisListType.X

P = 128
B, S = 8, 256
T = B * S
NT = T // P
CH = 512
NC = T // CH
H, DH = 16, 8
E, F = 8, 512
FC = F // P
NR = NT + E - 1
ROWS = 9 * DH
AUG = ROWS + 2
ROW = P + 1
SLOTS = 3
SLOT = H * S
LN_EPS = 1e-5
RMS_EPS = 1.1920929e-07
NEG = -1e30
HEAD_SCALE = DH ** -0.5
PART = P * T
PB = P * S


def at_least(eng, sem, count):
    if isinstance(count, int) and count <= 0:
        return
    eng.wait_ge(sem, count)


def hybrid_block_kernel(nc, a, out):
    ctx = ExitStack()
    with ctx:
        ctx.enter_context(nc.allow_non_contiguous_dma("small weights are laid out on load"))

        def sb(name, shape, dt=F32):
            return ctx.enter_context(nc.sbuf_tensor(name, shape, dt))

        def sems(prefix, names):
            each = {n: ctx.enter_context(nc.semaphore(prefix + "_" + n)) for n in names.split()}
            return each

        qk_parts = nc.dram_tensor("qk_parts", (2, 3, B, P * S), BF16, kind="Internal")
        routed_x = [nc.dram_tensor(f"routed_x{i}", (NR * P, ROW), F32, kind="Internal") for i in range(2)]
        moe_out = nc.dram_tensor("moe_out", (T + NR * P, P), F32, kind="Internal")

        X = sb("X", [P, T])
        HAT = sb("HAT", [P, NT * ROW])
        U = sb("U", [P, T])
        V = sb("V", [P, T])
        XT = sb("XT", [P, T])
        QP = sb("QP", [P, 3 * T], BF16)
        KP = sb("KP", [P, 3 * T], BF16)
        QS = sb("QS", [P, SLOTS * SLOT], BF16)
        KS = sb("KS", [P, SLOTS * SLOT], BF16)
        VP = sb("VP", [P, 2 * H * 32])
        PR = sb("PR", [P, 8 * CH])
        OT = sb("OT", [P, S])
        RC = sb("RC", [P, S])
        RES = sb("RES", [P, 2 * CH])
        MN = sb("MN", [P, 2 * 2 * 8])
        MHI = sb("MHI", [8, 2 * S], BF16)
        MLO = sb("MLO", [8, 2 * S], BF16)
        W1 = sb("W1", [P, E * F])
        W2 = sb("W2", [P, E * F])
        B1C = sb("B1C", [P, E * FC])
        B2R = sb("B2R", [P, E * P])
        wa = {n: sb("a_" + n, [P, P]) for n in ("Qw", "Kw", "Vw")}
        WN = RES[:, 0:2 * P]
        WQ, WK, WV, WO = (sb(n, [P, P]) for n in ("WQ", "WK", "WV", "WO"))
        GW = sb("GW", [P, E])
        GBR = sb("GBR", [P, E])
        BVR = sb("BVR", [P, P])
        BOR = sb("BOR", [P, P])
        COLS = sb("COLS", [P, 8])
        BQ, BK, G1, BE1, G2, BE2, QNW, KNW = (COLS[:, i:i + 1] for i in range(8))
        EPS = sb("EPS", [P, 2])
        TABLE = sb("TABLE", [P, 1])
        BDQ, BDK, BDG, BDV, BDO = (sb(n, [P, P]) for n in ("BDQ", "BDK", "BDG", "BDV", "BDO"))
        SMALL = sb("SMALL", [P, 64])
        IDF = sb("IDF", [P, P])
        IDB = sb("IDB", [P, P], BF16)
        MSK = sb("MSK", [P, 2 * P], BF16)
        MSKT = sb("MSKT", [P, P], BF16)
        TRI = sb("TRI", [P, P], BF16)
        ONB = sb("ONB", [P, P], BF16)
        SELN = [sb(f"SELN{g}", [P, P]) for g in range(2)]
        SELD = [sb(f"SELD{g}", [P, P]) for g in range(2)]
        BLK = sb("BLK", [P, P])
        BLKP = sb("BLKP", [P, P])
        BON = sb("BON", [P, P])
        REV = sb("REV", [P, E])
        J128 = sb("J128", [P, NT])
        I24 = sb("I24", [P, NR])
        ST = sb("ST", [P, NT * 6])
        tok = {n: sb("t_" + n, [P, NT]) for n in ("a", "b", "mean", "var", "std", "rstd", "c", "rt", "nm", "rs")}
        R = {n: RES[:, i * P:(i + 1) * P] for i, n in enumerate(("lg", "eq", "hot", "cnt", "s0", "s1", "slot"))}
        HOTB = sb("HOTB", [P, NT * E], BF16)
        RT_ = {n: sb("r_" + n, [P, E]) for n in ("n", "m0", "m1", "base")}
        TOP = sb("TOP", [P, NT])
        SLF = sb("SLF", [P, NT])
        SLOTI = sb("SLOTI", [P, NT], I32)
        CMP = RC[:, 0:NR * E]
        EXF = sb("EXF", [P, NR])
        EXI = sb("EXI", [P, NR], I32)
        IDS = sb("IDS", [P, NR], I32)

        bank = [ctx.enter_context(nc.psum_tensor(f"bank{i}", [P, CH], F32)) for i in range(8)]

        QT = QS[:, 0:2 * T].bitcast(F32)
        KT = QS[:, 2 * T:4 * T].bitcast(F32)
        PA = PR[:, 0:2 * S]
        PT = PR[:, 2 * S:4 * S]
        TW = PR
        TWS = V
        XS = [PR[:, i * ROW:(i + 1) * ROW] for i in range(4)]
        XST, YS, W1S, MIDT = ([PR[:, 4 * ROW + o + i * w:4 * ROW + o + (i + 1) * w] for i in range(n)]
                              for o, w, n in ((0, P, 2), (2 * P, P, 4), (6 * P, F, 2), (14 * P, F, 2)))
        FILL = QP[:, 0:2 * NR * ROW].bitcast(F32)
        GATH = XT
        RAW = [RES[:, g * S:(g + 1) * S] for g in range(2)]

        ld = sems("ld", "x wa wb ffn blk small moe zero")
        cst = sems("cst", "pool dve fill")
        ph = sems("phase", "pe act dve pool sp")
        step = sems("step", "dve act")
        norm_names = "var std hat xt_ps xt "
        parts_names = " qa ka r2 q_done parts0 parts1 parts2 parts3"
        pa = sems("a", norm_names + "q_ps k_ps v_ps q_ev k_ev v_ev scored maxed exped pt_ps pt o_ps done")
        core_names = ("qk_in0 qk_in1 qk_ready scored maxed m_t m_hi m_lo shift0 shift1 st exped pv v_padded raw0 raw1 selected "
                      "inverted normed projected added")
        ffn_names = ("v_var v_std v_hat v_xt_ps v_xt logits hot prefix slots experts "
                     "xs0 xs1 xs2 xs3 x_t x_tb w1 up mid relu down y xu back0 back1 back2 back3 done")
        s_pre = sems("p", norm_names + "var2 std2 q_ps k_ps v_ps v_ev u0 sq ms_ps sd g_ps kq" + parts_names)
        s_core = sems("c", core_names)
        s_post = sems("e", ffn_names)
        routed = [sems(f"rows{i}", "scattered out0 out1 out2 out3") for i in range(2)]
        prep = sems("prep", "repeated product blocks")
        FFN, ATTN_B = "ffn", "attention b"
        LAYERS = (FFN, ATTN_B, FFN)
        EARLY = 12
        s_out = ctx.enter_context(nc.semaphore("s_out"))

        counts = {"dve": 0, "act": 0}

        def dve_then(dve, ins):
            counts["dve"] += 1
            ins.then_inc(step["dve"], 1)
            dve.wait_ge(step["dve"], counts["dve"])

        def phase_end(eng, own, k):
            eng.drain().then_inc(own, 1)
            for other in (ph["pe"], ph["act"], ph["dve"], ph["pool"], ph["sp"]):
                if other is not own:
                    eng.wait_ge(other, k)

        def clear(eng, phase):
            for sem in phase.values():
                eng.sem_clear(sem)

        def tile_(buf, t, n=1):
            return buf[:, t * P:(t + n) * P]

        def hat_(t):
            return HAT[:, t * ROW:t * ROW + P]

        def stats(dve, src, t):
            return dve.bn_stats(ST[:, 6 * t:6 * t + 6], tile_(src, t))

        def ln_dve(dve, s, src, twice, first=0):
            for t in range(first, NT):
                last = stats(dve, src, t)
            if first < NT:
                dve_then(dve, last)
            st = ST[:, :].rearrange("p (t k) -> p t k", k=6)
            me, ve, mo, vo = (st[:, :, i] for i in (1, 2, 4, 5))
            ta, tb, mean, var = (tok[n][:, :] for n in ("a", "b", "mean", "var"))
            dve.tensor_tensor(ta, me, mo, ALU.subtract)
            dve.tensor_tensor(tb, ve, vo, ALU.add)
            dve_then(dve, dve.tensor_tensor(mean, me, mo, ALU.add))
            dve.tensor_scalar(mean, mean, 0.5, None, ALU.mult)
            dve_then(dve, dve.tensor_tensor(ta, ta, ta, ALU.mult))
            dve_then(dve, dve.scalar_tensor_tensor(out=var, in0=ta, scalar=float(P // 4), in1=tb,
                                                   op0=ALU.mult, op1=ALU.add))
            dve.tensor_scalar(var, var, 1.0 / P, None, ALU.mult).then_inc(s["var"], 1)
            dve.wait_ge(s["std"], 1)
            rstd = tok["rstd"][:, :]
            dve_then(dve, dve.reciprocal(rstd, tok["std"][:, :]))
            scale = rstd
            if twice:
                dve_then(dve, dve.tensor_tensor(ta, var, rstd, ALU.mult))
                dve.tensor_tensor(ta, ta, rstd, ALU.mult).then_inc(s["var2"], 1)
                dve.wait_ge(s["std2"], 1)
                dve_then(dve, dve.reciprocal(tb, tok["c"][:, :]))
                scale = tok["rt"][:, :]
                dve_then(dve, dve.tensor_tensor(scale, tb, rstd, ALU.mult))
            for t in range(NT):
                dve.tensor_scalar(hat_(t), tile_(src, t), mean[:, t:t + 1], scale[:, t:t + 1],
                                  ALU.subtract, ALU.mult).then_inc(s["hat"], 1)

        def ln_act(act, s, twice):
            act.activation(TABLE[:, :], EPS[:, 0:1], ACT.Sqrt)
            act.wait_ge(s["var"], 1)
            act.activation(tok["std"][:, :], tok["var"][:, :], ACT.Sqrt, bias=EPS[:, 0:1]).then_inc(s["std"], 1)
            if twice:
                act.wait_ge(s["var2"], 1)
                act.activation(tok["c"][:, :], tok["a"][:, :], ACT.Sqrt, bias=EPS[:, 0:1]).then_inc(s["std2"], 1)

        def transpose_pe(pe, s):
            for c in range(NC):
                pe.wait_ge(s["hat"], 4 * c + 4)
                for i in range(4):
                    last = pe.transpose(bank[c][:, i * P:(i + 1) * P], hat_(4 * c + i), IDF[:, :])
                last.then_inc(s["xt_ps"], 1)

        def transpose_act(act, s, gain=None, bias=None):
            for c in range(NC):
                act.wait_ge(s["xt_ps"], c + 1)
                dst = XT[:, c * CH:(c + 1) * CH]
                if gain is None:
                    act.activation(dst, bank[c][:, :], ACT.Copy).then_inc(s["xt"], 1)
                else:
                    act.activation(dst, bank[c][:, :], ACT.Identity, scale=gain, bias=bias).then_inc(s["xt"], 1)

        def attn_a_pe(pe):
            s = pa
            transpose_pe(pe, s)
            for c in range(NC):
                pe.wait_ge(s["xt"], c + 1)
                xc = XT[:, c * CH:(c + 1) * CH]
                if c == 0:
                    pe.wait_ge(ld["wa"], 48)
                if c >= 2:
                    pe.wait_ge(s["q_ev"], c - 1)
                    pe.wait_ge(s["k_ev"], c - 1)
                pe.matmul(bank[4 + c % 2][:, :], wa["Qw"][:, :], xc, start=True, stop=True).then_inc(s["q_ps"], 1)
                pe.matmul(bank[6 + c % 2][:, :], wa["Kw"][:, :], xc, start=True, stop=True).then_inc(s["k_ps"], 1)
                for i in range(4):
                    last = pe.matmul(bank[c][:, i * P:(i + 1) * P], tile_(XT, 4 * c + i), wa["Vw"][:, :],
                                     start=True, stop=True)
                last.then_inc(s["v_ps"], 1)
            pe.wait_ge(s["q_ev"], NC)
            pe.wait_ge(s["k_ev"], NC)
            pe.wait_ge(s["v_ev"], NC)
            for step_ in range(NT + 2):
                t = step_
                if t < NT:
                    b, w = t // 2, (t % 2 + 1) * P
                    at_least(pe, s["exped"], t - 1)
                    pe.matmul(bank[t % 2][:, 0:w], tile_(QT, t), KT[:, b * S:b * S + w], start=True, stop=False)
                    pe.matmul(bank[t % 2][:, w - P:w], IDB[:, :], MSK[:, 0:P], start=False, stop=True)\
                        .then_inc(s["scored"], 1)
                t = step_ - 1
                if 0 <= t < NT:
                    pe.wait_ge(s["exped"], t + 1)
                    at_least(pe, s["pt"], t - 1)
                    for k in range(t % 2 + 1):
                        last = pe.transpose(bank[2 + t % 2][:, k * P:(k + 1) * P],
                                            PA[:, (t % 2) * S + k * P:(t % 2) * S + (k + 1) * P], IDF[:, :])
                    last.then_inc(s["pt_ps"], 1)
                t = step_ - 2
                if 0 <= t < NT:
                    pe.wait_ge(s["pt"], t + 1)
                    at_least(pe, s["done"], t - 1)
                    n = t % 2 + 1
                    for k in range(n):
                        last = pe.matmul(bank[4 + t % 2][:, 0:P], PT[:, (t % 2) * S + k * P:(t % 2) * S + (k + 1) * P],
                                         tile_(V, 2 * (t // 2) + k), start=(k == 0), stop=(k == n - 1))
                    last.then_inc(s["o_ps"], 1)

        def attn_a_act(act):
            s = pa
            act.wait_ge(cst["dve"], 1)
            ln_act(act, s, False)
            transpose_act(act, s)
            for c in range(NC):
                act.wait_ge(s["q_ps"], c + 1)
                act.activation(QT[:, c * CH:(c + 1) * CH], bank[4 + c % 2][:, :], ACT.Copy).then_inc(s["q_ev"], 1)
                act.wait_ge(s["v_ps"], c + 1)
                act.activation(V[:, c * CH:(c + 1) * CH], bank[c][:, :], ACT.Copy).then_inc(s["v_ev"], 1)
            act.activation(TABLE[:, :], EPS[:, 0:1], ACT.Exp)
            for t in range(NT):
                w = (t % 2 + 1) * P
                act.wait_ge(s["maxed"], t + 1)
                at_least(act, s["pt_ps"], t - 1)
                act.activation(PA[:, (t % 2) * S:(t % 2) * S + w], bank[t % 2][:, 0:w], ACT.Exp,
                               bias=tok["nm"][:, t:t + 1], scale=float(P) ** -0.5,
                               accum_out=tok["rs"][:, t:t + 1]).then_inc(s["exped"], 1)

        def attn_a_dve(dve):
            s = pa
            dve.wait_ge(ld["x"], 16)
            ln_dve(dve, s, X, False)
            for c in range(NC):
                dve.wait_ge(s["k_ps"], c + 1)
                dve.tensor_copy(KT[:, c * CH:(c + 1) * CH], bank[6 + c % 2][:, :]).then_inc(s["k_ev"], 1)
            for step_ in range(NT + 2):
                t = step_
                if t < NT:
                    w = (t % 2 + 1) * P
                    dve.wait_ge(s["scored"], t + 1)
                    dve_then(dve, dve.tensor_reduce(out=tok["a"][:, t:t + 1], in_=bank[t % 2][:, 0:w], axis=AX_X,
                                                    op=ALU.max))
                    dve.tensor_scalar(tok["nm"][:, t:t + 1], tok["a"][:, t:t + 1], -(float(P) ** -0.5), None,
                                      ALU.mult).then_inc(s["maxed"], 1)
                t = step_ - 1
                if 0 <= t < NT:
                    w = (t % 2 + 1) * P
                    dve.wait_ge(s["pt_ps"], t + 1)
                    at_least(dve, s["o_ps"], t - 1)
                    dve.tensor_copy(PT[:, (t % 2) * S:(t % 2) * S + w], bank[2 + t % 2][:, 0:w]).then_inc(s["pt"], 1)
                t = step_ - 2
                if 0 <= t < NT:
                    dve_then(dve, dve.reciprocal(tok["b"][:, t:t + 1], tok["rs"][:, t:t + 1]))
                    dve.wait_ge(s["o_ps"], t + 1)
                    dve.scalar_tensor_tensor(out=tile_(X, t), in0=bank[4 + t % 2][:, 0:P], scalar=tok["b"][:, t:t + 1],
                                             in1=tile_(X, t), op0=ALU.mult, op1=ALU.add).then_inc(s["done"], 1)
                    if t:
                        dve.wait_ge(s["done"], t)
                        stats(dve, X, t - 1)

        def slot_of(b):
            return (b % SLOTS) * SLOT

        def core_pe(pe, s, causal, wout):
            def scores(b, n):
                if n == 0:
                    pe.wait_ge(s["qk_ready"], b + 1)
                at_least(pe, s["maxed"], 16 * b + n - 1)
                dst = bank[n % 2]
                k = KS[0:ROWS, bass.ds(slot_of(b) + n * S, S)]
                for qt in range(2):
                    d = dst[:, qt * S:(qt + 1) * S]
                    last = pe.matmul(d, QS[0:ROWS, bass.ds(slot_of(b) + n * S + qt * P, P)], k,
                                     start=True, stop=not causal)
                    if causal and qt == 0:
                        last = pe.matmul(d, IDB[:, :], MSK[:, :], start=False, stop=True)
                    elif causal:
                        last = pe.matmul(d[:, P:S], IDB[:, :], MSK[:, 0:P], start=False, stop=True)
                last.then_inc(s["scored"], 1)

            def shifted(b, n):
                if n == 0:
                    pe.wait_ge(s["shift0"], 32 * (b + 1))
                if n == 8:
                    pe.wait_ge(s["shift1"], 32 * (b + 1))
                at_least(pe, s["exped"], 16 * b + n - 1)
                dst = bank[2 + n % 2]
                for kt in range(2):
                    lo = P if causal and kt else 0
                    d = dst[:, kt * S:kt * S + S - lo]
                    last = pe.matmul(d, KS[0:AUG, bass.ds(slot_of(b) + n * S + kt * P, P)],
                                     QS[0:AUG, bass.ds(slot_of(b) + n * S + lo, S - lo)],
                                     start=True, stop=not causal)
                    if causal:
                        last = pe.matmul(d[:, 0:P], IDB[:, :], MSKT[:, :], start=False, stop=True)
                last.then_inc(s["st"], 1)

            def maxima(b, u):
                pe.wait_ge(s["maxed"], 16 * b + 8 * u + 8)
                at_least(pe, s["m_lo"], 2 * b + u)
                for qt in range(2):
                    last = pe.transpose(bank[5][0:8, u * S + qt * P:u * S + (qt + 1) * P],
                                        MN[:, u * 16 + qt * 8:u * 16 + qt * 8 + 8], IDF[:, :])
                last.then_inc(s["m_t"], 1)

            def values(b, q, kt):
                if kt == 0:
                    pe.wait_ge(s["exped"], 16 * b + 4 * q + 4)
                    pe.wait_ge(s["v_padded"], 4 * b + q + 1)
                if kt == 0 and q == 0:
                    at_least(pe, s["raw0"], b)
                if kt == 0 and q == 2:
                    at_least(pe, s["raw1"], b)
                lo = P if causal and kt else 0
                for j in range(4):
                    h, n = 4 * j + q, 4 * q + j
                    last = pe.matmul(bank[4 if q < 2 else 7][32 * j:32 * j + 32, lo:S],
                                     VP[:, (kt * H + h) * 32:(kt * H + h + 1) * 32],
                                     PR[:, (n % 8) * CH + kt * S:(n % 8) * CH + kt * S + S - lo],
                                     start=(q % 2 == 0 and kt == 0), stop=(q % 2 == 1 and kt == 1))
                if kt == 1:
                    last.then_inc(s["pv"], 1)

            def select(b, k):
                g = k % 2
                if k == 0:
                    pe.wait_ge(s["raw0"], b + 1)
                    at_least(pe, s["added"], b)
                if k == 1:
                    pe.wait_ge(s["raw1"], b + 1)
                o = (1 - k // 2) * S
                last = pe.matmul(bank[6][:, o:o + S], (SELD, SELN)[k // 2][g][:, :], RAW[g],
                                 start=(g == 0), stop=(g == 1))
                if k == 3:
                    last.then_inc(s["selected"], 1)

            def project(b):
                pe.wait_ge(s["normed"], b + 1)
                for i in range(2):
                    last = pe.matmul(bank[6][:, i * P:(i + 1) * P], OT[:, i * P:(i + 1) * P], wout[:, :],
                                     start=True, stop=True)
                last.then_inc(s["projected"], 1)

            def batch(b, now, before, last_):
                for n in range(H):
                    if now:
                        scores(b, n)
                    if before:
                        shifted(b - 1, n)
                    q, odd = n // 4, n % 2
                    if odd and q == 0 and last_:
                        values(b - 2, 3, n // 2)
                    if odd and q > 0 and before:
                        values(b - 1, q - 1, n // 2 % 2)
                    if n == 1 and before:
                        maxima(b - 1, 1)
                    if n == 9 and now:
                        maxima(b, 0)
                    if n in (6, 7, 8) and last_:
                        select(b - 2, n - 6)
                    if n == 8 and last_:
                        select(b - 2, 3)
                    if n == 14 and last_:
                        project(b - 2)

            pe.wait_ge(s_pre["q_done"], 2 * NC)
            batch(0, True, False, False)
            batch(1, True, True, False)
            with pe.Fori(2, B) as b:
                batch(b, True, True, True)
            batch(B, False, True, True)
            batch(B + 1, False, False, True)

        def core_act(act, s, causal):
            def exps(b, n):
                act.wait_ge(s["st"], 16 * b + n + 1)
                if n % 4 == 0:
                    at_least(act, s["pv"], 4 * b + n // 4 - 1)
                w = CH - P if causal else CH
                act.activation(PR[:, (n % 8) * CH:(n % 8) * CH + w], bank[2 + n % 2][:, 0:w], ACT.Exp,
                               scale=HEAD_SCALE).then_inc(s["exped"], 1)

            def high(b, u):
                act.wait_ge(s["m_t"], 2 * b + u + 1)
                at_least(act, s["shift1"] if u else s["shift0"], 32 * b)
                act.activation(MHI[:, u * S:(u + 1) * S], bank[5][0:8, u * S:(u + 1) * S], ACT.Copy)\
                    .then_inc(s["m_hi"], 1)

            def raw(b, g):
                act.wait_ge(s["pv"], 4 * b + 2 * g + 2)
                at_least(act, s["selected"], b)
                act.activation(RAW[g], bank[7 if g else 4][:, 0:S], ACT.Copy).then_inc(s["raw1" if g else "raw0"], 1)

            def batch(b, now, before, last_):
                for n in range(H):
                    if before:
                        exps(b - 1, n)
                    if n == 2 and before:
                        high(b - 1, 1)
                    if n == 4 and last_:
                        raw(b - 2, 1)
                    if n == 10 and now:
                        high(b, 0)
                    if n == 13 and before:
                        raw(b - 1, 0)

            act.activation(TABLE[:, :], EPS[:, 0:1], ACT.Exp)
            batch(0, True, False, False)
            batch(1, True, True, False)
            with act.Fori(2, B) as b:
                batch(b, True, True, True)
            batch(B, False, True, True)
            batch(B + 1, False, False, True)

        def core_dve(dve, s, acc):
            def maximum(b, n):
                dve.wait_ge(s["scored"], 16 * b + n + 1)
                if n % 8 == 0:
                    at_least(dve, s["m_t"], 2 * b - 1 + n // 8)
                u = n // 8
                o = MN[:, u * 16:(u + 1) * 16].rearrange("p (t n) -> p t n", n=8)[:, :, n % 8]
                dve.tensor_reduce(out=o, in_=bank[n % 2][:, :].rearrange("p (t k) -> p t k", k=S), axis=AX_X,
                                  op=ALU.max, negate=True).then_inc(s["maxed"], 1)

            def low(b, u):
                dve.wait_ge(s["m_hi"], 2 * b + u + 1)
                at_least(dve, s["shift1"] if u else s["shift0"], 32 * b)
                dve.tensor_tensor(MLO[:, u * S:(u + 1) * S], bank[5][0:8, u * S:(u + 1) * S],
                                  MHI[:, u * S:(u + 1) * S], ALU.subtract).then_inc(s["m_lo"], 1)

            def invert(b, i):
                dve.wait_ge(s["selected"], b + 1)
                dve.reciprocal(RC[:, i * P:(i + 1) * P], bank[6][:, S + i * P:S + (i + 1) * P]).then_inc(s["inverted"], 1)

            def divide(b):
                dve.wait_ge(s["inverted"], 2 * b + 2)
                at_least(dve, s["projected"], b)
                dve.tensor_tensor(OT[:, :], bank[6][:, 0:S], RC[:, :], ALU.mult).then_inc(s["normed"], 1)

            def add(b):
                dve.wait_ge(s["projected"], b + 1)
                d = acc[:, bass.ds(b * S, S)]
                dve.tensor_tensor(d, d, bank[6][:, 0:S], ALU.add).then_inc(s["added"], 1)

            def batch(b, now, before, last_):
                for n in range(H):
                    if now:
                        maximum(b, n)
                    if n == 3 and before:
                        low(b - 1, 1)
                    if n == 4 and not now and before:
                        dve.wait_ge(s["added"], EARLY // 2)
                        for t in range(EARLY):
                            stats(dve, acc, t)
                    if n in (9, 10) and last_:
                        invert(b - 2, n - 9)
                    if n == 11 and now:
                        low(b, 0)
                    if n == 12 and last_:
                        divide(b - 2)
                    if n == 15 and last_:
                        add(b - 2)

            if acc is U:
                dve.wait_ge(s_pre["u0"], NT + 1)
            batch(0, True, False, False)
            batch(1, True, True, False)
            with dve.Fori(2, B) as b:
                batch(b, True, True, True)
            batch(B, False, True, True)
            batch(B + 1, False, False, True)

        def core_pool(pool, s):
            def pad(b):
                src = V[:, bass.ds(b * S, S)].rearrange("p (k j r d) -> p k j r d", k=2, j=4, r=4)
                dst = VP[:, :].rearrange("p (k j r c) -> p k j r c", k=2, j=4, r=4)
                for r in range(4):
                    at_least(pool, s["pv"], 4 * b - 3 + r)
                    o = 16 * (r % 2)
                    pool.tensor_copy(dst[:, :, :, r, o:o + DH], src[:, :, :, r, :]).then_inc(s["v_padded"], 1)

            pool.wait_ge(s_pre["v_ev"], NC)
            pad(0)
            with pool.Fori(1, B) as b:
                pad(b)

        def core_sp(sp, s, parts):
            def store_parts(c):
                sp.wait_ge(s_pre["q_done"], 2 * (c + 1))
                for x, buf in ((0, QP), (1, KP)):
                    for i in range(3):
                        sp.dma_start(bass.AP(qk_parts, (3 * x + i) * PART + 2 * c * PB, [[S, P], [PB, 2], [1, S]]),
                                     buf[:, i * T + c * CH:i * T + (c + 1) * CH]).then_inc(parts[c], 16)

            def load(b):
                sp.wait_ge(parts[b // 2], 96)
                at_least(sp, s["st"], 16 * (b - SLOTS + 1))
                sem, o = (s["qk_in0"], s["qk_in1"])[b % 2], slot_of(b)
                for i in range(3):
                    rows = slice(3 * DH * i, 3 * DH * (i + 1))
                    sp.dma_start(QS[rows, o:o + SLOT],
                                 bass.AP(qk_parts, i * PART + b * PB, [[0, 3], [SLOT, DH], [1, SLOT]])).then_inc(sem, 16)
                    sp.dma_start(KS[rows, o:o + SLOT],
                                 bass.AP(qk_parts, 3 * PART + b * PB, [[PART, 3], [SLOT, DH], [1, SLOT]]))\
                        .then_inc(sem, 16)

            def ready(b):
                sp.wait_ge((s["qk_in0"], s["qk_in1"])[b % 2], 96 * (b // 2 + 1))
                sp.sem_inc(s["qk_ready"], 1)

            def shift(b, u):
                sp.wait_ge(s["m_lo"], 2 * b + u + 1)
                o = slot_of(b) + u * 8 * S
                for row, m in ((ROWS, MHI), (ROWS + 1, MLO)):
                    sp.dma_start(QS[row:row + 1, o:o + 8 * S].rearrange("o (n t) -> o n t", t=S),
                                 m[:, u * S:(u + 1) * S]).then_inc(s["shift1"] if u else s["shift0"], 16)

            for c in range(NC):
                store_parts(c)
                if c == 1:
                    load(0)
                    load(1)
            ready(0)
            for b in range(B + 1):
                if 1 <= b < B - 1:
                    load(b + 1)
                if b >= 1:
                    shift(b - 1, 1)
                if b < B:
                    shift(b, 0)
                if b + 1 < B:
                    ready(b + 1)

        def ffn_pre_pe(pe, s):
            transpose_pe(pe, s)
            for c in range(NC):
                pe.wait_ge(s["xt"], c + 1)
                xc = XT[:, c * CH:(c + 1) * CH]
                at_least(pe, s["r2"], 2 * (c - 1))
                pe.matmul(bank[4 + c % 2][:, :], WQ[:, :], xc, start=True, stop=True).then_inc(s["q_ps"], 1)
                pe.matmul(bank[6 + c % 2][:, :], WK[:, :], xc, start=True, stop=True).then_inc(s["k_ps"], 1)
                for i in range(4):
                    last = pe.matmul(bank[c][:, i * P:(i + 1) * P], tile_(XT, 4 * c + i), WV[:, :],
                                     start=True, stop=True)
                last.then_inc(s["v_ps"], 1)

        def ffn_pre_act(act, s):
            ln_act(act, s, True)
            transpose_act(act, s, G1, BE1)
            for c in range(NC):
                for i, (sem, bk, bias, buf) in enumerate(((s["q_ps"], 4, BQ, QP), (s["k_ps"], 6, BK, KP))):
                    act.wait_ge(sem, c + 1)
                    act.activation(buf[:, c * CH:(c + 1) * CH], bank[bk + c % 2][:, :], ACT.Identity, bias=bias)\
                        .then_inc(s["qa"], 1)
                for i, buf in enumerate((QP, KP)):
                    act.wait_ge(s["r2"], 2 * c + i + 1)
                    act.activation(buf[:, T + c * CH:T + (c + 1) * CH], RES[:, i * CH:(i + 1) * CH], ACT.Copy)\
                        .then_inc(s["ka"], 1)

        def ffn_pre_dve(dve, s, first):
            ln_dve(dve, s, X, True, first)
            for c in range(NC):
                for i, (bk, bias, buf) in enumerate(((4, BQ, QP), (6, BK, KP))):
                    dve.wait_ge(s["qa"], 2 * c + i + 1)
                    at_least(dve, s["q_done"], 2 * (c - 1) + i + 1)
                    dve.scalar_tensor_tensor(out=RES[:, i * CH:(i + 1) * CH], in0=bank[bk + c % 2][:, :], scalar=bias,
                                             in1=buf[:, c * CH:(c + 1) * CH], op0=ALU.add, op1=ALU.subtract)\
                        .then_inc(s["r2"], 1)
                dve.wait_ge(s["v_ps"], c + 1)
                dve.tensor_tensor(V[:, c * CH:(c + 1) * CH].rearrange("p (t n) -> p t n", n=P),
                                  bank[c][:, :].rearrange("p (t n) -> p t n", n=P),
                                  BVR[:, :].rearrange("p (o n) -> p o n", o=1).to_broadcast([P, 4, P]), ALU.add)\
                    .then_inc(s["v_ev"], 1)
                for i, buf in enumerate((QP, KP)):
                    dve.wait_ge(s["ka"], 2 * c + i + 1)
                    dve.tensor_tensor(buf[:, 2 * T + c * CH:2 * T + (c + 1) * CH], RES[:, i * CH:(i + 1) * CH],
                                      buf[:, T + c * CH:T + (c + 1) * CH], ALU.subtract).then_inc(s["q_done"], 1)

        def ffn_pre_pool(pool, s):
            for t in range(NT):
                pool.wait_ge(s["hat"], t + 1)
                pool.tensor_scalar(tile_(U, t), hat_(t), tok["c"][:, t:t + 1], None, ALU.mult)\
                    .then_inc(s["u0"], 1)
            pool.wait_ge(s["u0"], NT)
            u = U[:, :].rearrange("p (t n) -> p t n", n=P)
            pool.tensor_tensor(u, u, BOR[:, :].rearrange("p (o n) -> p o n", o=1).to_broadcast([P, NT, P]), ALU.add)\
                .then_inc(s["u0"], 1)

        def expert_reg(eng, i):
            return eng.value_load(EXI[0:1, i:i + 1], min_val=0, max_val=E - 1)

        def ffn_post_pe(pe, s, first_layer):
            v = dict(hat=s["v_hat"], xt_ps=s["v_xt_ps"])
            transpose_pe(pe, v)
            for t in range(NT):
                if t % 4 == 0:
                    pe.wait_ge(s["v_xt"], t // 4 + 1)
                last = pe.matmul(bank[4][:, t * E:(t + 1) * E], tile_(XT, t), GW[:, :], start=True, stop=True)
            last.then_inc(s["logits"], 1)
            pe.wait_ge(s["hot"], 1)
            pe.matmul(bank[5][:, 0:P], TRI[:, :], HOTB[:, :], start=True, stop=True)
            pe.matmul(bank[5][:, P:2 * P], ONB[:, :], HOTB[:, :], start=True, stop=True).then_inc(s["prefix"], 1)
            pe.wait_ge(s["experts"], 1)
            if first_layer:
                b_small_pe(pe)
                pe.wait_ge(prep["blocks"], 1)
            xs = (s["xs0"], s["xs1"], s["xs2"], s["xs3"])
            for k in range(NR + 2):
                i = k
                if i < NR:
                    pe.wait_ge(xs[i % 4], 16 * (i // 4 + 1))
                    at_least(pe, s["x_tb"], i - 1)
                    pe.transpose(bank[i % 2][:, 0:P], XS[i % 4][:, 0:P], IDF[:, :]).then_inc(s["x_t"], 1)
                i = k - 1
                if 0 <= i < NR:
                    pe.wait_ge(s["x_tb"], i + 1)
                    pe.wait_ge(s["w1"], i + 1)
                    at_least(pe, s["mid"], i - 1)
                    for c in range(FC):
                        last = pe.matmul(bank[2 + i % 2][:, c * P:(c + 1) * P], W1S[i % 2][:, c * P:(c + 1) * P],
                                         XST[i % 2], start=True, stop=True)
                    last.then_inc(s["up"], 1)
                i = k - 2
                if 0 <= i < NR:
                    e = expert_reg(pe, i)
                    pe.wait_ge(s["relu"], i + 1)
                    at_least(pe, s["y"], i - 1)
                    for c in range(FC):
                        last = pe.matmul(bank[6 + i % 2][:, 0:P], MIDT[i % 2][:, c * P:(c + 1) * P],
                                         W2[:, bass.ds(e * F + c * P, P)], start=(c == 0), stop=(c == FC - 1))
                    last.then_inc(s["down"], 1)

        def ffn_post_act(act, s):
            ln_act(act, dict(var=s["v_var"], std=s["v_std"]), False)
            transpose_act(act, dict(xt_ps=s["v_xt_ps"], xt=s["v_xt"]), G2, BE2)
            for k in range(NR + 1):
                i = k
                if i < NR:
                    act.wait_ge(s["x_t"], i + 1)
                    at_least(act, s["up"], i - 1)
                    act.activation(XST[i % 2], bank[i % 2][:, 0:P], ACT.Identity, scale=G2, bias=BE2).then_inc(s["x_tb"], 1)
                i = k - 1
                if i >= 0:
                    act.wait_ge(s["mid"], i + 1)
                    act.activation(MIDT[i % 2], MIDT[i % 2], ACT.Relu).then_inc(s["relu"], 1)

        def ffn_post_dve(dve, s, rows, first_layer, last_layer):
            ln_dve(dve, dict(var=s["v_var"], std=s["v_std"], hat=s["v_hat"]), U, False, EARLY)
            dve.wait_ge(s["logits"], 1)

            def te(buf):
                return buf.rearrange("p (t e) -> p t e", e=E)

            def over_t(row):
                return row.rearrange("p (o e) -> p o e", o=1).to_broadcast([P, NT, E])

            def over_e(col):
                return col.rearrange("p (t o) -> p t o", o=1).to_broadcast([P, NT, E])

            lg, eq, hot, cnt, s0, s1, sl = (te(R[n]) for n in ("lg", "eq", "hot", "cnt", "s0", "s1", "slot"))
            dve_then(dve, dve.tensor_tensor(lg, te(bank[4][:, 0:P]), over_t(GBR[:, :]), ALU.add))
            dve_then(dve, dve.tensor_reduce(out=TOP[:, :], in_=lg, axis=AX_X, op=ALU.max))
            dve_then(dve, dve.tensor_tensor(eq, lg, over_e(TOP[:, :]), ALU.is_equal))
            dve_then(dve, dve.tensor_tensor(eq, eq, over_t(REV[:, :]), ALU.mult))
            dve_then(dve, dve.tensor_reduce(out=TOP[:, :], in_=eq, axis=AX_X, op=ALU.max))
            dve_then(dve, dve.tensor_tensor(hot, over_e(TOP[:, :]), over_t(REV[:, :]), ALU.is_equal))
            dve.tensor_copy(HOTB[:, :], R["hot"]).then_inc(s["hot"], 1)
            dve.wait_ge(s["prefix"], 1)
            dve_then(dve, dve.tensor_copy(cnt, te(bank[5][:, P:2 * P])))
            src, dst, other = cnt, s0, s1
            for d in (1, 2, 4, 8):
                dve.tensor_copy(dst[:, 0:d, :], src[:, 0:d, :])
                dve_then(dve, dve.tensor_tensor(dst[:, d:, :], src[:, d:, :], src[:, 0:NT - d, :], ALU.add))
                src, dst, other = dst, other, dst
            total = src[:, NT - 1, :]
            cmp_n = CMP[:, 0:E * NT].rearrange("p (e j) -> p e j", j=NT)
            dve_then(dve, dve.tensor_tensor(cmp_n, total.rearrange("p (e o) -> p e o", o=1).to_broadcast([P, E, NT]),
                                            J128[:, :].rearrange("p (o j) -> p o j", o=1).to_broadcast([P, E, NT]),
                                            ALU.is_gt))
            dve_then(dve, dve.tensor_reduce(out=RT_["n"][:, :], in_=cmp_n, axis=AX_X, op=ALU.add))
            a_, b_ = RT_["n"], RT_["m0"]
            for d in (1, 2, 4):
                dve.tensor_copy(b_[:, 0:d], a_[:, 0:d])
                dve_then(dve, dve.tensor_tensor(b_[:, d:E], a_[:, d:E], a_[:, 0:E - d], ALU.add))
                a_, b_ = b_, (RT_["m1"] if b_ is RT_["m0"] else RT_["m0"])
            ends = a_
            dve_then(dve, dve.tensor_tensor(RT_["base"][:, :], ends[:, :], RT_["n"][:, :], ALU.subtract))
            dve_then(dve, dve.tensor_scalar(RT_["base"][:, :], RT_["base"][:, :], float(P), None, ALU.mult))
            dve_then(dve, dve.tensor_tensor(sl, src, cnt, ALU.subtract))
            dve_then(dve, dve.tensor_tensor(sl, te(bank[5][:, 0:P]), sl, ALU.add))
            dve_then(dve, dve.tensor_tensor(sl, sl, over_t(RT_["base"][:, :]), ALU.add))
            dve_then(dve, dve.tensor_tensor(sl, sl, hot, ALU.mult))
            dve_then(dve, dve.tensor_reduce(out=SLF[:, :], in_=sl, axis=AX_X, op=ALU.add))
            dve.tensor_copy(SLOTI[:, :], SLF[:, :]).then_inc(s["slots"], 1)
            cmp_i = CMP[:, :].rearrange("p (i e) -> p i e", e=E)
            dve_then(dve, dve.tensor_tensor(cmp_i, ends[:, :].rearrange("p (o e) -> p o e", o=1).to_broadcast([P, NR, E]),
                                            I24[:, :].rearrange("p (i o) -> p i o", o=1).to_broadcast([P, NR, E]),
                                            ALU.is_le))
            dve_then(dve, dve.tensor_reduce(out=EXF[:, :], in_=cmp_i, axis=AX_X, op=ALU.add))
            dve_then(dve, dve.tensor_scalar(EXF[:, :], EXF[:, :], float(E - 1), None, ALU.min))
            dve.tensor_copy(EXI[:, :], EXF[:, :]).then_inc(s["experts"], 1)
            dve.wait_ge(s["experts"], 1)
            if first_layer:
                b_small_dve(dve)
            for k in range(NR + 2):
                i = k
                if i < NR:
                    e = expert_reg(dve, i)
                    at_least(dve, s["up"], i - 1)
                    dve.tensor_copy(W1S[i % 2], W1[:, bass.ds(e * F, F)]).then_inc(s["w1"], 1)
                i = k - 1
                if 0 <= i < NR:
                    e = expert_reg(dve, i)
                    dve.wait_ge(s["up"], i + 1)
                    dve.tensor_copy(IDS[:, i:i + 1], XS[i % 4][:, P:ROW].bitcast(I32))
                    at_least(dve, s["down"], i - 1)
                    bias = B1C[:, bass.ds(e * FC, FC)].rearrange("p (c o) -> p c o", o=1).to_broadcast([P, FC, P])
                    dve.tensor_tensor(MIDT[i % 2].rearrange("p (c t) -> p c t", t=P),
                                      bank[2 + i % 2][:, :].rearrange("p (c t) -> p c t", t=P), bias, ALU.add)\
                        .then_inc(s["mid"], 1)
                i = k - 2
                if 0 <= i < NR:
                    e = expert_reg(dve, i)
                    dve.wait_ge(s["down"], i + 1)
                    at_least(dve, rows[f"out{i % 4}"], 16 * (i // 4))
                    dve.tensor_tensor(YS[i % 4], bank[6 + i % 2][:, 0:P], B2R[:, bass.ds(e * P, P)], ALU.add)\
                        .then_inc(s["y"], 1)
            for c in range(NC):
                c4 = slice(c * CH, (c + 1) * CH)
                dve.tensor_tensor(X[:, c4], X[:, c4], U[:, c4], ALU.add).then_inc(s["xu"], 1)
            dve.wait_ge(s["xu"], NC)
            for c in range(NC):
                c4 = slice(c * CH, (c + 1) * CH)
                dve.wait_ge(s[f"back{c}"], 16)
                dve.tensor_tensor(X[:, c4], X[:, c4], GATH[:, c4], ALU.add).then_inc(s["done"], 1)
                if not last_layer:
                    dve.wait_ge(s["done"], c + 1)
                    for t in range(4 * c, 4 * c + 4):
                        stats(dve, X, t)

        def rows_of(t):
            return bass.IndirectOffsetOnAxis(SLOTI[:, t:t + 1], 0)

        def ffn_post_pool(pool, s, rows, rx):
            pool.wait_ge(s["slots"], 1)
            for t in range(NT):
                pool.indirect_dma_start(bass.AP(rx, 0, [[ROW, NR * P], [1, ROW]]), rows_of(t),
                                        HAT[:, t * ROW:(t + 1) * ROW], None).then_inc(rows["scattered"], 16)
            for i in range(NR):
                pool.wait_ge(s["y"], i + 1)
                pool.indirect_dma_start(bass.AP(moe_out, 0, [[P, T + NR * P], [1, P]]),
                                        bass.IndirectOffsetOnAxis(IDS[:, i:i + 1], 0), YS[i % 4], None)\
                    .then_inc(rows[f"out{i % 4}"], 16)

        def ffn_post_sp(sp, s, rows, rx, last_layer):
            xs = (s["xs0"], s["xs1"], s["xs2"], s["xs3"])
            sp.wait_ge(rows["scattered"], 16 * NT)
            for i in range(NR):
                at_least(sp, s["x_t"], i - 3)
                at_least(sp, s["mid"], i - 3)
                sp.dma_start(XS[i % 4], bass.AP(rx, i * P * ROW, [[ROW, P], [1, ROW]])).then_inc(xs[i % 4], 16)
            for i in range(4):
                sp.wait_ge(rows[f"out{i}"], 16 * ((NR - 1 - i) // 4 + 1))
            for c in range(NC):
                sp.dma_start(GATH[:, c * CH:(c + 1) * CH].rearrange("p (t c) -> p t c", c=P),
                             bass.AP(moe_out, c * CH * P, [[P, P], [P * P, CH // P], [1, P]])).then_inc(s[f"back{c}"], 16)
            if last_layer:
                for c in range(NC):
                    sp.wait_ge(s["done"], c + 1)
                    sp.dma_start(bass.AP(out.tensor, c * CH * P, [[P, P], [P * P, CH // P], [1, P]]),
                                 X[:, c * CH:(c + 1) * CH].rearrange("p (t c) -> p t c", c=P)).then_inc(s_out, 16)
                sp.wait_ge(s_out, 16 * NC)

        def b_small_pe(pe):
            pe.wait_ge(prep["repeated"], 1)
            pe.matmul(bank[7][:, 0:P], TWS[0:64, 0:P], TWS[0:64, P:2 * P], start=True, stop=True)
            pe.matmul(bank[7][:, P:2 * P], TWS[:, 2 * P:3 * P], TWS[:, 3 * P:4 * P], start=True, stop=True)
            pe.matmul(bank[7][:, 2 * P:3 * P], TWS[0:64, 4 * P:5 * P], TWS[0:64, 5 * P:6 * P], start=True, stop=True)
            pe.matmul(bank[7][:, 3 * P:4 * P], TWS[:, 2 * P:3 * P], TWS[:, 6 * P:7 * P], start=True, stop=True)\
                .then_inc(prep["product"], 1)

        def b_pre_pe(pe, s):
            transpose_pe(pe, s)
            for c in range(NC):
                pe.wait_ge(s["xt"], c + 1)
                xc = XT[:, c * CH:(c + 1) * CH]
                for i in range(4):
                    last = pe.matmul(bank[c][:, i * P:(i + 1) * P], tile_(XT, 4 * c + i), BDV[:, :],
                                     start=True, stop=True)
                last.then_inc(s["v_ps"], 1)
                at_least(pe, s["kq"], 2 * c)
                pe.matmul(bank[4][:, :], BDQ[:, :], xc, start=True, stop=True).then_inc(s["q_ps"], 1)
                pe.matmul(bank[5][:, :], BDK[:, :], xc, start=True, stop=True).then_inc(s["q_ps"], 1)
                for i in range(2):
                    pe.wait_ge(s["sq"], 2 * c + i + 1)
                    at_least(pe, s["sd"], 2 * c + i)
                    pe.matmul(bank[6][:, :], BON[:, :], TW[:, i * CH:(i + 1) * CH], start=True, stop=True)\
                        .then_inc(s["ms_ps"], 1)
                pe.matmul(bank[7][:, :], BDG[:, :], xc, start=True, stop=True).then_inc(s["g_ps"], 1)

        def b_pre_act(act, s):
            ln_act(act, s, False)
            transpose_act(act, s)
            for c in range(NC):
                for i in range(2):
                    act.wait_ge(s["q_ps"], 2 * c + i + 1)
                    at_least(act, s["ms_ps"], 2 * (c - 1) + i + 1)
                    act.activation(TW[:, i * CH:(i + 1) * CH], bank[4 + i][:, :], ACT.Square).then_inc(s["sq"], 1)
                for i in range(2):
                    act.wait_ge(s["ms_ps"], 2 * c + i + 1)
                    at_least(act, s["kq"], 2 * (c - 1) + i + 1)
                    act.activation(TW[:, (2 + i) * CH:(3 + i) * CH], bank[6][:, :], ACT.Sqrt, bias=EPS[:, 1:2])\
                        .then_inc(s["sd"], 1)
                for i, buf in enumerate((QP, KP)):
                    act.wait_ge(s["kq"], 2 * c + i + 1)
                    act.activation(buf[:, c * CH:(c + 1) * CH], TW[:, (4 + i) * CH:(5 + i) * CH], ACT.Copy)\
                        .then_inc(s["qa"], 1)
                for i, buf in enumerate((QP, KP)):
                    act.wait_ge(s["r2"], 2 * c + i + 1)
                    act.activation(buf[:, T + c * CH:T + (c + 1) * CH], RES[:, i * CH:(i + 1) * CH], ACT.Copy)\
                        .then_inc(s["ka"], 1)

        def b_small_dve(dve):
            def tiled(dst, src, by_head, n):
                rep = src.rearrange("p (o d) -> p o d", o=1) if by_head else src.rearrange("p (d o) -> p d o", o=1)
                shape = [n, H, DH] if by_head else [n, DH, H]
                view = dst.rearrange("p (a b) -> p a b", b=shape[2])
                return dve.tensor_copy(view, rep.to_broadcast(shape))

            tiled(TWS[0:64, 0:P], SMALL[0:64, 0:8], True, 64)
            tiled(TWS[0:64, P:2 * P], SMALL[0:64, 8:16], False, 64)
            tiled(TWS[:, 2 * P:3 * P], SMALL[:, 16:24], True, P)
            tiled(TWS[:, 3 * P:4 * P], SMALL[:, 24:32], False, P)
            tiled(TWS[0:64, 4 * P:5 * P], SMALL[0:64, 40:48], True, 64)
            tiled(TWS[0:64, 5 * P:6 * P], SMALL[0:64, 48:56], False, 64)
            tiled(TWS[:, 6 * P:7 * P], SMALL[:, 32:40], True, P).then_inc(prep["repeated"], 1)
            dve.tensor_tensor(BDO[:, :].rearrange("p (h o) -> p h o", o=DH),
                              BLK[:, :].rearrange("p (h o) -> p h o", o=DH),
                              SMALL[:, 56:64].rearrange("p (x o) -> p x o", x=1).to_broadcast([P, H, DH]), ALU.mult)
            dve.wait_ge(prep["product"], 1)
            for i, (dst, blk) in enumerate(((BDQ, BLKP), (BDK, BLKP), (BDG, BLKP), (BDV, BLK))):
                last = dve.tensor_tensor(dst[:, :], bank[7][:, i * P:(i + 1) * P], blk[:, :], ALU.mult)
            last.then_inc(prep["blocks"], 1)

        def b_pre_dve(dve, s, first):
            ln_dve(dve, s, X, False, first)
            for c in range(NC):
                dve.wait_ge(s["v_ps"], c + 1)
                dve.tensor_copy(V[:, c * CH:(c + 1) * CH], bank[c][:, :]).then_inc(s["v_ev"], 1)
                for i, w in enumerate((QNW, KNW)):
                    dve.wait_ge(s["sd"], 2 * c + i + 1)
                    inv, dst = TW[:, (2 + i) * CH:(3 + i) * CH], TW[:, (4 + i) * CH:(5 + i) * CH]
                    at_least(dve, s["qa"], 2 * (c - 1) + i + 1)
                    dve_then(dve, dve.reciprocal(inv, inv))
                    norm = dve.scalar_tensor_tensor(out=dst, in0=bank[4 + i][:, :], scalar=w, in1=inv,
                                                    op0=ALU.mult, op1=ALU.mult)
                    if i == 0:
                        norm.then_inc(s["kq"], 1)
                    else:
                        dve_then(dve, norm)
                        dve.wait_ge(s["g_ps"], c + 1)
                        dve.tensor_tensor(dst, bank[7][:, :], dst, ALU.add).then_inc(s["kq"], 1)
                for i, buf in enumerate((QP, KP)):
                    dve.wait_ge(s["qa"], 2 * c + i + 1)
                    at_least(dve, s["q_done"], 2 * (c - 1) + i + 1)
                    dve.wait_ge(s["kq"], 2 * c + i + 1)
                    dve.tensor_tensor(RES[:, i * CH:(i + 1) * CH], TW[:, (4 + i) * CH:(5 + i) * CH],
                                      buf[:, c * CH:(c + 1) * CH], ALU.subtract).then_inc(s["r2"], 1)
                for i, buf in enumerate((QP, KP)):
                    dve.wait_ge(s["ka"], 2 * c + i + 1)
                    dve.tensor_tensor(buf[:, 2 * T + c * CH:2 * T + (c + 1) * CH], RES[:, i * CH:(i + 1) * CH],
                                      buf[:, T + c * CH:T + (c + 1) * CH], ALU.subtract).then_inc(s["q_done"], 1)

        def parts_of(p):
            return (p["parts0"], p["parts1"], p["parts2"], p["parts3"])

        block = ctx.enter_context(nc.Block())

        @block.sync
        def _(sp):
            sp.dma_start(X[:, :].rearrange("p (t c) -> p t c", c=P),
                         bass.AP(a["x"].tensor, 0, [[P, P], [P * P, NT], [1, P]])).then_inc(ld["x"], 16)
            for n in ("Qw", "Kw", "Vw"):
                sp.dma_start(wa[n][:, :], a[n]).then_inc(ld["wa"], 16)

            def column(dst, name, dims, first=0):
                sp.dma_start(dst, bass.AP(a[name].tensor, first, dims)).then_inc(ld["small"], 16)

            def repeated(dst, name, n, sem):
                sp.dma_start(dst, bass.AP(a[name].tensor, 0, [[0, P], [1, n]])).then_inc(sem, 16)

            for dst, name in ((WN[:, 0:P], "wq"), (WN[:, P:2 * P], "wk"), (WV[:, :], "wv"), (WO[:, :], "wo")):
                sp.dma_start(dst, a[name]).then_inc(ld["ffn"], 16)
            sp.dma_start(GW[:, :], a["gate_w"]).then_inc(ld["ffn"], 16)
            repeated(GBR[:, :], "gate_b", E, ld["ffn"])
            repeated(BVR[:, :], "bv", P, ld["ffn"])
            repeated(BOR[:, :], "bo", P, ld["ffn"])
            for dst, name in ((G1, "ln1_g"), (BE1, "ln1_b"), (G2, "ln2_g"), (BE2, "ln2_b")):
                column(dst, name, [[1, P], [1, 1]])
            for dst, name in ((BQ, "bq"), (BK, "bk")):
                for d in range(DH):
                    column(dst[H * d:H * (d + 1), :], name, [[DH, 4], [4 * DH, 4]], d)
            for dst, name in ((QNW, "q_norm_w"), (KNW, "k_norm_w")):
                column(dst, name, [[1, DH], [0, H]])
            column(SMALL[0:64, 0:8], "W_DQ", [[8, 64], [1, 8]])
            column(SMALL[0:64, 8:16], "W_UQ", [[1, 64], [64, 8]])
            column(SMALL[:, 16:24], "W_DKV", [[8, P], [1, 8]])
            column(SMALL[:, 24:40], "W_UKV", [[1, P], [P, 16]])
            column(SMALL[0:64, 40:48], "W_KR", [[8, 64], [1, 8]])
            column(SMALL[0:64, 48:56], "W_QR", [[8, 64], [1, 8]])
            for o in range(DH):
                column(SMALL[:, 56 + o:57 + o], "W_O", [[0, H], [1, DH]], DH * o)
            sp.dma_start(W1[:, :].rearrange("p (e f) -> p e f", f=F),
                         bass.AP(a["w1"].tensor, 0, [[F, P], [P * F, E], [1, F]])).then_inc(ld["moe"], 16)
            sp.dma_start(W2[:, :].rearrange("p (g n) -> p g n", n=P),
                         bass.AP(a["w2"].tensor, 0, [[P, P], [P * P, E * FC], [1, P]])).then_inc(ld["moe"], 16)
            for e in range(E):
                sp.dma_start(B1C[:, e * FC:(e + 1) * FC], bass.AP(a["b1"].tensor, e * F, [[1, P], [P, FC]]))\
                    .then_inc(ld["moe"], 16)
            repeated(B2R[:, :], "b2", E * P, ld["moe"])
            sp.wait_ge(cst["fill"], 3)
            for rx in routed_x:
                sp.dma_start(bass.AP(rx, 0, [[ROW, P], [P * ROW, NR], [1, ROW]]),
                             FILL.rearrange("p (i c) -> p i c", c=ROW)).then_inc(ld["zero"], 16)
            sp.wait_ge(ld["zero"], 32)
            sp.wait_ge(ld["moe"], 16 * (3 + E))
            sp.wait_ge(ld["ffn"], 128)
            sp.wait_ge(ld["small"], 36 * 16)
            k = 1
            phase_end(sp, ph["sp"], k)
            for n, layer in enumerate(LAYERS):
                if n:
                    clear(sp, s_post)
                core_sp(sp, s_core, parts_of(s_pre))
                k += 1
                phase_end(sp, ph["sp"], k)
                clear(sp, s_pre)
                clear(sp, s_core)
                if layer is ATTN_B:
                    k += 1
                    phase_end(sp, ph["sp"], k)
                else:
                    ffn_post_sp(sp, s_post, routed[n // 2], routed_x[n // 2], n == len(LAYERS) - 1)
                    k += 1
                    phase_end(sp, ph["sp"], k)

        @block.gpsimd
        def _(pool):
            built = 0

            def done(ins, k=1):
                nonlocal built
                ins.then_inc(cst["pool"], 1)
                built += 1
                if k:
                    pool.wait_ge(cst["pool"], built)

            def where(buf, pattern, cm, base, op, fill):
                done(pool.affine_select(out=buf, in_=buf, compare_op=op, fill=fill, base=base, pattern=pattern,
                                        channel_multiplier=cm))

            for buf, v in ((IDF, 0.0), (IDB, 0.0), (MSK, NEG), (MSKT, 0.0), (TRI, 1.0), (BLK, 1.0), (BLKP, 1.0),
                           (BON, 0.0), (SELN[0], 0.0), (SELN[1], 0.0), (SELD[0], 0.0), (SELD[1], 0.0)):
                done(pool.memset(buf[:, :], v))
            done(pool.memset(MSK[:, 0:P], 0.0))
            for buf in (IDF, IDB):
                where(buf[:, :], [[-1, P]], 1, 0, ALU.not_equal, 1.0)
            where(MSK[:, 0:P], [[-1, P]], 1, 0, ALU.is_ge, NEG)
            where(MSKT[:, :], [[1, P]], -1, 0, ALU.is_ge, NEG)
            where(TRI[:, :], [[1, P]], -1, -1, ALU.is_ge, 0.0)
            for g in range(2):
                for sel, base, d in ((SELN[g], 0, -1), (SELD[g], -DH, 0)):
                    v = sel[:, :].rearrange("p (j r d) -> p j r d", j=4, r=4)[:, :, 2 * g:2 * g + 2, :]
                    where(v, [[-32, 4], [-16, 2], [d, DH]], 1, base, ALU.not_equal, 1.0)
            v = BLK[:, :].rearrange("p (h d) -> p h d", d=DH)
            where(v, [[-DH, H], [0, DH]], 1, 0, ALU.is_ge, 0.0)
            where(v, [[DH, H], [0, DH]], -1, DH - 1, ALU.is_ge, 0.0)
            v = BLKP[:, :].rearrange("p (d r j) -> p d r j", r=4, j=4)
            where(v, [[0, DH], [-DH, 4], [-4 * DH, 4]], 1, 0, ALU.is_ge, 0.0)
            where(v, [[0, DH], [DH, 4], [4 * DH, 4]], -1, DH - 1, ALU.is_ge, 0.0)
            v = BON[:, :].rearrange("p (d n) -> p d n", n=H)
            for d in range(DH):
                where(v, [[0, DH], [-1, H]], 1, -H * d, ALU.not_equal, 1.0 / DH)
            done(pool.iota(REV[:, :], [[-1, E]], base=E, channel_multiplier=0, allow_small_or_imprecise_dtypes=True))
            done(pool.iota(J128[:, :], [[P, NT]], base=0, channel_multiplier=0, allow_small_or_imprecise_dtypes=True))
            done(pool.iota(I24[:, :], [[1, NR]], base=0, channel_multiplier=0, allow_small_or_imprecise_dtypes=True))
            pool.memset(FILL, 0.0).then_inc(cst["fill"], 1)
            pool.wait_ge(cst["fill"], 1)
            pool.iota(FILL.bitcast(I32).rearrange("p (i c) -> p i c", c=ROW)[:, :, P:ROW].rearrange("p i o -> p (i o)"),
                      [[P, NR]], base=T, channel_multiplier=1).then_inc(cst["fill"], 1)
            pool.iota(HAT[:, :].bitcast(I32).rearrange("p (t c) -> p t c", c=ROW)[:, :, P:ROW]
                      .rearrange("p t o -> p (t o)"), [[P, NT]], base=0, channel_multiplier=1).then_inc(cst["fill"], 1)
            pool.wait_ge(cst["fill"], 3)
            done(pool.memset(KS[64:96, :], 1.0))
            pool.wait_ge(ld["ffn"], 128)
            for i, dst in enumerate((WQ, WK)):
                src = WN[:, i * P:(i + 1) * P].rearrange("p (j r d) -> p j r d", j=4, r=4)
                view = dst[:, :].rearrange("p (d r j) -> p d r j", r=4, j=4)
                for r in range(4):
                    done(pool.tensor_copy(view[:, :, r, :].rearrange("p d j -> p j d"), src[:, :, r, :]), 0)
            k = 1
            phase_end(pool, ph["pool"], k)
            for n, layer in enumerate(LAYERS):
                if layer is FFN:
                    ffn_pre_pool(pool, s_pre)
                core_pool(pool, s_core)
                k += 1
                phase_end(pool, ph["pool"], k)
                if layer is FFN:
                    ffn_post_pool(pool, s_post, routed[n // 2], routed_x[n // 2])
                k += 1
                phase_end(pool, ph["pool"], k)

        @block.scalar
        def _(act):
            attn_a_act(act)
            k = 1
            phase_end(act, ph["act"], k)
            for n, layer in enumerate(LAYERS):
                if layer is ATTN_B:
                    b_pre_act(act, s_pre)
                else:
                    ffn_pre_act(act, s_pre)
                core_act(act, s_core, layer is ATTN_B)
                k += 1
                phase_end(act, ph["act"], k)
                if layer is FFN:
                    ffn_post_act(act, s_post)
                k += 1
                phase_end(act, ph["act"], k)

        @block.vector
        def _(dve):
            dve.memset(EPS[:, 0:1], LN_EPS)
            dve.memset(EPS[:, 1:2], RMS_EPS)
            dve.memset(ONB[:, :], 1.0)
            dve_then(dve, dve.memset(VP[:, :], 0.0))
            for i in range(2):
                v = VP[:, :].rearrange("p (kj g i c) -> p kj g i c", g=2, i=2, c=32)
                dve.memset(v[:, :, :, i, 16 * i + DH:16 * i + DH + 1], 1.0)
            dve.drain().then_inc(cst["dve"], 1)
            attn_a_dve(dve)
            k = 1
            phase_end(dve, ph["dve"], k)
            for n, layer in enumerate(LAYERS):
                if layer is ATTN_B:
                    b_pre_dve(dve, s_pre, NT)
                else:
                    ffn_pre_dve(dve, s_pre, EARLY if n else NT - 1)
                core_dve(dve, s_core, X if layer is ATTN_B else U)
                k += 1
                phase_end(dve, ph["dve"], k)
                if layer is FFN:
                    ffn_post_dve(dve, s_post, routed[n // 2], n == 0, n == len(LAYERS) - 1)
                k += 1
                phase_end(dve, ph["dve"], k)

        @block.tensor
        def _(pe):
            pe.wait_ge(cst["pool"], 19)
            attn_a_pe(pe)
            k = 1
            phase_end(pe, ph["pe"], k)
            for n, layer in enumerate(LAYERS):
                if layer is ATTN_B:
                    b_pre_pe(pe, s_pre)
                else:
                    ffn_pre_pe(pe, s_pre)
                core_pe(pe, s_core, layer is ATTN_B, BDO if layer is ATTN_B else WO)
                k += 1
                phase_end(pe, ph["pe"], k)
                if layer is FFN:
                    ffn_post_pe(pe, s_post, n == 0)
                k += 1
                phase_end(pe, ph["pe"], k)


_A, _B, _FF = "L0_attn_a_", "L0_attn_b_", "L0_ffn_"
_NAMES = {n: _A + n for n in ("x", "Qw", "Kw", "Vw")}
_NAMES |= {n: _B + n for n in ("W_DQ", "W_UQ", "W_DKV", "W_UKV", "W_QR", "W_KR", "W_O", "q_norm_w", "k_norm_w")}
_NAMES |= {n: _FF + n for n in ("ln1_g", "ln1_b", "ln2_g", "ln2_b", "wq", "bq", "wk", "bk", "wv", "bv", "wo", "bo",
                                "gate_w", "gate_b", "w1", "b1", "w2", "b2")}


def kernel(**inputs):
    import numpy as np
    import concourse.bacc as bacc
    from concourse.bass_utils import run_bass_kernel_spmd

    nc = bacc.Bacc("TRN2", target_bir_lowering=False, num_devices=1)
    arrays, args = {}, {}
    for short, name in _NAMES.items():
        arr = np.ascontiguousarray(inputs[name])
        arrays[f"in_{short}"] = arr
        args[short] = nc.dram_tensor(f"in_{short}", arr.shape, mybir.dt.from_np(arr.dtype), kind="ExternalInput").ap()
    out = nc.dram_tensor("out_x", (B, S, P), F32, kind="ExternalOutput").ap()
    hybrid_block_kernel(nc, args, out)
    r = run_bass_kernel_spmd(nc, [arrays], core_ids=[0])
    return r.results[0]["out_x"]
```

```python
from contextlib import ExitStack

import concourse.bass as bass
from concourse import mybir

F32 = mybir.dt.float32
BF16 = mybir.dt.bfloat16
I32 = mybir.dt.int32
ALU = mybir.AluOpType
ACT = mybir.ActivationFunctionType
AX_X = mybir.AxisListType.X

P = 128
B, S = 8, 256
T = B * S
NT = T // P
CH = 512
NC = T // CH
H, DH = 16, 8
E, F = 8, 512
FC = F // P
NR = NT + E - 1
ROWS = 9 * DH
AUG = ROWS + 2
ROW = P + 1
WARM = 16
SLOTS = 3
SLOT = H * S
LN_EPS = 1e-5
RMS_EPS = 1.1920929e-07
NEG = -1e30
HEAD_SCALE = DH ** -0.5
PB = P * S
QPARTS = 5


def at_least(eng, sem, count):
    if isinstance(count, int) and count <= 0:
        return
    eng.wait_ge(sem, count)


def hybrid_block_kernel(nc, a, out):
    ctx = ExitStack()
    with ctx:
        ctx.enter_context(nc.allow_non_contiguous_dma("small weights are laid out on load"))

        def sb(name, shape, dt=F32):
            return ctx.enter_context(nc.sbuf_tensor(name, shape, dt))

        def sems(prefix, names):
            each = {n: ctx.enter_context(nc.semaphore(prefix + "_" + n)) for n in names.split()}
            return each

        q_parts = nc.dram_tensor("q_parts", (B, QPARTS, P * S), BF16, kind="Internal")
        k_parts = nc.dram_tensor("k_parts", (B, 3, P * S), BF16, kind="Internal")
        routed_x = [nc.dram_tensor(f"routed_x{i}", (NR * P, ROW), F32, kind="Internal") for i in range(2)]
        moe_out = nc.dram_tensor("moe_out", (T + NR * P, P), F32, kind="Internal")

        X = sb("X", [P, T])
        HAT = sb("HAT", [P, NT * ROW])
        U = sb("U", [P, T])
        V = sb("V", [P, T])
        XT = sb("XT", [P, T])
        QP = sb("QP", [P, 3 * T], BF16)
        KP = sb("KP", [P, 3 * T], BF16)
        QS = sb("QS", [P, SLOTS * SLOT], BF16)
        KS = sb("KS", [P, SLOTS * SLOT], BF16)
        VP = sb("VP", [P, 2 * H * 32])
        PR = sb("PR", [P, 8 * CH])
        OT = sb("OT", [P, S])
        RC = sb("RC", [P, S])
        RES, RES2 = (sb(n, [P, 2 * CH]) for n in ("RES", "RES2"))
        MN = sb("MN", [P, 2 * 2 * 8])
        MHI = sb("MHI", [8, 2 * S], BF16)
        MLO = sb("MLO", [8, 2 * S], BF16)
        W1 = sb("W1", [P, E * F])
        W2 = sb("W2", [P, E * F])
        B1C = sb("B1C", [P, E * FC])
        B2R = sb("B2R", [P, E * P])
        wa = {n: sb("a_" + n, [P, P]) for n in ("Qw", "Kw", "Vw")}
        WN = RES[:, 0:2 * P]
        WQ, WK, WV, WO = (sb(n, [P, P]) for n in ("WQ", "WK", "WV", "WO"))
        GW = sb("GW", [P, E])
        GBR = sb("GBR", [P, E])
        BVR = sb("BVR", [P, P])
        BOR = sb("BOR", [P, P])
        COLS = sb("COLS", [P, 8])
        BQ, BK, G1, BE1, G2, BE2, QNW, KNW = (COLS[:, i:i + 1] for i in range(8))
        EPS = sb("EPS", [P, 2])
        TABLE = sb("TABLE", [P, 1])
        BDQK = sb("BDQK", [P, 2 * P])
        BDQ, BDK = BDQK[:, 0:P], BDQK[:, P:2 * P]
        BDG, BDV, BDO = (sb(n, [P, P]) for n in ("BDG", "BDV", "BDO"))
        SMALL = sb("SMALL", [P, 64])
        IDF = sb("IDF", [P, P])
        IDB = sb("IDB", [P, P], BF16)
        MSK = sb("MSK", [P, 2 * P], BF16)
        MSKT = sb("MSKT", [P, P], BF16)
        TRI = sb("TRI", [P, P], BF16)
        ONB = sb("ONB", [P, P], BF16)
        SELN = [sb(f"SELN{g}", [P, P]) for g in range(2)]
        SELD = [sb(f"SELD{g}", [P, P]) for g in range(2)]
        BLK = sb("BLK", [P, P])
        BLKP = sb("BLKP", [P, P])
        REV = sb("REV", [P, E])
        J128 = sb("J128", [P, NT])
        I24 = sb("I24", [P, NR])
        ST = sb("ST", [P, NT * 6])
        tok = {n: sb("t_" + n, [P, NT]) for n in ("a", "b", "mean", "var", "std", "rstd", "c", "rt", "nm", "rs")}
        R = {n: RES[:, i * P:(i + 1) * P] for i, n in enumerate(("lg", "eq", "hot", "cnt", "s0", "s1", "slot"))}
        HOTB = sb("HOTB", [P, NT * E], BF16)
        RT_ = {n: sb("r_" + n, [P, E]) for n in ("n", "m0", "m1", "base")}
        TOP = sb("TOP", [P, NT])
        SLF = sb("SLF", [P, NT])
        SLOTI = sb("SLOTI", [P, NT], I32)
        CMP = RC[:, 0:NR * E]
        EXF = sb("EXF", [P, NR])
        EXI = sb("EXI", [P, NR], I32)
        IDS = sb("IDS", [P, NR], I32)

        bank = [ctx.enter_context(nc.psum_tensor(f"bank{i}", [P, CH], F32)) for i in range(8)]

        QT = QS[:, 0:2 * T].bitcast(F32)
        KT = QS[:, 2 * T:4 * T].bitcast(F32)
        PA = PR[:, 0:2 * S]
        PT = PR[:, 2 * S:4 * S]
        SQ, TOK = ([PR[:, o + i * CH:o + (i + 1) * CH] for i in range(n)] for o, n in ((0, 2), (2 * CH, 3)))
        MS, SD, INV = ([PR[:, 7 * CH + o + i * 64:7 * CH + o + (i + 1) * 64] for i in range(2)] for o in (0, P, 2 * P))
        KW, KK = PR[:, 5 * CH:6 * CH], PR[:, 6 * CH:7 * CH]
        TWS = V
        XS = [PR[:, i * ROW:(i + 1) * ROW] for i in range(4)]
        XST, YS, W1S, MIDT = ([PR[:, 4 * ROW + o + i * w:4 * ROW + o + (i + 1) * w] for i in range(n)]
                              for o, w, n in ((0, P, 2), (2 * P, P, 4), (6 * P, F, 2), (14 * P, F, 2)))
        FILL = QP[:, 0:2 * NR * ROW].bitcast(F32)
        GATH = XT
        RAW = [RES[:, g * S:(g + 1) * S] for g in range(2)]

        ld = sems("ld", "x wa ffn small moe zero")
        cst = sems("cst", "pool dve fill")
        ph = sems("phase", "pe act dve pool sp")
        step = sems("step", "dve act")
        norm_names = "var std hat xt_ps xt "
        parts_names = " qa ka r2 q_done parts0 parts1 parts2 parts3"
        pa = sems("a", norm_names + "q_ps k_ps v_ps q_ev k_ev v_ev scored maxed exped pt_ps pt o_ps done")
        core_names = ("qk_in0 qk_in1 qk_ready scored maxed m_t m_hi m_lo shift0 shift1 st exped pv v_padded raw0 raw1 selected "
                      "inverted normed projected added")
        ffn_names = ("v_var v_std v_hat v_xt_ps v_xt logits hot prefix slots experts "
                     "xs0 xs1 xs2 xs3 x_t x_tb w1 up mid ids relu down y xu back0 back1 back2 back3 done")
        s_pre = sems("p", norm_names + "var2 std2 q_ps k_ps v_ps v_ev u0 qk_ps sq ms sd scaled turned g_ps kw kk" + parts_names)
        s_core = sems("c", core_names)
        s_post = sems("e", ffn_names)
        routed = [sems(f"rows{i}", "scattered out0 out1 out2 out3") for i in range(2)]
        prep = sems("prep", "repeated product blocks")
        post_ln = dict(var=s_post["v_var"], std=s_post["v_std"], hat=s_post["v_hat"], xt_ps=s_post["v_xt_ps"],
                       xt=s_post["v_xt"])
        FFN, ATTN_B = "ffn", "attention b"
        LAYERS = (FFN, ATTN_B, FFN)
        EARLY = 12
        s_out = ctx.enter_context(nc.semaphore("s_out"))

        counts = {"dve": 0, "act": 0}

        def dve_then(dve, ins):
            counts["dve"] += 1
            ins.then_inc(step["dve"], 1)
            dve.wait_ge(step["dve"], counts["dve"])

        def phase_end(eng, own, k):
            eng.drain().then_inc(own, 1)
            for other in (ph["pe"], ph["act"], ph["dve"], ph["pool"], ph["sp"]):
                if other is not own:
                    eng.wait_ge(other, k)

        def clear(eng, phase):
            for sem in phase.values():
                eng.sem_clear(sem)

        def tile_(buf, t, n=1):
            return buf[:, t * P:(t + n) * P]

        def hat_(t):
            return HAT[:, t * ROW:t * ROW + P]

        def stats(dve, src, t):
            return dve.bn_stats(ST[:, 6 * t:6 * t + 6], tile_(src, t))

        def part(buf, c, i):
            return buf[:, 6 * c * S:6 * (c + 1) * S].rearrange("p (b i s) -> p b i s", i=3, s=S)[:, :, i, :]

        def halves(x):
            return x.rearrange("p (b s) -> p b s", s=S)

        def ln_variance(dve, s, src, first, lo, hi):
            for t in range(first, hi):
                last = stats(dve, src, t)
            if first < hi:
                dve_then(dve, last)
            st = ST[:, 6 * lo:6 * hi].rearrange("p (t k) -> p t k", k=6)
            me, ve, mo, vo = (st[:, :, i] for i in (1, 2, 4, 5))
            ta, tb, mean, var = (tok[n][:, lo:hi] for n in ("a", "b", "mean", "var"))
            dve.tensor_tensor(ta, me, mo, ALU.subtract)
            dve.tensor_tensor(tb, ve, vo, ALU.add)
            dve_then(dve, dve.tensor_tensor(mean, me, mo, ALU.add))
            dve.tensor_scalar(mean, mean, 0.5, None, ALU.mult)
            dve_then(dve, dve.tensor_tensor(ta, ta, ta, ALU.mult))
            dve_then(dve, dve.scalar_tensor_tensor(out=var, in0=ta, scalar=float(P // 4), in1=tb,
                                                   op0=ALU.mult, op1=ALU.add))
            dve.tensor_scalar(var, var, 1.0 / P, None, ALU.mult).then_inc(s["var"], 1)

        def ln_scale(dve, s, twice, lo, hi, k):
            ta, tb, var, rstd = (tok[n][:, lo:hi] for n in ("a", "b", "var", "rstd"))
            dve.wait_ge(s["std"], k)
            dve_then(dve, dve.reciprocal(rstd, tok["std"][:, lo:hi]))
            if twice:
                dve_then(dve, dve.tensor_tensor(ta, var, rstd, ALU.mult))
                dve.tensor_tensor(ta, ta, rstd, ALU.mult).then_inc(s["var2"], 1)
                dve.wait_ge(s["std2"], 1)
                dve_then(dve, dve.reciprocal(tb, tok["c"][:, lo:hi]))
                dve_then(dve, dve.tensor_tensor(tok["rt"][:, lo:hi], tb, rstd, ALU.mult))

        def ln_hat(dve, s, src, twice, lo, hi):
            mean, scale = tok["mean"], tok["rt" if twice else "rstd"]
            for t in range(lo, hi):
                dve.tensor_scalar(hat_(t), tile_(src, t), mean[:, t:t + 1], scale[:, t:t + 1],
                                  ALU.subtract, ALU.mult).then_inc(s["hat"], 1)

        def ln_dve(dve, s, src, twice, first=0):
            ln_variance(dve, s, src, first, 0, NT)
            ln_scale(dve, s, twice, 0, NT, 1)
            ln_hat(dve, s, src, twice, 0, NT)

        def deviation(act, s, lo, hi, k):
            act.wait_ge(s["var"], k)
            act.activation(tok["std"][:, lo:hi], tok["var"][:, lo:hi], ACT.Sqrt, bias=EPS[:, 0:1]).then_inc(s["std"], 1)

        def ln_act(act, s, twice):
            act.activation(TABLE[:, :], EPS[:, 0:1], ACT.Sqrt)
            deviation(act, s, 0, NT, 1)
            if twice:
                act.wait_ge(s["var2"], 1)
                act.activation(tok["c"][:, :], tok["a"][:, :], ACT.Sqrt, bias=EPS[:, 0:1]).then_inc(s["std2"], 1)

        def warm(pe, n, bk=7):
            for _ in range(n):
                pe.matmul(bank[bk][:, 0:S], IDB[:, :], MSK[:, :], start=True, stop=True)

        def transpose_chunk(pe, s, c):
            pe.wait_ge(s["hat"], 4 * c + 4)
            for i in range(4):
                last = pe.transpose(bank[c][:, i * P:(i + 1) * P], hat_(4 * c + i), IDF[:, :])
            last.then_inc(s["xt_ps"], 1)

        def transpose_pe(pe, s):
            warm(pe, WARM)
            for c in range(NC):
                transpose_chunk(pe, s, c)

        def transpose_act(act, s, gain=None, bias=None, chunks=range(NC)):
            for c in chunks:
                act.wait_ge(s["xt_ps"], c + 1)
                dst = XT[:, c * CH:(c + 1) * CH]
                if gain is None:
                    act.activation(dst, bank[c][:, :], ACT.Copy).then_inc(s["xt"], 1)
                else:
                    act.activation(dst, bank[c][:, :], ACT.Identity, scale=gain, bias=bias).then_inc(s["xt"], 1)

        def attn_a_pe(pe):
            s = pa
            transpose_pe(pe, s)
            for c in range(NC):
                pe.wait_ge(s["xt"], c + 1)
                xc = XT[:, c * CH:(c + 1) * CH]
                if c == 0:
                    pe.wait_ge(ld["wa"], 48)
                if c >= 2:
                    pe.wait_ge(s["q_ev"], c - 1)
                    pe.wait_ge(s["k_ev"], c - 1)
                pe.matmul(bank[4 + c % 2][:, :], wa["Qw"][:, :], xc, start=True, stop=True).then_inc(s["q_ps"], 1)
                pe.matmul(bank[6 + c % 2][:, :], wa["Kw"][:, :], xc, start=True, stop=True).then_inc(s["k_ps"], 1)
                for i in range(4):
                    last = pe.matmul(bank[c][:, i * P:(i + 1) * P], tile_(XT, 4 * c + i), wa["Vw"][:, :],
                                     start=True, stop=True)
                last.then_inc(s["v_ps"], 1)
            pe.wait_ge(s["q_ev"], NC)
            pe.wait_ge(s["k_ev"], NC)
            pe.wait_ge(s["v_ev"], NC)
            for step_ in range(NT + 2):
                t = step_
                if t < NT:
                    b, w = t // 2, (t % 2 + 1) * P
                    at_least(pe, s["exped"], t - 1)
                    pe.matmul(bank[t % 2][:, 0:w], tile_(QT, t), KT[:, b * S:b * S + w], start=True, stop=False)
                    pe.matmul(bank[t % 2][:, w - P:w], IDB[:, :], MSK[:, 0:P], start=False, stop=True)\
                        .then_inc(s["scored"], 1)
                t = step_ - 1
                if 0 <= t < NT:
                    pe.wait_ge(s["exped"], t + 1)
                    at_least(pe, s["pt"], t - 1)
                    for k in range(t % 2 + 1):
                        last = pe.transpose(bank[2 + t % 2][:, k * P:(k + 1) * P],
                                            PA[:, (t % 2) * S + k * P:(t % 2) * S + (k + 1) * P], IDF[:, :])
                    last.then_inc(s["pt_ps"], 1)
                t = step_ - 2
                if 0 <= t < NT:
                    pe.wait_ge(s["pt"], t + 1)
                    at_least(pe, s["done"], t - 1)
                    n = t % 2 + 1
                    for k in range(n):
                        last = pe.matmul(bank[4 + t % 2][:, 0:P], PT[:, (t % 2) * S + k * P:(t % 2) * S + (k + 1) * P],
                                         tile_(V, 2 * (t // 2) + k), start=(k == 0), stop=(k == n - 1))
                    last.then_inc(s["o_ps"], 1)

        def attn_a_act(act):
            s = pa
            act.wait_ge(cst["dve"], 1)
            ln_act(act, s, False)
            transpose_act(act, s)
            for c in range(NC):
                act.wait_ge(s["q_ps"], c + 1)
                act.activation(QT[:, c * CH:(c + 1) * CH], bank[4 + c % 2][:, :], ACT.Copy).then_inc(s["q_ev"], 1)
                act.wait_ge(s["v_ps"], c + 1)
                act.activation(V[:, c * CH:(c + 1) * CH], bank[c][:, :], ACT.Copy).then_inc(s["v_ev"], 1)
            act.activation(TABLE[:, :], EPS[:, 0:1], ACT.Exp)
            for t in range(NT + 1):
                w = (t % 2 + 1) * P
                if t < NT:
                    act.wait_ge(s["maxed"], t + 1)
                    at_least(act, s["pt_ps"], t - 1)
                    act.activation(PA[:, (t % 2) * S:(t % 2) * S + w], bank[t % 2][:, 0:w], ACT.Exp,
                                   bias=tok["nm"][:, t:t + 1], scale=float(P) ** -0.5,
                                   accum_out=tok["rs"][:, t:t + 1]).then_inc(s["exped"], 1)
                t, w = t - 1, ((t - 1) % 2 + 1) * P
                if t >= 0:
                    act.wait_ge(s["pt_ps"], t + 1)
                    at_least(act, s["o_ps"], t - 1)
                    act.activation(PT[:, (t % 2) * S:(t % 2) * S + w], bank[2 + t % 2][:, 0:w], ACT.Copy)\
                        .then_inc(s["pt"], 1)

        def attn_a_dve(dve):
            s = pa
            dve.wait_ge(ld["x"], 16)
            ln_dve(dve, s, X, False)
            for c in range(NC):
                dve.wait_ge(s["k_ps"], c + 1)
                dve.tensor_copy(KT[:, c * CH:(c + 1) * CH], bank[6 + c % 2][:, :]).then_inc(s["k_ev"], 1)
            for step_ in range(NT + 2):
                t = step_
                if t < NT:
                    w = (t % 2 + 1) * P
                    dve.wait_ge(s["scored"], t + 1)
                    dve_then(dve, dve.tensor_reduce(out=tok["a"][:, t:t + 1], in_=bank[t % 2][:, 0:w], axis=AX_X,
                                                    op=ALU.max))
                    dve.tensor_scalar(tok["nm"][:, t:t + 1], tok["a"][:, t:t + 1], -(float(P) ** -0.5), None,
                                      ALU.mult).then_inc(s["maxed"], 1)
                t = step_ - 2
                if 0 <= t < NT:
                    dve_then(dve, dve.reciprocal(tok["b"][:, t:t + 1], tok["rs"][:, t:t + 1]))
                    dve.wait_ge(s["o_ps"], t + 1)
                    dve.scalar_tensor_tensor(out=tile_(X, t), in0=bank[4 + t % 2][:, 0:P], scalar=tok["b"][:, t:t + 1],
                                             in1=tile_(X, t), op0=ALU.mult, op1=ALU.add).then_inc(s["done"], 1)
                    if t:
                        dve.wait_ge(s["done"], t)
                        stats(dve, X, t - 1)

        def slot_of(b):
            return (b % SLOTS) * SLOT

        def core_pe(pe, s, causal, wout):
            def scores(b, n):
                if n == 0 and isinstance(b, int):
                    pe.wait_ge((s["qk_in0"], s["qk_in1"])[b], 96)
                elif n == 0:
                    pe.wait_ge(s["qk_ready"], b + 1)
                at_least(pe, s["maxed"], 16 * b + n - 1)
                dst = bank[n % 2]
                for qt in range(2):
                    w = P if causal and qt == 0 else S
                    d = dst[:, qt * S:qt * S + w]
                    last = pe.matmul(d, QS[0:ROWS, bass.ds(slot_of(b) + n * S + qt * P, P)],
                                     KS[0:ROWS, bass.ds(slot_of(b) + n * S, w)], start=True, stop=not causal)
                    if causal:
                        last = pe.matmul(d[:, w - P:w], IDB[:, :], MSK[:, 0:P], start=False, stop=True)
                last.then_inc(s["scored"], 1)

            def shifted(b, n):
                if n == 0:
                    pe.wait_ge(s["shift0"], 32 * (b + 1))
                if n == 8:
                    pe.wait_ge(s["shift1"], 32 * (b + 1))
                at_least(pe, s["exped"], 16 * b + n - 1)
                dst = bank[2 + n % 2]
                for kt in range(2):
                    lo = P if causal and kt else 0
                    d = dst[:, kt * S:kt * S + S - lo]
                    last = pe.matmul(d, KS[0:AUG, bass.ds(slot_of(b) + n * S + kt * P, P)],
                                     QS[0:AUG, bass.ds(slot_of(b) + n * S + lo, S - lo)],
                                     start=True, stop=not causal)
                    if causal:
                        last = pe.matmul(d[:, 0:P], IDB[:, :], MSKT[:, :], start=False, stop=True)
                last.then_inc(s["st"], 1)

            def maxima(b, u):
                pe.wait_ge(s["maxed"], 16 * b + 8 * u + 8)
                at_least(pe, s["m_lo"], 2 * b + u)
                for qt in range(2):
                    last = pe.transpose(bank[5][0:8, u * S + qt * P:u * S + (qt + 1) * P],
                                        MN[:, u * 16 + qt * 8:u * 16 + qt * 8 + 8], IDF[:, :])
                last.then_inc(s["m_t"], 1)

            def values(b, q, kt):
                if kt == 0:
                    pe.wait_ge(s["exped"], 16 * b + 4 * q + 4)
                    pe.wait_ge(s["v_padded"], 4 * b + q + 1)
                if kt == 0 and q == 0:
                    at_least(pe, s["raw0"], b)
                if kt == 0 and q == 2:
                    at_least(pe, s["raw1"], b)
                lo = P if causal and kt else 0
                for j in range(4):
                    h, n = 4 * j + q, 4 * q + j
                    last = pe.matmul(bank[4 if q < 2 else 7][32 * j:32 * j + 32, lo:S],
                                     VP[:, (kt * H + h) * 32:(kt * H + h + 1) * 32],
                                     PR[:, (n % 8) * CH + kt * S:(n % 8) * CH + kt * S + S - lo],
                                     start=(q % 2 == 0 and kt == 0), stop=(q % 2 == 1 and kt == 1))
                if kt == 1:
                    last.then_inc(s["pv"], 1)

            def select(b, k):
                g = k % 2
                if k == 0:
                    pe.wait_ge(s["raw0"], b + 1)
                    at_least(pe, s["added"], b)
                if k == 1:
                    pe.wait_ge(s["raw1"], b + 1)
                o = (1 - k // 2) * S
                last = pe.matmul(bank[6][:, o:o + S], (SELD, SELN)[k // 2][g][:, :], RAW[g],
                                 start=(g == 0), stop=(g == 1))
                if k == 3:
                    last.then_inc(s["selected"], 1)

            def project(b):
                pe.wait_ge(s["normed"], b + 1)
                for i in range(2):
                    last = pe.matmul(bank[6][:, i * P:(i + 1) * P], OT[:, i * P:(i + 1) * P], wout[:, :],
                                     start=True, stop=True)
                last.then_inc(s["projected"], 1)

            def batch(b, now, before, last_):
                for n in range(H):
                    if now:
                        scores(b, n)
                    if before:
                        shifted(b - 1, n)
                    q, odd = n // 4, n % 2
                    if odd and q == 0 and last_:
                        values(b - 2, 3, n // 2)
                    if odd and q > 0 and before:
                        values(b - 1, q - 1, n // 2 % 2)
                    if n == 1 and before:
                        maxima(b - 1, 1)
                    if n == 9 and now:
                        maxima(b, 0)
                    if n in (5, 6, 7, 8) and last_:
                        select(b - 2, n - 5)
                    if n == 12 and last_ and not before and not causal:
                        transpose_chunk(pe, post_ln, 0)
                        warm(pe, WARM // 2, 1)
                    if n == 14 and last_:
                        project(b - 2)

            pe.wait_ge(s_pre["v_ev"], NC)
            pe.wait_ge(s_pre["r2"], 2 * NC)
            warm(pe, WARM, 0)
            if causal:
                for i in range(2):
                    pe.matmul(bank[i][:, P:S], IDB[:, :], MSK[:, P:2 * P], start=True, stop=True)
            pe.wait_ge(s_pre["q_done"], 2 * NC)
            batch(0, True, False, False)
            batch(1, True, True, False)
            with pe.Fori(2, B) as b:
                batch(b, True, True, True)
            batch(B, False, True, True)
            batch(B + 1, False, False, True)

        def core_act(act, s, causal):
            def exps(b, n):
                act.wait_ge(s["st"], 16 * b + n + 1)
                if n % 4 == 0:
                    at_least(act, s["pv"], 4 * b + n // 4 - 1)
                w = CH - P if causal else CH
                act.activation(PR[:, (n % 8) * CH:(n % 8) * CH + w], bank[2 + n % 2][:, 0:w], ACT.Exp,
                               scale=HEAD_SCALE).then_inc(s["exped"], 1)

            def high(b, u):
                act.wait_ge(s["m_t"], 2 * b + u + 1)
                at_least(act, s["shift1"] if u else s["shift0"], 32 * b)
                act.activation(MHI[:, u * S:(u + 1) * S], bank[5][0:8, u * S:(u + 1) * S], ACT.Copy)\
                    .then_inc(s["m_hi"], 1)

            def raw(b, g):
                act.wait_ge(s["pv"], 4 * b + 2 * g + 2)
                at_least(act, s["selected"], b)
                act.activation(RAW[g], bank[7 if g else 4][:, 0:S], ACT.Copy).then_inc(s["raw1" if g else "raw0"], 1)

            def batch(b, now, before, last_):
                for n in range(H):
                    if before:
                        exps(b - 1, n)
                    if n == 2 and before:
                        high(b - 1, 1)
                    if n == 4 and last_:
                        raw(b - 2, 1)
                    if n == 10 and now:
                        high(b, 0)
                    if n == 13 and before:
                        raw(b - 1, 0)

            act.activation(TABLE[:, :], EPS[:, 0:1], ACT.Exp)
            batch(0, True, False, False)
            batch(1, True, True, False)
            with act.Fori(2, B) as b:
                batch(b, True, True, True)
            batch(B, False, True, True)
            if not causal:
                deviation(act, post_ln, 0, EARLY, 1)
            batch(B + 1, False, False, True)

        def core_dve(dve, s, acc):
            def maximum(b, n):
                dve.wait_ge(s["scored"], 16 * b + n + 1)
                if n % 8 == 0:
                    at_least(dve, s["m_t"], 2 * b - 1 + n // 8)
                u = n // 8
                o = MN[:, u * 16:(u + 1) * 16].rearrange("p (t n) -> p t n", n=8)[:, :, n % 8]
                dve.tensor_reduce(out=o, in_=bank[n % 2][:, :].rearrange("p (t k) -> p t k", k=S), axis=AX_X,
                                  op=ALU.max, negate=True).then_inc(s["maxed"], 1)

            def low(b, u):
                dve.wait_ge(s["m_hi"], 2 * b + u + 1)
                at_least(dve, s["shift1"] if u else s["shift0"], 32 * b)
                dve.tensor_tensor(MLO[:, u * S:(u + 1) * S], bank[5][0:8, u * S:(u + 1) * S],
                                  MHI[:, u * S:(u + 1) * S], ALU.subtract).then_inc(s["m_lo"], 1)

            def invert(b, i):
                dve.wait_ge(s["selected"], b + 1)
                dve.reciprocal(RC[:, i * P:(i + 1) * P], bank[6][:, S + i * P:S + (i + 1) * P]).then_inc(s["inverted"], 1)

            def divide(b):
                dve.wait_ge(s["inverted"], 2 * b + 2)
                at_least(dve, s["projected"], b)
                dve.tensor_tensor(OT[:, :], bank[6][:, 0:S], RC[:, :], ALU.mult).then_inc(s["normed"], 1)

            def add(b):
                dve.wait_ge(s["projected"], b + 1)
                d = acc[:, bass.ds(b * S, S)]
                dve.tensor_tensor(d, d, bank[6][:, 0:S], ALU.add).then_inc(s["added"], 1)

            def batch(b, now, before, last_):
                for n in range(H):
                    if now:
                        maximum(b, n)
                    if n == 3 and before:
                        low(b - 1, 1)
                    if n == 4 and not now and before:
                        dve.wait_ge(s["added"], EARLY // 2)
                        if acc is U:
                            ln_variance(dve, post_ln, U, 0, 0, EARLY)
                        else:
                            for t in range(EARLY):
                                stats(dve, X, t)
                    if n in (0, 13) and acc is U and last_ and not before:
                        if n == 0:
                            ln_scale(dve, post_ln, False, 0, EARLY, 1)
                        lo, hi = ((0, 4), (4, EARLY))[n // 13]
                        ln_hat(dve, post_ln, U, False, lo, hi)
                    if n in (8, 10) and last_:
                        invert(b - 2, (8, 10).index(n))
                    if n == 11 and now:
                        low(b, 0)
                    if n == 12 and last_:
                        divide(b - 2)
                    if n == 15 and last_:
                        add(b - 2)

            batch(0, True, False, False)
            batch(1, True, True, False)
            if acc is U:
                dve.wait_ge(s_pre["u0"], NT + 1)
            with dve.Fori(2, B) as b:
                batch(b, True, True, True)
            batch(B, False, True, True)
            batch(B + 1, False, False, True)

        def core_pool(pool, s, inner):
            def pad(b):
                src = V[:, bass.ds(b * S, S)].rearrange("p (k j r d) -> p k j r d", k=2, j=4, r=4)
                dst = VP[:, :].rearrange("p (k j r c) -> p k j r c", k=2, j=4, r=4)
                for r in range(4):
                    at_least(pool, s["pv"], 4 * b - 3 + r)
                    o = 16 * (r % 2)
                    pool.tensor_copy(dst[:, :, :, r, o:o + DH], src[:, :, :, r, :]).then_inc(s["v_padded"], 1)

            pool.wait_ge(s_pre["v_ev"], NC)
            pad(0)
            if inner:
                inner_residual(pool, s_pre)
            with pool.Fori(1, B) as b:
                pad(b)

        def core_sp(sp, s, parts):
            def store_parts(c):
                sp.wait_ge(s_pre["q_done"], 2 * (c + 1))
                sp.dma_start(bass.AP(k_parts, 6 * c * PB, [[S, P], [PB, 6], [1, S]]),
                             KP[:, 6 * c * S:6 * (c + 1) * S].rearrange("p (x s) -> p x s", s=S)).then_inc(parts[c], 16)
                for b in (2 * c, 2 * c + 1):
                    for first, n in ((0, 3), (3, 2)):
                        sp.dma_start(bass.AP(q_parts, (QPARTS * b + first) * PB, [[S, P], [PB, n], [1, S]]),
                                     QP[:, 3 * b * S:(3 * b + n) * S].rearrange("p (i s) -> p i s", s=S))\
                            .then_inc(parts[c], 16)

            def load(b):
                sp.wait_ge(parts[b // 2], 80)
                at_least(sp, s["st"], 16 * (b - SLOTS + 1))
                sem, o = (s["qk_in0"], s["qk_in1"])[b % 2], slot_of(b)
                for i in range(3):
                    rows = slice(3 * DH * i, 3 * DH * (i + 1))
                    sp.dma_start(QS[rows, o:o + SLOT],
                                 bass.AP(q_parts, (QPARTS * b + i) * PB, [[SLOT, 3 * DH], [1, SLOT]])).then_inc(sem, 16)
                    sp.dma_start(KS[rows, o:o + SLOT],
                                 bass.AP(k_parts, 3 * b * PB, [[SLOT, 3 * DH], [1, SLOT]])).then_inc(sem, 16)

            def ready(b):
                sp.wait_ge((s["qk_in0"], s["qk_in1"])[b % 2], 96 * (b // 2 + 1))
                sp.sem_inc(s["qk_ready"], 1)

            def shift(b, u):
                sp.wait_ge(s["m_lo"], 2 * b + u + 1)
                o = slot_of(b) + u * 8 * S
                for row, m in ((ROWS, MHI), (ROWS + 1, MLO)):
                    sp.dma_start(QS[row:row + 1, o:o + 8 * S].rearrange("o (n t) -> o n t", t=S),
                                 m[:, u * S:(u + 1) * S]).then_inc(s["shift1"] if u else s["shift0"], 16)

            for c in range(NC):
                store_parts(c)
                if c == 0:
                    load(0)
                if c == 2:
                    load(1)
            ready(0)
            for b in range(B + 1):
                if 1 <= b < B - 1:
                    load(b + 1)
                if b >= 1:
                    shift(b - 1, 1)
                if b < B:
                    shift(b, 0)
                if b + 1 < B:
                    ready(b + 1)

        def rest(c, i):
            return halves((RES, RES2)[c % 2][:, i * CH:(i + 1) * CH])

        def second_part(act, s, c, i):
            act.wait_ge(s["r2"], 2 * c + i + 1)
            act.activation(part((QP, KP)[i], c, 1), rest(c, i), ACT.Copy).then_inc(s["ka"], 1)

        def third_parts(pool, s):
            for c in range(NC):
                for i, buf in enumerate((QP, KP)):
                    pool.wait_ge(s["ka"], 2 * c + i + 1)
                    pool.tensor_tensor(part(buf, c, 2), rest(c, i), part(buf, c, 1),
                                       ALU.subtract).then_inc(s["q_done"], 1)

        def ffn_pre_pe(pe, s):
            warm(pe, WARM)
            transpose_chunk(pe, s, 0)
            for c in range(NC):
                if c + 1 < NC:
                    transpose_chunk(pe, s, c + 1)
                pe.wait_ge(s["xt"], c + 1)
                xc = XT[:, c * CH:(c + 1) * CH]
                at_least(pe, s["r2"], 2 * (c - 1))
                pe.matmul(bank[4 + c % 2][:, :], WQ[:, :], xc, start=True, stop=True).then_inc(s["q_ps"], 1)
                pe.matmul(bank[6 + c % 2][:, :], WK[:, :], xc, start=True, stop=True).then_inc(s["k_ps"], 1)
                for i in range(4):
                    last = pe.matmul(bank[c][:, i * P:(i + 1) * P], tile_(XT, 4 * c + i), WV[:, :],
                                     start=True, stop=True)
                last.then_inc(s["v_ps"], 1)

        def ffn_pre_act(act, s):
            ln_act(act, s, True)
            for step_ in range(NC + 2):
                if step_ < NC:
                    transpose_act(act, s, G1, BE1, (step_,))
                c = step_ - 1
                if 0 <= c < NC:
                    for sem, bk, bias, buf in ((s["q_ps"], 4, BQ, QP), (s["k_ps"], 6, BK, KP)):
                        act.wait_ge(sem, c + 1)
                        act.activation(part(buf, c, 0), halves(bank[bk + c % 2][:, :]), ACT.Identity, bias=bias)\
                            .then_inc(s["qa"], 1)
                c = step_ - 2
                if c >= 0:
                    for i in range(2):
                        second_part(act, s, c, i)

        def ffn_pre_dve(dve, s, first):
            ln_dve(dve, s, X, True, first)
            for c in range(NC):
                for i, (bk, bias, buf) in enumerate(((4, BQ, QP), (6, BK, KP))):
                    dve.wait_ge(s["qa"], 2 * c + i + 1)
                    at_least(dve, s["q_done"], 2 * (c - 2) + i + 1)
                    dve.scalar_tensor_tensor(out=rest(c, i), in0=halves(bank[bk + c % 2][:, :]),
                                             scalar=bias, in1=part(buf, c, 0), op0=ALU.add, op1=ALU.subtract)\
                        .then_inc(s["r2"], 1)
                dve.wait_ge(s["v_ps"], c + 1)
                dve.tensor_tensor(V[:, c * CH:(c + 1) * CH].rearrange("p (t n) -> p t n", n=P),
                                  bank[c][:, :].rearrange("p (t n) -> p t n", n=P),
                                  BVR[:, :].rearrange("p (o n) -> p o n", o=1).to_broadcast([P, 4, P]), ALU.add)\
                    .then_inc(s["v_ev"], 1)

        def inner_residual(pool, s):
            for t in range(NT):
                pool.wait_ge(s["hat"], t + 1)
                pool.tensor_scalar(tile_(U, t), hat_(t), tok["c"][:, t:t + 1], None, ALU.mult)\
                    .then_inc(s["u0"], 1)
            pool.wait_ge(s["u0"], NT)
            u = U[:, :].rearrange("p (t n) -> p t n", n=P)
            pool.tensor_tensor(u, u, BOR[:, :].rearrange("p (o n) -> p o n", o=1).to_broadcast([P, NT, P]), ALU.add)\
                .then_inc(s["u0"], 1)

        def expert_reg(eng, i):
            return eng.value_load(EXI[0:1, i:i + 1], min_val=0, max_val=E - 1)

        def ffn_post_pe(pe, s, rows, first_layer):

            def logits(t):
                pe.wait_ge(s["v_xt"], t // 4 + 1)
                return pe.matmul(bank[4][:, t * E:(t + 1) * E], tile_(XT, t), GW[:, :], start=True, stop=True)

            for c in range(1, EARLY // 4):
                transpose_chunk(pe, post_ln, c)
            warm(pe, WARM // 4)
            for t in range(EARLY - 4):
                logits(t)
            transpose_chunk(pe, post_ln, NC - 1)
            for t in range(EARLY - 4, NT):
                last = logits(t)
            last.then_inc(s["logits"], 1)
            pe.wait_ge(s["hot"], 1)
            pe.matmul(bank[5][:, 0:P], TRI[:, :], HOTB[:, :], start=True, stop=True)
            pe.matmul(bank[5][:, P:2 * P], ONB[:, :], HOTB[:, :], start=True, stop=True).then_inc(s["prefix"], 1)
            pe.wait_ge(s["experts"], 1)
            if first_layer:
                b_small_pe(pe)
                pe.wait_ge(prep["blocks"], 1)
            pe.wait_ge(rows["scattered"], 16 * NT)
            warm(pe, WARM // 2)
            xs = (s["xs0"], s["xs1"], s["xs2"], s["xs3"])
            for k in range(NR + 2):
                i = k
                if i < NR:
                    pe.wait_ge(xs[i % 4], 16 * (i // 4 + 1))
                    at_least(pe, s["x_tb"], i - 1)
                    pe.transpose(bank[i % 2][:, 0:P], XS[i % 4][:, 0:P], IDF[:, :]).then_inc(s["x_t"], 1)
                i = k - 1
                if 0 <= i < NR:
                    pe.wait_ge(s["x_tb"], i + 1)
                    pe.wait_ge(s["w1"], i + 1)
                    at_least(pe, s["mid"], i - 1)
                    for c in range(FC):
                        last = pe.matmul(bank[2 + i % 2][:, c * P:(c + 1) * P], W1S[i % 2][:, c * P:(c + 1) * P],
                                         XST[i % 2], start=True, stop=True)
                    last.then_inc(s["up"], 1)
                i = k - 2
                if 0 <= i < NR:
                    e = expert_reg(pe, i)
                    pe.wait_ge(s["relu"], i + 1)
                    at_least(pe, s["y"], i - 1)
                    for c in range(FC):
                        last = pe.matmul(bank[6 + i % 2][:, 0:P], MIDT[i % 2][:, c * P:(c + 1) * P],
                                         W2[:, bass.ds(e * F + c * P, P)], start=(c == 0), stop=(c == FC - 1))
                    last.then_inc(s["down"], 1)

        def ffn_post_act(act, s):
            transpose_act(act, post_ln, G2, BE2, range(2))
            deviation(act, post_ln, EARLY, NT, 2)
            transpose_act(act, post_ln, G2, BE2, range(2, NC))
            for k in range(NR + 1):
                i = k
                if i < NR:
                    act.wait_ge(s["x_t"], i + 1)
                    at_least(act, s["up"], i - 1)
                    act.activation(XST[i % 2], bank[i % 2][:, 0:P], ACT.Identity, scale=G2, bias=BE2).then_inc(s["x_tb"], 1)
                i = k - 1
                if i >= 0:
                    act.wait_ge(s["mid"], i + 1)
                    act.activation(MIDT[i % 2], MIDT[i % 2], ACT.Relu).then_inc(s["relu"], 1)

        def ffn_post_dve(dve, s, rows, first_layer, last_layer):
            ln_variance(dve, post_ln, U, EARLY, EARLY, NT)
            ln_scale(dve, post_ln, False, EARLY, NT, 2)
            ln_hat(dve, post_ln, U, False, EARLY, NT)
            dve.wait_ge(s["logits"], 1)

            def te(buf):
                return buf.rearrange("p (t e) -> p t e", e=E)

            def over_t(row):
                return row.rearrange("p (o e) -> p o e", o=1).to_broadcast([P, NT, E])

            def over_e(col):
                return col.rearrange("p (t o) -> p t o", o=1).to_broadcast([P, NT, E])

            lg, eq, hot, cnt, s0, s1, sl = (te(R[n]) for n in ("lg", "eq", "hot", "cnt", "s0", "s1", "slot"))
            dve_then(dve, dve.tensor_tensor(lg, te(bank[4][:, 0:P]), over_t(GBR[:, :]), ALU.add))
            dve_then(dve, dve.tensor_reduce(out=TOP[:, :], in_=lg, axis=AX_X, op=ALU.max))
            dve_then(dve, dve.tensor_tensor(eq, lg, over_e(TOP[:, :]), ALU.is_equal))
            dve_then(dve, dve.tensor_tensor(eq, eq, over_t(REV[:, :]), ALU.mult))
            dve_then(dve, dve.tensor_reduce(out=TOP[:, :], in_=eq, axis=AX_X, op=ALU.max))
            dve_then(dve, dve.tensor_tensor(hot, over_e(TOP[:, :]), over_t(REV[:, :]), ALU.is_equal))
            dve.tensor_copy(HOTB[:, :], R["hot"]).then_inc(s["hot"], 1)
            dve.wait_ge(s["prefix"], 1)
            dve_then(dve, dve.tensor_copy(cnt, te(bank[5][:, P:2 * P])))
            src, dst, other = cnt, s0, s1
            for d in (1, 2, 4, 8):
                dve.tensor_copy(dst[:, 0:d, :], src[:, 0:d, :])
                dve_then(dve, dve.tensor_tensor(dst[:, d:, :], src[:, d:, :], src[:, 0:NT - d, :], ALU.add))
                src, dst, other = dst, other, dst
            total = src[:, NT - 1, :]
            cmp_n = CMP[:, 0:E * NT].rearrange("p (e j) -> p e j", j=NT)
            dve_then(dve, dve.tensor_tensor(cmp_n, total.rearrange("p (e o) -> p e o", o=1).to_broadcast([P, E, NT]),
                                            J128[:, :].rearrange("p (o j) -> p o j", o=1).to_broadcast([P, E, NT]),
                                            ALU.is_gt))
            dve_then(dve, dve.tensor_reduce(out=RT_["n"][:, :], in_=cmp_n, axis=AX_X, op=ALU.add))
            a_, b_ = RT_["n"], RT_["m0"]
            for d in (1, 2, 4):
                dve.tensor_copy(b_[:, 0:d], a_[:, 0:d])
                dve_then(dve, dve.tensor_tensor(b_[:, d:E], a_[:, d:E], a_[:, 0:E - d], ALU.add))
                a_, b_ = b_, (RT_["m1"] if b_ is RT_["m0"] else RT_["m0"])
            ends = a_
            dve_then(dve, dve.tensor_tensor(RT_["base"][:, :], ends[:, :], RT_["n"][:, :], ALU.subtract))
            dve_then(dve, dve.tensor_scalar(RT_["base"][:, :], RT_["base"][:, :], float(P), None, ALU.mult))
            dve_then(dve, dve.tensor_tensor(sl, src, cnt, ALU.subtract))
            dve_then(dve, dve.tensor_tensor(sl, te(bank[5][:, 0:P]), sl, ALU.add))
            dve_then(dve, dve.tensor_tensor(sl, sl, over_t(RT_["base"][:, :]), ALU.add))
            dve_then(dve, dve.tensor_tensor(sl, sl, hot, ALU.mult))
            dve_then(dve, dve.tensor_reduce(out=SLF[:, :], in_=sl, axis=AX_X, op=ALU.add))
            dve.tensor_copy(SLOTI[:, :], SLF[:, :]).then_inc(s["slots"], 1)
            cmp_i = CMP[:, :].rearrange("p (i e) -> p i e", e=E)
            dve_then(dve, dve.tensor_tensor(cmp_i, ends[:, :].rearrange("p (o e) -> p o e", o=1).to_broadcast([P, NR, E]),
                                            I24[:, :].rearrange("p (i o) -> p i o", o=1).to_broadcast([P, NR, E]),
                                            ALU.is_le))
            dve_then(dve, dve.tensor_reduce(out=EXF[:, :], in_=cmp_i, axis=AX_X, op=ALU.add))
            dve_then(dve, dve.tensor_scalar(EXF[:, :], EXF[:, :], float(E - 1), None, ALU.min))
            dve.tensor_copy(EXI[:, :], EXF[:, :]).then_inc(s["experts"], 1)
            dve.wait_ge(s["experts"], 1)
            if first_layer:
                b_small_dve(dve)
            expert = [expert_reg(dve, i) for i in range(2)]

            def first_weights(i):
                at_least(dve, s["up"], i - 1)
                dve.tensor_copy(W1S[i % 2], W1[:, bass.ds(expert[i] * F, F)]).then_inc(s["w1"], 1)

            first_weights(0)
            first_weights(1)
            for k in range(1, NR + 2):
                i = k - 1
                if i < NR:
                    dve.wait_ge(s["up"], i + 1)
                    at_least(dve, s["down"], i - 1)
                    bias = B1C[:, bass.ds(expert[i] * FC, FC)].rearrange("p (c o) -> p c o", o=1)
                    dve.tensor_tensor(MIDT[i % 2].rearrange("p (c t) -> p c t", t=P),
                                      bank[2 + i % 2][:, :].rearrange("p (c t) -> p c t", t=P),
                                      bias.to_broadcast([P, FC, P]), ALU.add).then_inc(s["mid"], 1)
                    dve.tensor_copy(IDS[:, i:i + 1], XS[i % 4][:, P:ROW].bitcast(I32)).then_inc(s["ids"], 1)
                i = k + 1
                if i < NR:
                    expert.append(expert_reg(dve, i))
                    first_weights(i)
                i = k - 2
                if 0 <= i < NR:
                    dve.wait_ge(s["down"], i + 1)
                    at_least(dve, rows[f"out{i % 4}"], 16 * (i // 4))
                    dve.tensor_tensor(YS[i % 4], bank[6 + i % 2][:, 0:P], B2R[:, bass.ds(expert[i] * P, P)], ALU.add)\
                        .then_inc(s["y"], 1)
            for c in range(NC):
                c4 = slice(c * CH, (c + 1) * CH)
                dve.tensor_tensor(X[:, c4], X[:, c4], U[:, c4], ALU.add).then_inc(s["xu"], 1)
            dve.wait_ge(s["xu"], NC)
            for c in range(NC):
                c4 = slice(c * CH, (c + 1) * CH)
                dve.wait_ge(s[f"back{c}"], 16)
                dve.tensor_tensor(X[:, c4], X[:, c4], GATH[:, c4], ALU.add).then_inc(s["done"], 1)
                if not last_layer:
                    dve.wait_ge(s["done"], c + 1)
                    for t in range(4 * c, 4 * c + 4):
                        stats(dve, X, t)

        def rows_of(t):
            return bass.IndirectOffsetOnAxis(SLOTI[:, t:t + 1], 0)

        def ffn_post_pool(pool, s, rows, rx):
            pool.wait_ge(s["slots"], 1)
            for t in range(NT):
                pool.indirect_dma_start(bass.AP(rx, 0, [[ROW, NR * P], [1, ROW]]), rows_of(t),
                                        HAT[:, t * ROW:(t + 1) * ROW], None).then_inc(rows["scattered"], 16)
            for i in range(NR):
                pool.wait_ge(s["ids"], i + 1)
                pool.wait_ge(s["y"], i + 1)
                pool.indirect_dma_start(bass.AP(moe_out, 0, [[P, T + NR * P], [1, P]]),
                                        bass.IndirectOffsetOnAxis(IDS[:, i:i + 1], 0), YS[i % 4], None)\
                    .then_inc(rows[f"out{i % 4}"], 16)

        def ffn_post_sp(sp, s, rows, rx, last_layer):
            xs = (s["xs0"], s["xs1"], s["xs2"], s["xs3"])
            sp.wait_ge(rows["scattered"], 16 * NT)
            for i in range(NR):
                at_least(sp, s["x_t"], i - 3)
                at_least(sp, s["ids"], i - 3)
                sp.dma_start(XS[i % 4], bass.AP(rx, i * P * ROW, [[ROW, P], [1, ROW]])).then_inc(xs[i % 4], 16)
            for i in range(4):
                sp.wait_ge(rows[f"out{i}"], 16 * ((NR - 1 - i) // 4 + 1))
            for c in range(NC):
                sp.dma_start(GATH[:, c * CH:(c + 1) * CH].rearrange("p (t c) -> p t c", c=P),
                             bass.AP(moe_out, c * CH * P, [[P, P], [P * P, CH // P], [1, P]])).then_inc(s[f"back{c}"], 16)
            if last_layer:
                for c in range(NC):
                    sp.wait_ge(s["done"], c + 1)
                    sp.dma_start(bass.AP(out.tensor, c * CH * P, [[P, P], [P * P, CH // P], [1, P]]),
                                 X[:, c * CH:(c + 1) * CH].rearrange("p (t c) -> p t c", c=P)).then_inc(s_out, 16)
                sp.wait_ge(s_out, 16 * NC)

        def b_small_pe(pe):
            pe.wait_ge(prep["repeated"], 1)
            pe.matmul(bank[7][:, 0:P], TWS[0:64, 0:P], TWS[0:64, P:2 * P], start=True, stop=True)
            pe.matmul(bank[7][:, P:2 * P], TWS[:, 2 * P:3 * P], TWS[:, 3 * P:4 * P], start=True, stop=True)
            pe.matmul(bank[7][:, 2 * P:3 * P], TWS[0:64, 4 * P:5 * P], TWS[0:64, 5 * P:6 * P], start=True, stop=True)
            pe.matmul(bank[7][:, 3 * P:4 * P], TWS[:, 2 * P:3 * P], TWS[:, 6 * P:7 * P], start=True, stop=True)\
                .then_inc(prep["product"], 1)

        GROUPS = NT // 2
        QKB, VB = (7, 0, 3), (1, 2)

        def b_pre_pe(pe, s):
            transpose_pe(pe, s)
            for step_ in range(GROUPS + 3):
                g = step_
                c = g // 2
                if g < GROUPS:
                    pe.wait_ge(s["xt"], 2 if c == 0 else NC)
                    at_least(pe, s["scaled"], g - 2)
                    for i in range(2):
                        last = pe.matmul(bank[QKB[g % 3]][:, i * S:(i + 1) * S], tile_(XT, 2 * g + i), BDQK[:, :],
                                         start=True, stop=True)
                    last.then_inc(s["qk_ps"], 1)
                    if g % 2 == 0:
                        at_least(pe, s["v_ev"], c - 1)
                    for i in range(2):
                        o = (2 * (g % 2) + i) * P
                        last = pe.matmul(bank[VB[c % 2]][:, o:o + P], tile_(XT, 2 * g + i), BDV[:, :],
                                         start=True, stop=True)
                    if g % 2:
                        last.then_inc(s["v_ps"], 1)
                g = step_ - 3
                c = g // 2
                if g >= 0:
                    pe.wait_ge(s["scaled"], g + 1)
                    if g % 2 == 0:
                        at_least(pe, s["r2"], 2 * c - 1)
                        at_least(pe, s["kw"], c)
                    for i in range(2):
                        for x in range(2):
                            o = (2 * (g % 2) + i) * P
                            last = pe.transpose(bank[4 + x][:, o:o + P], TOK[g % 3][:, (2 * i + x) * P:(2 * i + x + 1) * P],
                                                IDF[:, :])
                    last.then_inc(s["turned"], 1)
                    if g % 2 == 0:
                        at_least(pe, s["kk"], c)
                        pe.matmul(bank[6][:, :], BDG[:, :], XT[:, c * CH:(c + 1) * CH], start=True, stop=True)\
                            .then_inc(s["g_ps"], 1)

        def b_pre_act(act, s):
            ln_act(act, s, False)
            transpose_act(act, s)
            for step_ in range(GROUPS + 5):
                g = step_
                if g < GROUPS:
                    act.wait_ge(s["qk_ps"], g + 1)
                    at_least(act, s["ms"], g - 1)
                    act.activation(SQ[g % 2], bank[QKB[g % 3]][:, :], ACT.Square).then_inc(s["sq"], 1)
                g = step_ - 1
                if 0 <= g < GROUPS:
                    act.wait_ge(s["ms"], g + 1)
                    act.activation(SD[g % 2], MS[g % 2], ACT.Sqrt, bias=EPS[:, 1:2], scale=1.0 / DH)\
                        .then_inc(s["sd"], 1)
                c = (step_ - 2) // 2
                if step_ % 2 == 0 and 0 <= c < NC:
                    act.wait_ge(s["v_ps"], c + 1)
                    act.activation(V[:, c * CH:(c + 1) * CH], bank[VB[c % 2]][:, :], ACT.Copy).then_inc(s["v_ev"], 1)
                c = (step_ - 6) // 2
                if step_ % 2 == 0 and 0 <= c < NC:
                    second_part(act, s, c, 1)
                c = (step_ - 4) // 2
                if step_ % 2 == 0 and 0 <= c < NC:
                    act.wait_ge(s["turned"], 2 * c + 2)
                    at_least(act, s["kk"], c)
                    act.activation(KW, bank[5][:, :], ACT.Identity, scale=KNW).then_inc(s["kw"], 1)
                    act.activation(part(QP, c, 0), halves(bank[4][:, :]), ACT.Identity, scale=QNW).then_inc(s["qa"], 1)
                c = (step_ - 5) // 2
                if step_ % 2 and 0 <= c < NC:
                    act.wait_ge(s["kk"], c + 1)
                    act.activation(part(KP, c, 0), halves(KK), ACT.Copy).then_inc(s["qa"], 1)
                    second_part(act, s, c, 0)

        def b_small_dve(dve):
            def tiled(dst, src, by_head, n):
                rep = src.rearrange("p (o d) -> p o d", o=1) if by_head else src.rearrange("p (d o) -> p d o", o=1)
                shape = [n, H, DH] if by_head else [n, DH, H]
                view = dst.rearrange("p (a b) -> p a b", b=shape[2])
                return dve.tensor_copy(view, rep.to_broadcast(shape))

            tiled(TWS[0:64, 0:P], SMALL[0:64, 0:8], True, 64)
            tiled(TWS[0:64, P:2 * P], SMALL[0:64, 8:16], False, 64)
            tiled(TWS[:, 2 * P:3 * P], SMALL[:, 16:24], True, P)
            tiled(TWS[:, 3 * P:4 * P], SMALL[:, 24:32], False, P)
            tiled(TWS[0:64, 4 * P:5 * P], SMALL[0:64, 40:48], True, 64)
            tiled(TWS[0:64, 5 * P:6 * P], SMALL[0:64, 48:56], False, 64)
            tiled(TWS[:, 6 * P:7 * P], SMALL[:, 32:40], True, P).then_inc(prep["repeated"], 1)
            dve.tensor_tensor(BDO[:, :].rearrange("p (h o) -> p h o", o=DH),
                              BLK[:, :].rearrange("p (h o) -> p h o", o=DH),
                              SMALL[:, 56:64].rearrange("p (x o) -> p x o", x=1).to_broadcast([P, H, DH]), ALU.mult)
            dve.wait_ge(prep["product"], 1)
            for i, (dst, blk) in enumerate(((BDQ, BLKP), (BDK, BLKP), (BDG, BLKP), (BDV, BLK))):
                last = dve.tensor_tensor(dst[:, :], bank[7][:, i * P:(i + 1) * P], blk[:, :], ALU.mult)
            last.then_inc(prep["blocks"], 1)

        def b_pre_dve(dve, s, first):
            ln_dve(dve, s, X, False, first)

            def by_head(x):
                return x.rearrange("p (y n) -> p y n", n=H)

            for step_ in range(GROUPS + 4):
                g = step_
                if g < GROUPS:
                    dve.wait_ge(s["sq"], g + 1)
                    at_least(dve, s["sd"], g - 1)
                    dve.tensor_reduce(out=by_head(MS[g % 2]), in_=SQ[g % 2].rearrange("p (y d n) -> p y n d", d=DH, n=H),
                                      axis=AX_X, op=ALU.add).then_inc(s["ms"], 1)
                g = step_ - 1
                if 0 <= g < GROUPS:
                    dve.wait_ge(s["sd"], g + 1)
                    dve_then(dve, dve.reciprocal(INV[g % 2], SD[g % 2]))
                    at_least(dve, s["turned"], g - 2)
                    inv = INV[g % 2].rearrange("p (y o n) -> p y o n", o=1, n=H).to_broadcast([P, 4, DH, H])
                    dve.tensor_tensor(TOK[g % 3].rearrange("p (y d n) -> p y d n", d=DH, n=H),
                                      bank[QKB[g % 3]][:, :].rearrange("p (y d n) -> p y d n", d=DH, n=H), inv, ALU.mult)\
                        .then_inc(s["scaled"], 1)
                c = (step_ - 4) // 2
                if step_ % 2 == 0 and 0 <= c < NC:
                    dve.wait_ge(s["g_ps"], c + 1)
                    at_least(dve, s["qa"], 2 * c)
                    at_least(dve, s["r2"], 2 * c)
                    dve.wait_ge(s["kw"], c + 1)
                    dve.tensor_tensor(KK, bank[6][:, :], KW, ALU.add).then_inc(s["kk"], 1)
                    dve.wait_ge(s["qa"], 2 * c + 1)
                    at_least(dve, s["q_done"], 2 * c - 3)
                    dve.scalar_tensor_tensor(out=rest(c, 0), in0=halves(bank[4][:, :]), scalar=QNW,
                                             in1=part(QP, c, 0), op0=ALU.mult, op1=ALU.subtract).then_inc(s["r2"], 1)
                c = (step_ - 5) // 2
                if step_ % 2 and 0 <= c < NC:
                    dve.wait_ge(s["qa"], 2 * c + 2)
                    at_least(dve, s["q_done"], 2 * c - 2)
                    dve.tensor_tensor(rest(c, 1), halves(KK), part(KP, c, 0), ALU.subtract)\
                        .then_inc(s["r2"], 1)

        def parts_of(p):
            return (p["parts0"], p["parts1"], p["parts2"], p["parts3"])

        block = ctx.enter_context(nc.Block())

        @block.sync
        def _(sp):
            sp.dma_start(X[:, :].rearrange("p (t c) -> p t c", c=P),
                         bass.AP(a["x"].tensor, 0, [[P, P], [P * P, NT], [1, P]])).then_inc(ld["x"], 16)
            for n in ("Qw", "Kw", "Vw"):
                sp.dma_start(wa[n][:, :], a[n]).then_inc(ld["wa"], 16)

            def column(dst, name, dims, first=0):
                sp.dma_start(dst, bass.AP(a[name].tensor, first, dims)).then_inc(ld["small"], 16)

            def repeated(dst, name, n, sem):
                sp.dma_start(dst, bass.AP(a[name].tensor, 0, [[0, P], [1, n]])).then_inc(sem, 16)

            for dst, name in ((WN[:, 0:P], "wq"), (WN[:, P:2 * P], "wk"), (WV[:, :], "wv"), (WO[:, :], "wo")):
                sp.dma_start(dst, a[name]).then_inc(ld["ffn"], 16)
            sp.dma_start(GW[:, :], a["gate_w"]).then_inc(ld["ffn"], 16)
            repeated(GBR[:, :], "gate_b", E, ld["ffn"])
            repeated(BVR[:, :], "bv", P, ld["ffn"])
            repeated(BOR[:, :], "bo", P, ld["ffn"])
            for dst, name in ((G1, "ln1_g"), (BE1, "ln1_b"), (G2, "ln2_g"), (BE2, "ln2_b")):
                column(dst, name, [[1, P], [1, 1]])
            for dst, name in ((BQ, "bq"), (BK, "bk")):
                for d in range(DH):
                    column(dst[H * d:H * (d + 1), :], name, [[DH, 4], [4 * DH, 4]], d)
            for dst, name in ((QNW, "q_norm_w"), (KNW, "k_norm_w")):
                column(dst, name, [[1, DH], [0, H]])
            column(SMALL[0:64, 0:8], "W_DQ", [[8, 64], [1, 8]])
            column(SMALL[0:64, 8:16], "W_UQ", [[1, 64], [64, 8]])
            column(SMALL[:, 16:24], "W_DKV", [[8, P], [1, 8]])
            column(SMALL[:, 24:40], "W_UKV", [[1, P], [P, 16]])
            column(SMALL[0:64, 40:48], "W_KR", [[8, 64], [1, 8]])
            column(SMALL[0:64, 48:56], "W_QR", [[8, 64], [1, 8]])
            for o in range(DH):
                column(SMALL[:, 56 + o:57 + o], "W_O", [[0, H], [1, DH]], DH * o)
            sp.dma_start(W1[:, :].rearrange("p (e f) -> p e f", f=F),
                         bass.AP(a["w1"].tensor, 0, [[F, P], [P * F, E], [1, F]])).then_inc(ld["moe"], 16)
            sp.dma_start(W2[:, :].rearrange("p (g n) -> p g n", n=P),
                         bass.AP(a["w2"].tensor, 0, [[P, P], [P * P, E * FC], [1, P]])).then_inc(ld["moe"], 16)
            for e in range(E):
                sp.dma_start(B1C[:, e * FC:(e + 1) * FC], bass.AP(a["b1"].tensor, e * F, [[1, P], [P, FC]]))\
                    .then_inc(ld["moe"], 16)
            repeated(B2R[:, :], "b2", E * P, ld["moe"])
            sp.wait_ge(cst["fill"], 3)
            for rx in routed_x:
                sp.dma_start(bass.AP(rx, 0, [[ROW, P], [P * ROW, NR], [1, ROW]]),
                             FILL.rearrange("p (i c) -> p i c", c=ROW)).then_inc(ld["zero"], 16)
            sp.wait_ge(ld["zero"], 32)
            sp.wait_ge(ld["moe"], 16 * (3 + E))
            sp.wait_ge(ld["ffn"], 128)
            sp.wait_ge(ld["small"], 36 * 16)
            k = 1
            phase_end(sp, ph["sp"], k)
            for n, layer in enumerate(LAYERS):
                if n:
                    clear(sp, s_post)
                core_sp(sp, s_core, parts_of(s_pre))
                k += 1
                phase_end(sp, ph["sp"], k)
                clear(sp, s_pre)
                clear(sp, s_core)
                if layer is ATTN_B:
                    k += 1
                    phase_end(sp, ph["sp"], k)
                else:
                    ffn_post_sp(sp, s_post, routed[n // 2], routed_x[n // 2], n == len(LAYERS) - 1)
                    k += 1
                    phase_end(sp, ph["sp"], k)

        @block.gpsimd
        def _(pool):
            built = 0

            def done(ins, k=1):
                nonlocal built
                ins.then_inc(cst["pool"], 1)
                built += 1
                if k:
                    pool.wait_ge(cst["pool"], built)

            def where(buf, pattern, cm, base, op, fill):
                done(pool.affine_select(out=buf, in_=buf, compare_op=op, fill=fill, base=base, pattern=pattern,
                                        channel_multiplier=cm))

            for buf, v in ((IDF, 0.0), (IDB, 0.0), (MSK, NEG), (MSKT, 0.0), (TRI, 1.0), (BLK, 1.0), (BLKP, 1.0),
                           (SELN[0], 0.0), (SELN[1], 0.0), (SELD[0], 0.0), (SELD[1], 0.0)):
                done(pool.memset(buf[:, :], v))
            done(pool.memset(MSK[:, 0:P], 0.0))
            for buf in (IDF, IDB):
                where(buf[:, :], [[-1, P]], 1, 0, ALU.not_equal, 1.0)
            where(MSK[:, 0:P], [[-1, P]], 1, 0, ALU.is_ge, NEG)
            where(MSKT[:, :], [[1, P]], -1, 0, ALU.is_ge, NEG)
            where(TRI[:, :], [[1, P]], -1, -1, ALU.is_ge, 0.0)
            for g in range(2):
                for sel, base, d in ((SELN[g], 0, -1), (SELD[g], -DH, 0)):
                    v = sel[:, :].rearrange("p (j r d) -> p j r d", j=4, r=4)[:, :, 2 * g:2 * g + 2, :]
                    where(v, [[-32, 4], [-16, 2], [d, DH]], 1, base, ALU.not_equal, 1.0)
            v = BLK[:, :].rearrange("p (h d) -> p h d", d=DH)
            where(v, [[-DH, H], [0, DH]], 1, 0, ALU.is_ge, 0.0)
            where(v, [[DH, H], [0, DH]], -1, DH - 1, ALU.is_ge, 0.0)
            v = BLKP[:, :].rearrange("p (d r j) -> p d r j", r=4, j=4)
            where(v, [[0, DH], [-DH, 4], [-4 * DH, 4]], 1, 0, ALU.is_ge, 0.0)
            where(v, [[0, DH], [DH, 4], [4 * DH, 4]], -1, DH - 1, ALU.is_ge, 0.0)
            done(pool.iota(REV[:, :], [[-1, E]], base=E, channel_multiplier=0, allow_small_or_imprecise_dtypes=True))
            done(pool.iota(J128[:, :], [[P, NT]], base=0, channel_multiplier=0, allow_small_or_imprecise_dtypes=True))
            done(pool.iota(I24[:, :], [[1, NR]], base=0, channel_multiplier=0, allow_small_or_imprecise_dtypes=True))
            pool.memset(FILL, 0.0).then_inc(cst["fill"], 1)
            pool.wait_ge(cst["fill"], 1)
            pool.iota(FILL.bitcast(I32).rearrange("p (i c) -> p i c", c=ROW)[:, :, P:ROW].rearrange("p i o -> p (i o)"),
                      [[P, NR]], base=T, channel_multiplier=1).then_inc(cst["fill"], 1)
            pool.iota(HAT[:, :].bitcast(I32).rearrange("p (t c) -> p t c", c=ROW)[:, :, P:ROW]
                      .rearrange("p t o -> p (t o)"), [[P, NT]], base=0, channel_multiplier=1).then_inc(cst["fill"], 1)
            pool.wait_ge(cst["fill"], 3)
            done(pool.memset(KS[64:96, :], 1.0))
            pool.wait_ge(ld["ffn"], 128)
            for i, dst in enumerate((WQ, WK)):
                src = WN[:, i * P:(i + 1) * P].rearrange("p (j r d) -> p j r d", j=4, r=4)
                view = dst[:, :].rearrange("p (d r j) -> p d r j", r=4, j=4)
                for r in range(4):
                    done(pool.tensor_copy(view[:, :, r, :].rearrange("p d j -> p j d"), src[:, :, r, :]), 0)
            k = 1
            phase_end(pool, ph["pool"], k)
            for n, layer in enumerate(LAYERS):
                third_parts(pool, s_pre)
                core_pool(pool, s_core, layer is FFN)
                k += 1
                phase_end(pool, ph["pool"], k)
                if layer is FFN:
                    ffn_post_pool(pool, s_post, routed[n // 2], routed_x[n // 2])
                k += 1
                phase_end(pool, ph["pool"], k)

        @block.scalar
        def _(act):
            attn_a_act(act)
            k = 1
            phase_end(act, ph["act"], k)
            for n, layer in enumerate(LAYERS):
                if layer is ATTN_B:
                    b_pre_act(act, s_pre)
                else:
                    ffn_pre_act(act, s_pre)
                core_act(act, s_core, layer is ATTN_B)
                k += 1
                phase_end(act, ph["act"], k)
                if layer is FFN:
                    ffn_post_act(act, s_post)
                k += 1
                phase_end(act, ph["act"], k)

        @block.vector
        def _(dve):
            dve.memset(EPS[:, 0:1], LN_EPS)
            dve.memset(EPS[:, 1:2], RMS_EPS)
            dve.memset(ONB[:, :], 1.0)
            dve_then(dve, dve.memset(VP[:, :], 0.0))
            for i in range(2):
                v = VP[:, :].rearrange("p (kj g i c) -> p kj g i c", g=2, i=2, c=32)
                dve.memset(v[:, :, :, i, 16 * i + DH:16 * i + DH + 1], 1.0)
            dve.drain().then_inc(cst["dve"], 1)
            attn_a_dve(dve)
            k = 1
            phase_end(dve, ph["dve"], k)
            for n, layer in enumerate(LAYERS):
                if layer is ATTN_B:
                    b_pre_dve(dve, s_pre, NT)
                else:
                    ffn_pre_dve(dve, s_pre, EARLY if n else NT - 1)
                core_dve(dve, s_core, X if layer is ATTN_B else U)
                k += 1
                phase_end(dve, ph["dve"], k)
                if layer is FFN:
                    ffn_post_dve(dve, s_post, routed[n // 2], n == 0, n == len(LAYERS) - 1)
                k += 1
                phase_end(dve, ph["dve"], k)

        @block.tensor
        def _(pe):
            pe.wait_ge(cst["pool"], 19)
            attn_a_pe(pe)
            k = 1
            phase_end(pe, ph["pe"], k)
            for n, layer in enumerate(LAYERS):
                if layer is ATTN_B:
                    b_pre_pe(pe, s_pre)
                else:
                    ffn_pre_pe(pe, s_pre)
                core_pe(pe, s_core, layer is ATTN_B, BDO if layer is ATTN_B else WO)
                k += 1
                phase_end(pe, ph["pe"], k)
                if layer is FFN:
                    ffn_post_pe(pe, s_post, routed[n // 2], n == 0)
                k += 1
                phase_end(pe, ph["pe"], k)


_A, _B, _FF = "L0_attn_a_", "L0_attn_b_", "L0_ffn_"
_NAMES = {n: _A + n for n in ("x", "Qw", "Kw", "Vw")}
_NAMES |= {n: _B + n for n in ("W_DQ", "W_UQ", "W_DKV", "W_UKV", "W_QR", "W_KR", "W_O", "q_norm_w", "k_norm_w")}
_NAMES |= {n: _FF + n for n in ("ln1_g", "ln1_b", "ln2_g", "ln2_b", "wq", "bq", "wk", "bk", "wv", "bv", "wo", "bo",
                                "gate_w", "gate_b", "w1", "b1", "w2", "b2")}


def kernel(**inputs):
    import numpy as np
    import concourse.bacc as bacc
    from concourse.bass_utils import run_bass_kernel_spmd

    nc = bacc.Bacc("TRN2", target_bir_lowering=False, num_devices=1)
    arrays, args = {}, {}
    for short, name in _NAMES.items():
        arr = np.ascontiguousarray(inputs[name])
        arrays[f"in_{short}"] = arr
        args[short] = nc.dram_tensor(f"in_{short}", arr.shape, mybir.dt.from_np(arr.dtype), kind="ExternalInput").ap()
    out = nc.dram_tensor("out_x", (B, S, P), F32, kind="ExternalOutput").ap()
    hybrid_block_kernel(nc, args, out)
    r = run_bass_kernel_spmd(nc, [arrays], core_ids=[0])
    return r.results[0]["out_x"]
```
